# Optimizing a Trainium2 kernel written in Bass

```python
import numpy as np
import jax
import jax.numpy as jnp

def _softmax(x, axis=-1):
    return jax.nn.softmax(x, axis=axis)

def _gelu(x):
    return jax.nn.gelu(x, approximate=True)

def _silu(x):
    return jax.nn.silu(x)

def _sigmoid(x):
    return jax.nn.sigmoid(x)

def _layernorm(x, axis=-1, eps=1e-05):
    m = jnp.mean(x, axis=axis, keepdims=True)
    v = jnp.var(x, axis=axis, keepdims=True)
    return (x - m) / jnp.sqrt(v + eps)

def _scatter_add(tgt, idx, src, axis=0):
    return tgt.at[idx].add(src)

def _segment_sum(src, seg, n):
    return jax.ops.segment_sum(src, seg, n)
kernel_name = 'mk_xattn_ffn_d4_seqx_r8_4c4521'

def setup_inputs(seed: int=0):
    np.random.seed(seed)
    _w = jnp.asarray

    def _rec_inputs():
        import jax
        import jax.numpy as jnp
        _rk = jax.random.key(seed)
        x = 7.22e-05 + 1 * jax.random.normal(jax.random.fold_in(_rk, 1), (16, 56, 128), jnp.float32)
        _lenS = 56 - jax.random.randint(jax.random.fold_in(_rk, 7), (16,), 0, max(1, 56 // 4) + 1, jnp.int32)
        _lenS2 = 1500 - jax.random.randint(jax.random.fold_in(_rk, 8), (16,), 0, max(1, 1500 // 4) + 1, jnp.int32)
        _ctx_1024P = jax.random.normal(jax.random.fold_in(_rk, 11), (16, 16, 128), jnp.float32)
        _ctx_1024c = jax.random.dirichlet(jax.random.fold_in(_rk, 511), 0.3 * jnp.ones((16,), jnp.float32), (16, 1500))
        _ctx_1024t = jnp.einsum('bsk,bkd->bsd', _ctx_1024c, _ctx_1024P)
        _ctx_1024t = _ctx_1024t * jax.lax.rsqrt(jnp.mean(jnp.square(_ctx_1024t)) + 1e-12) * 0.953939
        ctx_1024 = 4.13588e-05 + 0.999923 * (_ctx_1024t + 0.3 * jax.random.normal(jax.random.fold_in(_rk, 611), (16, 1500, 128), jnp.float32))
        fside_1x16xSxS2_0 = 8.74812e-05 + 1.00005 * jax.random.normal(jax.random.fold_in(_rk, 12), (1, 16, 56, 1500), jnp.float32)
        _validS = jnp.arange(56)[None, :] < _lenS[:, None]
        _validS2 = jnp.arange(1500)[None, :] < _lenS2[:, None]
        _causal = jnp.tril(jnp.ones((56, 56), dtype=bool))
        mask_Bx1x1xS2_ff0 = jnp.where(jnp.ones((16, 1, 1, 1500), dtype=bool), 0.0, -1000000000.0).astype(jnp.float32)
        return (x, ctx_1024, fside_1x16xSxS2_0, mask_Bx1x1xS2_ff0)
    x, ctx_1024, fside_1x16xSxS2_0, mask_Bx1x1xS2_ff0 = _rec_inputs()

    def _L0_xattn_setup():
        import jax, jax.numpy as jnp
        import numpy as np
        B, SQ, SK, D, H = (4, 256, 256, 128, 16)
        HD = D // H
        key = jax.random.key(seed)
        ks = jax.random.split(key, 8)
        s = 1.0 / np.sqrt(D)
        return {'query': jax.random.normal(ks[0], (B, SQ, D), jnp.float32), 'key_value': jax.random.normal(ks[1], (B, SK, D), jnp.float32), 'Wq': jax.random.normal(ks[2], (D, D), jnp.float32) * s, 'bq': jnp.zeros((D,), jnp.float32), 'Wkv': jax.random.normal(ks[3], (D, 2 * D), jnp.float32) * s, 'bkv': jnp.zeros((2 * D,), jnp.float32), 'Wo': jax.random.normal(ks[4], (D, D), jnp.float32) * s, 'bo': jnp.zeros((D,), jnp.float32)}
    _L0_xattn_all = _L0_xattn_setup()
    _L0_xattn_in = {k: v for k, v in _L0_xattn_all.items() if k in ('Wq', 'bq', 'Wkv', 'bkv', 'Wo', 'bo')}
    del _L0_xattn_all

    def _L0_ffn_setup():
        import jax, jax.numpy as jnp
        import numpy as np
        B, S, D, H, L, E, K = (4, 128, 128, 16, 2, 8, 2)
        DFF = 4 * D

        def _ln(x, w, b):
            m = x.mean(-1, keepdims=True)
            v = x.var(-1, keepdims=True)
            return (x - m) / jnp.sqrt(v + 1e-05) * w + b

        def _attn(x, wq, wk, wv, wo, bq, bk, bv, bo):
            Bb, T, C = x.shape
            hd = C // H
            q = (x @ wq + bq).reshape(Bb, T, H, hd).transpose(0, 2, 1, 3)
            k = (x @ wk + bk).reshape(Bb, T, H, hd).transpose(0, 2, 1, 3)
            v = (x @ wv + bv).reshape(Bb, T, H, hd).transpose(0, 2, 1, 3)
            att = jnp.einsum('bhqd,bhkd->bhqk', q, k) * hd ** (-0.5)
            causal = jnp.tril(jnp.ones((T, T), bool))
            att = jnp.where(causal, att, -jnp.inf)
            att = jax.nn.softmax(att, axis=-1)
            y = jnp.einsum('bhqk,bhkd->bhqd', att, v).transpose(0, 2, 1, 3).reshape(Bb, T, C)
            return y @ wo + bo

        def _ffn(h, w1, b1, w2, b2):
            return jax.nn.gelu(h @ w1 + b1, approximate=False) @ w2 + b2

        def _combine_weights(logits):
            vals, idx = jax.lax.top_k(logits, K)
            w = jax.nn.softmax(vals, axis=-1)
            onehot = (idx[..., None] == jnp.arange(E)).astype(w.dtype)
            return jnp.sum(w[..., None] * onehot, axis=-2)

        def _token_moe(h, gw, gb, w1, b1, w2, b2):
            cw = _combine_weights(h @ gw + gb)
            out = jnp.zeros_like(h)
            for e in range(E):
                out = out + _ffn(h, w1[e], b1[e], w2[e], b2[e]) * cw[..., e:e + 1]
            return out

        def _seq_moe(h, gw, gb, w1, b1, w2, b2):
            cw = _combine_weights(h.mean(axis=1) @ gw + gb)
            out = jnp.zeros_like(h)
            for e in range(E):
                out = out + _ffn(h, w1[e], b1[e], w2[e], b2[e]) * cw[:, e, None, None]
            return out
        key = jax.random.key(seed)
        ks = jax.random.split(key, 9)
        n = lambda k, shp: jax.random.normal(k, shp, dtype=jnp.float32) * 0.02
        return {'x': jax.random.normal(ks[0], (B, S, D), dtype=jnp.float32), 'ln1_w': jnp.ones((L, D), jnp.float32), 'ln1_b': jnp.zeros((L, D), jnp.float32), 'ln2_w': jnp.ones((L, D), jnp.float32), 'ln2_b': jnp.zeros((L, D), jnp.float32), 'wq': n(ks[1], (L, D, D)), 'wk': n(ks[2], (L, D, D)), 'wv': n(ks[3], (L, D, D)), 'wo': n(ks[4], (L, D, D)), 'bq': jnp.zeros((L, D), jnp.float32), 'bk': jnp.zeros((L, D), jnp.float32), 'bv': jnp.zeros((L, D), jnp.float32), 'bo': jnp.zeros((L, D), jnp.float32), 'gate_w': n(ks[5], (L, D, E)), 'gate_b': jnp.zeros((L, E), jnp.float32), 'e_w1': n(ks[6], (L, E, D, DFF)), 'e_b1': jnp.zeros((L, E, DFF), jnp.float32), 'e_w2': n(ks[7], (L, E, DFF, D)), 'e_b2': jnp.zeros((L, E, D), jnp.float32)}
    _L0_ffn_all = _L0_ffn_setup()
    _L0_ffn_in = {k: v for k, v in _L0_ffn_all.items() if k in ('ln1_w', 'ln1_b', 'ln2_w', 'ln2_b', 'wq', 'wk', 'wv', 'wo', 'bq', 'bk', 'bv', 'bo', 'gate_w', 'gate_b', 'e_w1', 'e_b1', 'e_w2', 'e_b2')}
    del _L0_ffn_all

    def _L1_xattn_setup():
        import jax, jax.numpy as jnp
        import numpy as np
        EPS = 1e-05

        def layer_norm(x, g, b):
            mu = jnp.mean(x, axis=-1, keepdims=True)
            var = jnp.var(x, axis=-1, keepdims=True)
            return (x - mu) * jax.lax.rsqrt(var + EPS) * g + b
        key = jax.random.key(seed)
        ks = jax.random.split(key, 8)
        dim, heads, dim_head = (128, 16, 64)
        inner = heads * dim_head
        b, n, m = (8, 512, 64)
        s = dim ** (-0.5)
        return {'x': jax.random.normal(ks[0], (b, n, dim), jnp.float32), 'latents': jax.random.normal(ks[1], (b, m, dim), jnp.float32), 'ln_m_g': jnp.ones((dim,), jnp.float32), 'ln_m_b': jnp.zeros((dim,), jnp.float32), 'ln_l_g': jnp.ones((dim,), jnp.float32), 'ln_l_b': jnp.zeros((dim,), jnp.float32), 'Wq': jax.random.normal(ks[2], (dim, inner), jnp.float32) * s, 'Wkv': jax.random.normal(ks[3], (dim, 2 * inner), jnp.float32) * s, 'Wout': jax.random.normal(ks[4], (inner, dim), jnp.float32) * s}
    _L1_xattn_all = _L1_xattn_setup()
    _L1_xattn_in = {k: v for k, v in _L1_xattn_all.items() if k in ('ln_m_g', 'ln_m_b', 'ln_l_g', 'ln_l_b', 'Wq', 'Wkv', 'Wout')}
    del _L1_xattn_all

    def _L1_ffn_setup():
        import jax, jax.numpy as jnp
        import numpy as np
        EMB = 128
        FF = 4 * EMB

        def _ternary(w):
            scale = jnp.maximum(jnp.mean(jnp.abs(w)), 1e-08)
            w_t = jnp.clip(jnp.round(w / scale), -1.0, 1.0)
            return w + jax.lax.stop_gradient(w_t - w)
        key = jax.random.key(seed)
        kx, k1, k2, kb1, kb2 = jax.random.split(key, 5)
        x = jax.random.normal(kx, (4, 256, EMB), dtype=jnp.float32)
        lim1 = 1.0 / np.sqrt(EMB)
        lim2 = 1.0 / np.sqrt(FF)
        W1 = jax.random.uniform(k1, (FF, EMB), jnp.float32, -lim1, lim1)
        b1 = jax.random.uniform(kb1, (FF,), jnp.float32, -lim1, lim1)
        W2 = jax.random.uniform(k2, (EMB, FF), jnp.float32, -lim2, lim2)
        b2 = jax.random.uniform(kb2, (EMB,), jnp.float32, -lim2, lim2)
        return {'x': x, 'W1': W1, 'b1': b1, 'W2': W2, 'b2': b2}
    _L1_ffn_all = _L1_ffn_setup()
    _L1_ffn_in = {k: v for k, v in _L1_ffn_all.items() if k in ('W1', 'b1', 'W2', 'b2')}
    del _L1_ffn_all

    def _L2_xattn_setup():
        import jax, jax.numpy as jnp
        import numpy as np
        B, T, D = (8, 256, 128)
        key = jax.random.key(seed)
        kq, kk, kv = jax.random.split(key, 3)
        return {'query': jax.random.normal(kq, (B, T, D), dtype=jnp.float32), 'key': jax.random.normal(kk, (B, T, D), dtype=jnp.float32), 'value': jax.random.normal(kv, (B, T, D), dtype=jnp.float32)}
    _L2_xattn_all = _L2_xattn_setup()
    _L2_xattn_in = {k: v for k, v in _L2_xattn_all.items() if k in ()}
    del _L2_xattn_all

    def _L2_ffn_setup():
        import jax, jax.numpy as jnp
        import numpy as np
        NUM_EXPERTS = 8
        EXPERT_CAPACITY = 2.0
        key = jax.random.key(seed)
        k1, k2, k3, k4 = jax.random.split(key, 4)
        B, T, C, H, E = (4, 512, 128, 512, NUM_EXPERTS)
        x = jax.random.normal(k1, (B, T, C), jnp.float32)
        gate_w = jax.random.normal(k2, (C, E), jnp.float32) * 0.02
        w1 = jax.random.normal(k3, (E, C, H), jnp.float32) * 0.02
        w2 = jax.random.normal(k4, (E, H, C), jnp.float32) * 0.02
        return {'x': x, 'gate_w': gate_w, 'w1': w1, 'w2': w2}
    _L2_ffn_all = _L2_ffn_setup()
    _L2_ffn_in = {k: v for k, v in _L2_ffn_all.items() if k in ('gate_w', 'w1', 'w2')}
    del _L2_ffn_all

    def _L3_xattn_setup():
        import jax, jax.numpy as jnp
        import numpy as np
        HIDDEN = 128
        NUM_HEADS = 16
        HEAD_DIM = 64
        key = jax.random.key(seed)
        ks = jax.random.split(key, 8)
        B, Sq, Skv = (4, 256, 256)
        scale = 1.0 / np.sqrt(HIDDEN)
        inp = {'q_hidden_states': jax.random.normal(ks[0], (B, Sq, HIDDEN), jnp.float32), 'kv_hidden_states': jax.random.normal(ks[1], (B, Skv, HIDDEN), jnp.float32), 'attention_bias': jax.random.normal(ks[2], (1, NUM_HEADS, Sq, Skv), jnp.float32), 'attention_mask': jnp.zeros((B, 1, 1, Skv), jnp.float32), 'Wq': jax.random.normal(ks[3], (HIDDEN, NUM_HEADS * HEAD_DIM), jnp.float32) * scale, 'Wk': jax.random.normal(ks[4], (HIDDEN, NUM_HEADS * HEAD_DIM), jnp.float32) * scale, 'Wv': jax.random.normal(ks[5], (HIDDEN, NUM_HEADS * HEAD_DIM), jnp.float32) * scale, 'Wo': jax.random.normal(ks[6], (NUM_HEADS * HEAD_DIM, HIDDEN), jnp.float32) * scale}
        return inp
    _L3_xattn_all = _L3_xattn_setup()
    _L3_xattn_in = {k: v for k, v in _L3_xattn_all.items() if k in ('Wq', 'Wk', 'Wv', 'Wo')}
    del _L3_xattn_all

    def _L3_ffn_setup():
        import jax, jax.numpy as jnp
        import numpy as np
        D = 128
        P = 4
        DEPTH = 5
        FAN = 4
        G = (FAN ** (DEPTH + 1) - 1) // 3
        N_NODES = G * FAN
        HID = P * N_NODES
        key = jax.random.key(seed)
        k0, k1, k2, k3 = jax.random.split(key, 4)
        return {'oldx': jax.random.normal(k0, (2, 256, D), dtype=jnp.float32), 'W_in': jax.random.normal(k1, (HID, D), dtype=jnp.float32) * (1.0 / np.sqrt(D)), 'b_in': jax.random.normal(k2, (HID,), dtype=jnp.float32) * (1.0 / np.sqrt(D)), 'W_out': jax.random.normal(k3, (D, HID), dtype=jnp.float32) * (1.0 / np.sqrt((DEPTH + 1) * P))}
    _L3_ffn_all = _L3_ffn_setup()
    _L3_ffn_in = {k: v for k, v in _L3_ffn_all.items() if k in ('W_in', 'b_in', 'W_out')}
    del _L3_ffn_all
    return {'x': x, 'ctx_1024': ctx_1024, 'fside_1x16xSxS2_0': fside_1x16xSxS2_0, 'mask_Bx1x1xS2_ff0': mask_Bx1x1xS2_ff0, 'L0_xattn_Wq': _L0_xattn_in['Wq'], 'L0_xattn_bq': _L0_xattn_in['bq'], 'L0_xattn_Wkv': _L0_xattn_in['Wkv'], 'L0_xattn_bkv': _L0_xattn_in['bkv'], 'L0_xattn_Wo': _L0_xattn_in['Wo'], 'L0_xattn_bo': _L0_xattn_in['bo'], 'L0_ffn_ln1_w': _L0_ffn_in['ln1_w'], 'L0_ffn_ln1_b': _L0_ffn_in['ln1_b'], 'L0_ffn_ln2_w': _L0_ffn_in['ln2_w'], 'L0_ffn_ln2_b': _L0_ffn_in['ln2_b'], 'L0_ffn_wq': _L0_ffn_in['wq'], 'L0_ffn_wk': _L0_ffn_in['wk'], 'L0_ffn_wv': _L0_ffn_in['wv'], 'L0_ffn_wo': _L0_ffn_in['wo'], 'L0_ffn_bq': _L0_ffn_in['bq'], 'L0_ffn_bk': _L0_ffn_in['bk'], 'L0_ffn_bv': _L0_ffn_in['bv'], 'L0_ffn_bo': _L0_ffn_in['bo'], 'L0_ffn_gate_w': _L0_ffn_in['gate_w'], 'L0_ffn_gate_b': _L0_ffn_in['gate_b'], 'L0_ffn_e_w1': _L0_ffn_in['e_w1'], 'L0_ffn_e_b1': _L0_ffn_in['e_b1'], 'L0_ffn_e_w2': _L0_ffn_in['e_w2'], 'L0_ffn_e_b2': _L0_ffn_in['e_b2'], 'L1_xattn_ln_m_g': _L1_xattn_in['ln_m_g'], 'L1_xattn_ln_m_b': _L1_xattn_in['ln_m_b'], 'L1_xattn_ln_l_g': _L1_xattn_in['ln_l_g'], 'L1_xattn_ln_l_b': _L1_xattn_in['ln_l_b'], 'L1_xattn_Wq': _L1_xattn_in['Wq'], 'L1_xattn_Wkv': _L1_xattn_in['Wkv'], 'L1_xattn_Wout': _L1_xattn_in['Wout'], 'L1_ffn_W1': _L1_ffn_in['W1'], 'L1_ffn_b1': _L1_ffn_in['b1'], 'L1_ffn_W2': _L1_ffn_in['W2'], 'L1_ffn_b2': _L1_ffn_in['b2'], 'L2_ffn_gate_w': _L2_ffn_in['gate_w'], 'L2_ffn_w1': _L2_ffn_in['w1'], 'L2_ffn_w2': _L2_ffn_in['w2'], 'L3_xattn_Wq': _L3_xattn_in['Wq'], 'L3_xattn_Wk': _L3_xattn_in['Wk'], 'L3_xattn_Wv': _L3_xattn_in['Wv'], 'L3_xattn_Wo': _L3_xattn_in['Wo'], 'L3_ffn_W_in': _L3_ffn_in['W_in'], 'L3_ffn_b_in': _L3_ffn_in['b_in'], 'L3_ffn_W_out': _L3_ffn_in['W_out']}

def reference(x, ctx_1024, fside_1x16xSxS2_0, mask_Bx1x1xS2_ff0, L0_xattn_Wq, L0_xattn_bq, L0_xattn_Wkv, L0_xattn_bkv, L0_xattn_Wo, L0_xattn_bo, L0_ffn_ln1_w, L0_ffn_ln1_b, L0_ffn_ln2_w, L0_ffn_ln2_b, L0_ffn_wq, L0_ffn_wk, L0_ffn_wv, L0_ffn_wo, L0_ffn_bq, L0_ffn_bk, L0_ffn_bv, L0_ffn_bo, L0_ffn_gate_w, L0_ffn_gate_b, L0_ffn_e_w1, L0_ffn_e_b1, L0_ffn_e_w2, L0_ffn_e_b2, L1_xattn_ln_m_g, L1_xattn_ln_m_b, L1_xattn_ln_l_g, L1_xattn_ln_l_b, L1_xattn_Wq, L1_xattn_Wkv, L1_xattn_Wout, L1_ffn_W1, L1_ffn_b1, L1_ffn_W2, L1_ffn_b2, L2_ffn_gate_w, L2_ffn_w1, L2_ffn_w2, L3_xattn_Wq, L3_xattn_Wk, L3_xattn_Wv, L3_xattn_Wo, L3_ffn_W_in, L3_ffn_b_in, L3_ffn_W_out):
    import jax
    import jax.numpy as jnp

    def _L0_xattn_ref(query, key_value, Wq, bq, Wkv, bkv, Wo, bo):
        import jax, jax.numpy as jnp
        import numpy as np
        B, SQ, SK, D, H = (4, 256, 256, 128, 16)
        HD = D // H
        b, sq, _ = query.shape
        sk = key_value.shape[1]
        Q = (query @ Wq + bq).reshape(b, sq, H, HD).transpose(0, 2, 1, 3)
        KV = (key_value @ Wkv + bkv).reshape(b, sk, 2, H, HD)
        K = KV[:, :, 0].transpose(0, 2, 1, 3)
        V = KV[:, :, 1].transpose(0, 2, 1, 3)
        scale = 1.0 / np.sqrt(HD).astype(np.float32)
        scores = jnp.einsum('bhqd,bhkd->bhqk', Q, K) * scale
        attn = jax.nn.softmax(scores, axis=-1)
        out = jnp.einsum('bhqk,bhkd->bhqd', attn, V)
        out = out.transpose(0, 2, 1, 3).reshape(b, sq, D)
        return out @ Wo + bo

    def _L0_ffn_ref(x, ln1_w, ln1_b, ln2_w, ln2_b, wq, wk, wv, wo, bq, bk, bv, bo, gate_w, gate_b, e_w1, e_b1, e_w2, e_b2):
        import jax, jax.numpy as jnp
        import numpy as np
        B, S, D, H, L, E, K = (4, 128, 128, 16, 2, 8, 2)
        DFF = 4 * D

        def _ln(x, w, b):
            m = x.mean(-1, keepdims=True)
            v = x.var(-1, keepdims=True)
            return (x - m) / jnp.sqrt(v + 1e-05) * w + b

        def _attn(x, wq, wk, wv, wo, bq, bk, bv, bo):
            Bb, T, C = x.shape
            hd = C // H
            q = (x @ wq + bq).reshape(Bb, T, H, hd).transpose(0, 2, 1, 3)
            k = (x @ wk + bk).reshape(Bb, T, H, hd).transpose(0, 2, 1, 3)
            v = (x @ wv + bv).reshape(Bb, T, H, hd).transpose(0, 2, 1, 3)
            att = jnp.einsum('bhqd,bhkd->bhqk', q, k) * hd ** (-0.5)
            causal = jnp.tril(jnp.ones((T, T), bool))
            att = jnp.where(causal, att, -jnp.inf)
            att = jax.nn.softmax(att, axis=-1)
            y = jnp.einsum('bhqk,bhkd->bhqd', att, v).transpose(0, 2, 1, 3).reshape(Bb, T, C)
            return y @ wo + bo

        def _ffn(h, w1, b1, w2, b2):
            return jax.nn.gelu(h @ w1 + b1, approximate=False) @ w2 + b2

        def _combine_weights(logits):
            vals, idx = jax.lax.top_k(logits, K)
            w = jax.nn.softmax(vals, axis=-1)
            onehot = (idx[..., None] == jnp.arange(E)).astype(w.dtype)
            return jnp.sum(w[..., None] * onehot, axis=-2)

        def _token_moe(h, gw, gb, w1, b1, w2, b2):
            cw = _combine_weights(h @ gw + gb)
            out = jnp.zeros_like(h)
            for e in range(E):
                out = out + _ffn(h, w1[e], b1[e], w2[e], b2[e]) * cw[..., e:e + 1]
            return out

        def _seq_moe(h, gw, gb, w1, b1, w2, b2):
            cw = _combine_weights(h.mean(axis=1) @ gw + gb)
            out = jnp.zeros_like(h)
            for e in range(E):
                out = out + _ffn(h, w1[e], b1[e], w2[e], b2[e]) * cw[:, e, None, None]
            return out
        for l in range(L):
            x = x + _attn(_ln(x, ln1_w[l], ln1_b[l]), wq[l], wk[l], wv[l], wo[l], bq[l], bk[l], bv[l], bo[l])
            h = _ln(x, ln2_w[l], ln2_b[l])
            moe = _token_moe if l % 2 == 0 else _seq_moe
            x = x + moe(h, gate_w[l], gate_b[l], e_w1[l], e_b1[l], e_w2[l], e_b2[l])
        return x

    def _L1_xattn_ref(x, latents, ln_m_g, ln_m_b, ln_l_g, ln_l_b, Wq, Wkv, Wout):
        import jax, jax.numpy as jnp
        import numpy as np
        EPS = 1e-05

        def layer_norm(x, g, b):
            mu = jnp.mean(x, axis=-1, keepdims=True)
            var = jnp.var(x, axis=-1, keepdims=True)
            return (x - mu) * jax.lax.rsqrt(var + EPS) * g + b
        heads, dim_head = (16, 64)
        scale = dim_head ** (-0.5)
        x = layer_norm(x, ln_m_g, ln_m_b)
        lat = layer_norm(latents, ln_l_g, ln_l_b)
        b, m, _ = lat.shape
        q = lat @ Wq
        kv_input = jnp.concatenate([x, lat], axis=1)
        kv = kv_input @ Wkv
        k, v = jnp.split(kv, 2, axis=-1)

        def split_heads(t):
            return t.reshape(t.shape[0], t.shape[1], heads, dim_head).transpose(0, 2, 1, 3)
        q, k, v = (split_heads(q), split_heads(k), split_heads(v))
        dots = jnp.einsum('bhid,bhjd->bhij', q, k) * scale
        attn = jax.nn.softmax(dots, axis=-1)
        out = jnp.einsum('bhij,bhjd->bhid', attn, v)
        out = out.transpose(0, 2, 1, 3).reshape(b, m, heads * dim_head)
        return out @ Wout

    def _L1_ffn_ref(x, W1, b1, W2, b2):
        import jax, jax.numpy as jnp
        import numpy as np
        EMB = 128
        FF = 4 * EMB

        def _ternary(w):
            scale = jnp.maximum(jnp.mean(jnp.abs(w)), 1e-08)
            w_t = jnp.clip(jnp.round(w / scale), -1.0, 1.0)
            return w + jax.lax.stop_gradient(w_t - w)
        h = jnp.einsum('bsd,fd->bsf', x, _ternary(W1)) + b1
        h = jax.nn.gelu(h, approximate=False)
        out = jnp.einsum('bsf,df->bsd', h, _ternary(W2)) + b2
        return out

    def _L2_xattn_ref(query, key, value):
        import jax, jax.numpy as jnp
        import numpy as np
        B, T, D = (8, 256, 128)
        d = query.shape[-1]
        scores = jnp.einsum('bqd,bkd->bqk', query, key) * d ** (-0.5)
        tril = jnp.tril(jnp.ones((query.shape[1], key.shape[1]), dtype=bool))
        scores = jnp.where(tril, scores, -jnp.inf)
        attn = jax.nn.softmax(scores, axis=-1)
        return jnp.einsum('bqk,bkd->bqd', attn, value)

    def _L2_ffn_ref(x, gate_w, w1, w2):
        import jax, jax.numpy as jnp
        import numpy as np
        NUM_EXPERTS = 8
        EXPERT_CAPACITY = 2.0
        B, T, C = x.shape
        E = gate_w.shape[1]
        cap = int(EXPERT_CAPACITY * T / E)
        scores = jnp.einsum('BTC,CE->BTE', x, gate_w)
        probs = jax.nn.softmax(scores, axis=-1)
        probs_et = jnp.transpose(probs, (0, 2, 1))
        top_p, top_idx = jax.lax.top_k(probs_et, cap)
        xin = jnp.take_along_axis(x[:, None, :, :], top_idx[..., None], axis=2)
        h = jax.nn.gelu(jnp.einsum('BElC,ECH->BElH', xin, w1), approximate=False)
        y = jnp.einsum('BElH,EHC->BElC', h, w2)
        y = y * top_p[..., None]
        b_idx = jnp.arange(B)[:, None, None]
        out = jnp.zeros((B, T, C), x.dtype).at[b_idx, top_idx].add(y)
        return out

    def _L3_xattn_ref(q_hidden_states, kv_hidden_states, attention_bias, attention_mask, Wq, Wk, Wv, Wo):
        import jax, jax.numpy as jnp
        import numpy as np
        HIDDEN = 128
        NUM_HEADS = 16
        HEAD_DIM = 64
        B, Sq, D = q_hidden_states.shape
        Skv = kv_hidden_states.shape[1]
        H, Dh = (NUM_HEADS, HEAD_DIM)
        q = (q_hidden_states @ Wq).reshape(B, Sq, H, Dh)
        k = (kv_hidden_states @ Wk).reshape(B, Skv, H, Dh)
        v = (kv_hidden_states @ Wv).reshape(B, Skv, H, Dh)
        bias = attention_bias + attention_mask
        scores = jnp.einsum('bqhd,bkhd->bhqk', q, k) + bias
        probs = jax.nn.softmax(scores, axis=-1)
        attn = jnp.einsum('bhqk,bkhd->bqhd', probs, v)
        attn = attn.reshape(B, Sq, H * Dh)
        return attn @ Wo

    def _L3_ffn_ref(oldx, W_in, b_in, W_out):
        import jax, jax.numpy as jnp
        import numpy as np
        D = 128
        P = 4
        DEPTH = 5
        FAN = 4
        G = (FAN ** (DEPTH + 1) - 1) // 3
        N_NODES = G * FAN
        HID = P * N_NODES
        x = oldx.reshape(-1, D)
        B = x.shape[0]
        logits = x @ W_in.T + b_in
        act = jax.nn.gelu(logits, approximate=False)
        act4 = act.reshape(B, P, G, FAN)
        decisions = jnp.argmax(act4, axis=-1)
        current = jnp.zeros((B, P), dtype=jnp.int32)
        nodes = [current]
        platform = 0
        for d in range(DEPTH):
            moves = jnp.take_along_axis(decisions, current[..., None].astype(jnp.int64), axis=2)[..., 0].astype(jnp.int32)
            next_platform = platform + FAN ** d
            current = next_platform + FAN * (current - platform) + moves
            nodes.append(current)
            platform = next_platform
        mask = sum((jax.nn.one_hot(n, G, dtype=act4.dtype) for n in nodes))
        mask = jax.lax.stop_gradient(mask)
        masked = act4 * mask[..., None]
        new_logits = masked.reshape(B, HID) @ W_out.T
        return new_logits.reshape(oldx.shape)
    x = x + _L0_xattn_ref(_layernorm(x, axis=-1), ctx_1024, L0_xattn_Wq, L0_xattn_bq, L0_xattn_Wkv, L0_xattn_bkv, L0_xattn_Wo, L0_xattn_bo)
    x = x + _L0_ffn_ref(_layernorm(x, axis=-1), L0_ffn_ln1_w, L0_ffn_ln1_b, L0_ffn_ln2_w, L0_ffn_ln2_b, L0_ffn_wq, L0_ffn_wk, L0_ffn_wv, L0_ffn_wo, L0_ffn_bq, L0_ffn_bk, L0_ffn_bv, L0_ffn_bo, L0_ffn_gate_w, L0_ffn_gate_b, L0_ffn_e_w1, L0_ffn_e_b1, L0_ffn_e_w2, L0_ffn_e_b2)
    x = x + _L1_xattn_ref(ctx_1024, _layernorm(x, axis=-1), L1_xattn_ln_m_g, L1_xattn_ln_m_b, L1_xattn_ln_l_g, L1_xattn_ln_l_b, L1_xattn_Wq, L1_xattn_Wkv, L1_xattn_Wout)
    x = x + _L1_ffn_ref(_layernorm(x, axis=-1), L1_ffn_W1, L1_ffn_b1, L1_ffn_W2, L1_ffn_b2)
    x = x + _L2_xattn_ref(_layernorm(x, axis=-1), ctx_1024, ctx_1024)
    x = x + _L2_ffn_ref(_layernorm(x, axis=-1), L2_ffn_gate_w, L2_ffn_w1, L2_ffn_w2)
    x = x + _L3_xattn_ref(_layernorm(x, axis=-1), ctx_1024, fside_1x16xSxS2_0, mask_Bx1x1xS2_ff0, L3_xattn_Wq, L3_xattn_Wk, L3_xattn_Wv, L3_xattn_Wo)
    x = x + _L3_ffn_ref(_layernorm(x, axis=-1), L3_ffn_W_in, L3_ffn_b_in, L3_ffn_W_out)
    return x

_drawn_inputs = setup_inputs


def setup_inputs(seed=0):
    import zlib

    import numpy as np

    out = dict(_drawn_inputs(seed))
    spreads = {'L0_xattn_bq': (0.0, 0.453),
     'L0_xattn_bkv': (0.0, 0.1),
     'L0_xattn_bo': (0.0, 0.1),
     'L0_ffn_ln1_w': (1.0, 0.6),
     'L0_ffn_ln1_b': (0.0, 0.8),
     'L0_ffn_ln2_w': (1.0, 0.6),
     'L0_ffn_ln2_b': (0.0, 0.779),
     'L0_ffn_bq': (0.0, 0.8),
     'L0_ffn_bk': (0.0, 0.8),
     'L0_ffn_bv': (0.0, 0.577),
     'L0_ffn_bo': (0.0, 0.1),
     'L0_ffn_gate_b': (0.0, 0.1),
     'L0_ffn_e_b1': (0.0, 0.8),
     'L0_ffn_e_b2': (0.0, 0.1),
     'L1_xattn_ln_m_g': (1.0, 0.2),
     'L1_xattn_ln_m_b': (0.0, 0.1),
     'L1_xattn_ln_l_g': (1.0, 0.2),
     'L1_xattn_ln_l_b': (0.0, 0.394)}
    factors = {'fside_1x16xSxS2_0': 8.0,
     'L0_ffn_wq': 8.0,
     'L0_ffn_wk': 8.0,
     'L0_ffn_wv': 3.476,
     'L0_ffn_wo': 2.68,
     'L0_ffn_e_w1': 2.72,
     'L1_ffn_b1': 8.0,
     'L1_ffn_b2': 8.0,
     'L2_ffn_gate_w': 8.0,
     'L2_ffn_w1': 8.0,
     'L2_ffn_w2': 8.0,
     'L3_ffn_W_in': 6.377,
     'L3_ffn_b_in': 8.0,
     'L3_ffn_W_out': 6.141}
    for name, (base, spread) in spreads.items():
        noise = np.random.default_rng([zlib.crc32(name.encode()), seed]).standard_normal(out[name].shape)
        drawn = base * np.exp(spread * noise) if base else spread * noise
        out[name] = jnp.asarray(drawn.astype(out[name].dtype))
    for name, factor in factors.items():
        out[name] = (out[name] * factor).astype(out[name].dtype)
    return out
```

```python
from contextlib import ExitStack

import concourse.bass as bass
from concourse import mybir

F32 = mybir.dt.float32
F32R = mybir.dt.float32r
U32 = mybir.dt.uint32
ALU = mybir.AluOpType
ACT = mybir.ActivationFunctionType
X = mybir.AxisListType.X

B, S, D, SK = 16, 56, 128, 1500
H = 16
PAIRS, TP = B // 2, 2 * S
TOK = B * S
HALF = TOK // 2
HQ = H * S
KT = 125
E, DFF = 8, 512
CAP = 2 * S // E
TREE_P, FAN, DEPTH = 4, 4, 5
G = (FAN ** (DEPTH + 1) - 1) // 3
LN_EPS = 1e-5
DMA = 16


class Signals:

    def __init__(self, nc, stage):
        self.nc, self.stage, self.stack, self.by_name = nc, stage, ExitStack(), {}

    def __getitem__(self, what):
        if what not in self.by_name:
            self.by_name[what] = self.stack.enter_context(self.nc.semaphore(f"{self.stage}_{what}"))
        return self.by_name[what]


class Core:

    def __init__(self, nc, dram):
        self.nc, self.dram = nc, dram
        self.old = None
        self.now = None
        self.count = 0

    def stage(self, name):
        if self.old is not None:
            self.old.stack.close()
        self.old, self.now = self.now, Signals(self.nc, f"s{self.count}_{name}")
        self.count += 1
        return self.now

    def clear_old(self, eng):
        if self.old is not None:
            for sem in self.old.by_name.values():
                eng.sem_clear(sem)


class Link:

    def __init__(self, eng, sem):
        self.eng, self.sem, self.n = eng, sem, 0

    def __call__(self, ins):
        self.n += 1
        ins.then_inc(self.sem, 1)
        self.eng.wait_ge(self.sem, self.n)


def halves(psum_two_banks):
    return psum_two_banks[:, :, 0:HALF]


def two(ap):
    return ap.rearrange("p (a c) -> p a c", a=2)


def alloc(c, stack):
    def sb(name, shape, dt=F32):
        return stack.enter_context(c.nc.sbuf_tensor(f"sb{c.count}_{name}", shape, dt))
    return sb


def stage_load(c):
    nc, d, sg = c.nc, c.dram, c.stage("load")
    with nc.Block() as block:
        @block.sync
        def _(sp):
            sp.dma_start(c.x[:], d["x"].rearrange("(t p) d -> p t d", p=TP)).then_inc(sg["loaded"], DMA)
            sp.dma_start(c.ident[:], d["ident"]).then_inc(sg["loaded"], DMA)
            sp.dma_start(c.ones[:], d["ones"]).then_inc(sg["loaded"], DMA)
            sp.wait_ge(sg["loaded"], 3 * DMA)


def stage_norm(c, src, dst, dst_t=None, affine=None):
    nc, d, sg = c.nc, c.dram, c.stage("norm")
    ps = c.ps
    with ExitStack() as st:
        sb = alloc(c, st)
        stats = sb(f"stats{c.count}", [TP, PAIRS, 6])
        mv = sb(f"mv{c.count}", [TP, PAIRS, 2])
        var = sb(f"var{c.count}", [TP, PAIRS])
        std = sb(f"std{c.count}", [TP, PAIRS])
        rstd = sb(f"rstd{c.count}", [TP, PAIRS])
        gb = sb(f"gb{c.count}", [TP, 2, D]) if affine else None
        with nc.Block() as block:
            @block.sync
            def _(sp):
                c.clear_old(sp)
                if affine:
                    for n, name in enumerate(affine):
                        sp.dma_start(gb[:, n, :], name).then_inc(sg["affine_loaded"], DMA)
                    sp.wait_ge(sg["affine_loaded"], 2 * DMA)

            @block.vector
            def _(dve):
                link = Link(dve, sg["dve_chain"])
                for t in range(PAIRS):
                    last = dve.bn_stats(stats[:, t, :], src[:, t, :])
                link(last)
                for t in range(PAIRS):
                    last = dve.bn_aggr(mv[:, t, :], stats[:, t, :])
                link(last)
                dve.tensor_scalar(var[:], mv[:, :, 1], LN_EPS, None, ALU.add).then_inc(sg["var_ready"], 1)
                dve.wait_ge(sg["std_ready"], 1)
                link(dve.reciprocal(rstd[:], std[:]))
                for t in range(PAIRS):
                    last = dve.tensor_scalar(dst[:, t, :], src[:, t, :], mv[:, t, 0:1], rstd[:, t:t + 1],
                                             ALU.subtract, ALU.mult)
                if affine:
                    link(last)
                    dve.wait_ge(sg["affine_loaded"], 2 * DMA)
                    link(dve.tensor_tensor(dst[:], dst[:], gb[:, 0:1, :].to_broadcast([TP, PAIRS, D]), ALU.mult))
                    last = dve.tensor_tensor(dst[:], dst[:], gb[:, 1:2, :].to_broadcast([TP, PAIRS, D]), ALU.add)
                last.then_inc(sg["dst_ready"], 1)
                if dst_t is not None:
                    dve.wait_ge(sg["transposed"], 1)
                    dve.tensor_copy(two(dst_t[:]), halves(ps[:, 0:2, :])).then_inc(sg["dst_t_ready"], 1)

            @block.scalar
            def _(act):
                act.wait_ge(sg["var_ready"], 1)
                act.activation(std[:], var[:], ACT.Sqrt).then_inc(sg["std_ready"], 1)

            if dst_t is not None:
                @block.tensor
                def _(pe):
                    pe.wait_ge(sg["dst_ready"], 1)
                    for t in range(PAIRS):
                        last = pe.transpose(ps[:, t // 4, (t % 4) * TP:(t % 4 + 1) * TP], dst[:, t, :],
                                            c.ident[0:TP, 0:TP])
                    last.then_inc(sg["transposed"], 1)


def stage_fold(c, name, hd, zt, n_out, biased):
    nc, d, sg = c.nc, c.dram, c.stage("fold")
    ps = c.ps
    with ExitStack() as st:
        sb = alloc(c, st)
        w = {k: sb(f"{k}_{name}", [hd, H, D]) for k in ("wqT", "wkT", "wvT", "wo")}
        m = sb(f"m_{name}", [D, H, D])
        qk = sb(f"qk_{name}", [D, B, H, S])
        if biased:
            bq = sb(f"bq_{name}", [hd, H])
            bv = sb(f"bv_{name}", [hd, H, TP])
            bo = sb(f"bo_{name}", [1, D])
            wb = sb(f"wb_{name}", [D, H])
        with nc.Block() as block:
            @block.sync
            def _(sp):
                c.clear_old(sp)
                for k in ("wqT", "wkT", "wvT", "wo"):
                    sp.dma_start(w[k][:], d[f"{name}_{k}"]).then_inc(sg["weights"], DMA)
                if biased:
                    sp.dma_start(bq[:], d[f"{name}_bq"]).then_inc(sg["weights"], DMA)
                    sp.dma_start(bv[:], d[f"{name}_bv"]).then_inc(sg["weights"], DMA)
                    sp.dma_start(bo[:], d[f"{name}_bo"]).then_inc(sg["weights"], DMA)
                sp.wait_ge(sg["q_folded"], H)
                sp.dma_start(d["qk"].rearrange("b p n -> p b n"), qk[:].rearrange("p b h q -> p b (h q)")).then_inc(
                    sg["stored"], DMA)
                sp.wait_ge(sg["stored"], DMA)

            @block.tensor
            def _(pe):
                pe.wait_ge(sg["weights"], (7 if biased else 4) * DMA)
                for h in range(H):
                    last = pe.matmul(ps[:, h // 4, (h % 4) * D:(h % 4 + 1) * D], w["wqT"][:, h, :], w["wkT"][:, h, :],
                                     start=True, stop=True)
                last.then_inc(sg["m_product"], 1)
                for h in range(H):
                    last = pe.matmul(ps[:, 4 + h // 4, (h % 4) * D:(h % 4 + 1) * D], w["wvT"][:, h, :],
                                     w["wo"][:, h, :], start=True, stop=True)
                last.then_inc(sg["n_product"], 1)
                if biased:
                    pe.wait_ge(sg["n_ready"], 1)
                    for h in range(H):
                        last = pe.matmul(ps[:, 4, h:h + 1], w["wkT"][:, h, :], bq[:, h:h + 1], start=True, stop=True)
                    last.then_inc(sg["wb_product"], 1)
                    for h in range(H):
                        pe.matmul(ps[0:TP, 5, 0:D], bv[:, h, :], w["wo"][:, h, :], start=(h == 0), stop=False)
                    pe.matmul(ps[0:TP, 5, 0:D], c.ones[0:1, 0:TP], bo[:], start=False, stop=True).then_inc(
                        sg["ybias_product"], 1)
                pe.wait_ge(sg["m_ready"], 1)
                for h in range(H):
                    slot = 2 * (h % 2)
                    if h >= 2:
                        pe.wait_ge(sg["q_folded"], h - 1)
                    for a in range(2):
                        last = pe.matmul(ps[:, slot + a, 0:HALF], m[:, h, :], zt[:, a * HALF:(a + 1) * HALF],
                                         start=True, stop=True)
                    last.then_inc(sg["q_product"], 1)

            @block.scalar
            def _(act):
                act.wait_ge(sg["m_product"], 1)
                act.activation(m[:].rearrange("p (a h) d -> p a (h d)", a=4), ps[:, 0:4, :], ACT.Copy).then_inc(
                    sg["m_ready"], 1)
                if biased:
                    act.wait_ge(sg["wb_ready"], 1)
                for h in range(H):
                    slot = 2 * (h % 2)
                    act.wait_ge(sg["q_product"], h + 1)
                    src = halves(ps[:, slot:slot + 2, :]).rearrange("p a (b q) -> p a b q", b=B // 2)
                    dst = qk[:, :, h, :].rearrange("p (a b) q -> p a b q", a=2)
                    if biased:
                        act.activation(dst, src, ACT.Identity, bias=wb[:, h:h + 1]).then_inc(sg["q_folded"], 1)
                    else:
                        act.activation(dst, src, ACT.Copy).then_inc(sg["q_folded"], 1)

            @block.vector
            def _(dve):
                dve.wait_ge(sg["n_product"], 1)
                dve.tensor_copy(n_out[:].rearrange("p (a h) d -> p a (h d)", a=4), ps[:, 4:8, :]).then_inc(
                    sg["n_ready"], 1)
                if biased:
                    dve.wait_ge(sg["wb_product"], 1)
                    dve.tensor_copy(wb[:], ps[:, 4, 0:H]).then_inc(sg["wb_ready"], 1)
                    dve.wait_ge(sg["ybias_product"], 1)
                    dve.tensor_copy(c.ybias[:], ps[0:TP, 5, 0:D]).then_inc(sg["ybias_ready"], 1)


def stage_context_norm(c):
    nc, d, sg = c.nc, c.dram, c.stage("ctxnorm")
    ps = c.ps
    NT = SK // KT
    with ExitStack() as st:
        sb = alloc(c, st)
        raw = sb("cn_raw", [KT, 2, NT, D])
        z = sb("cn_z", [KT, 2, NT, D])
        zt = sb("cn_zt", [D, 2, SK])
        stats = sb("cn_stats", [KT, NT, 6])
        mv = sb("cn_mv", [KT, NT, 2])
        var = sb("cn_var", [KT, NT])
        std = sb("cn_std", [KT, NT])
        rstd = sb("cn_rstd", [KT, NT])
        shift = sb("cn_shift", [KT, 2, NT])
        scale = sb("cn_scale", [KT, 2, NT])
        gb = sb("cn_gb", [D, 2])
        waiter = sb("cn_waiter", [D, 1])
        gbrow = sb("cn_gbrow", [KT, 2, D])
        src = d["ctx"].rearrange("b (t p) d -> b p t d", p=KT)
        dst = d["ctx1"][:, 0:SK, :].rearrange("b (t p) d -> b p t d", p=KT)
        with nc.Block() as block:
            @block.sync
            def _(sp):
                c.clear_old(sp)
                sp.dma_start(gb[:], d["ln_m_col"]).then_inc(sg["affine"], DMA)
                sp.dma_start(gbrow[:], d["ln_m_row"]).then_inc(sg["affine"], DMA)
                for j in range(2):
                    sp.dma_start(raw[:, j, :, :], src[j]).then_inc(sg[f"raw_loaded_{j}"], DMA)
                with sp.Fori(0, PAIRS) as i:
                    for j in range(2):
                        sp.wait_ge(sg["rows_ready"], i * 2 + (j + 1))
                        sp.dma_start(dst[i * 2 + j], z[:, j, :, :]).then_inc(sg["rows_stored"], DMA)
                        sp.wait_ge(sg["zt_ready"], i * 8 + 4 * (j + 1))
                        sp.dma_start(d["ctx1T"][i * 2 + j, :, 0:SK], zt[:, j, :]).then_inc(sg["zt_stored"], DMA)
                sp.wait_ge(sg["rows_stored"], B * DMA)
                sp.wait_ge(sg["zt_stored"], B * DMA)

            @block.vector
            def _(dve):
                dve.wait_ge(sg["affine"], 2 * DMA)
                with dve.Fori(0, PAIRS) as i:
                    for j in range(2):
                        dve.wait_ge(sg[f"raw_loaded_{j}"], i * DMA + DMA)
                        for t in range(NT):
                            last = dve.bn_stats(stats[:, t, :], raw[:, j, t, :])
                        last.then_inc(sg["stats"], 1)
                        dve.wait_ge(sg["stats"], i * 2 + (j + 1))
                        dve.tensor_copy(waiter[:], gb[:, 0:1])
                        for t in range(NT):
                            last = dve.bn_aggr(mv[:, t, :], stats[:, t, :])
                        last.then_inc(sg["aggr"], 1)
                        dve.wait_ge(sg["aggr"], i * 2 + (j + 1))
                        dve.tensor_scalar(var[:], mv[:, :, 1], LN_EPS, None, ALU.add).then_inc(sg["var"], 1)
                        dve.wait_ge(sg["std"], i * 2 + (j + 1))
                        dve.reciprocal(scale[:, j, :], std[:]).then_inc(sg["rstd"], 1)
                        dve.wait_ge(sg["rstd"], i * 2 + (j + 1))
                        dve.scalar_tensor_tensor(shift[:, j, :], mv[:, :, 0], -1.0, scale[:, j, :], ALU.mult,
                                                 ALU.mult).then_inc(sg["shift"], 1)
                        dve.wait_ge(sg["normalised"], i * 2 + (j + 1))
                        dve.wait_ge(sg["transposed"], i * 8 + 4 * (j + 1))
                        dve.tensor_tensor(z[:, j, :, :], z[:, j, :, :],
                                          gbrow[:, 0:1, :].to_broadcast([KT, NT, D]), ALU.mult).then_inc(sg["times_g"], 1)
                        dve.wait_ge(sg["times_g"], i * 2 + (j + 1))
                        dve.tensor_tensor(z[:, j, :, :], z[:, j, :, :],
                                          gbrow[:, 1:2, :].to_broadcast([KT, NT, D]), ALU.add).then_inc(sg["rows_ready"], 1)

            @block.scalar
            def _(act):
                act.wait_ge(sg["affine"], 2 * DMA)

                def pair(i, final):
                    for j in range(2):
                        act.wait_ge(sg["var"], i * 2 + (j + 1))
                        act.activation(std[:], var[:], ACT.Sqrt).then_inc(sg["std"], 1)
                        act.wait_ge(sg["shift"], i * 2 + (j + 1))
                        act.wait_ge(sg["z_free"], i * 2 + (j + 1))
                        for t in range(NT):
                            last = act.activation(z[:, j, t, :], raw[:, j, t, :], ACT.Identity,
                                                  scale=scale[:, j, t:t + 1], bias=shift[:, j, t:t + 1])
                        last.then_inc(sg["normalised"], 1)
                        for q in range(4):
                            act.wait_ge(sg["transposed"], i * 8 + (4 * j + q + 1))
                            act.activation(zt[:, j, q * 375:(q + 1) * 375], ps[:, 4 * j + q, 0:375], ACT.Identity,
                                           scale=gb[:, 0:1], bias=gb[:, 1:2]).then_inc(sg["zt_ready"], 1)
                        if not final:
                            act.dma_start(raw[:, j, :, :], src[i * 2 + (j + 2)]).then_inc(sg[f"raw_loaded_{j}"], DMA)

                with act.Fori(0, PAIRS - 1) as i:
                    pair(i, False)
                pair(PAIRS - 1, True)

            @block.tensor
            def _(pe):
                pe.sem_inc(sg["z_free"], 2)
                with pe.Fori(0, PAIRS) as i:
                    for j in range(2):
                        pe.wait_ge(sg["normalised"], i * 2 + (j + 1))
                        for q in range(4):
                            for k in range(3):
                                last = pe.transpose(ps[:, 4 * j + q, k * KT:(k + 1) * KT], z[:, j, 3 * q + k, :],
                                                    c.ident[0:KT, 0:KT])
                            last.then_inc(sg["transposed"], 1)
                        pe.wait_ge(sg["rows_stored"], i * 2 * DMA + (j + 1) * DMA)
                        pe.wait_ge(sg["zt_stored"], i * 2 * DMA + (j + 1) * DMA)
                        pe.sem_inc(sg["z_free"], 1)


def stage_attention(c, name, n_in, scale, own_keys, side):
    nc, d, sg = c.nc, c.dram, c.stage(name)
    ps = c.ps
    widths = [KT] * (SK // KT) + ([S] if own_keys else [])
    NT = len(widths)
    NK = sum(widths)
    NKP = KT * NT
    chunks = [(k, 500) for k in range(0, SK, 500)] + ([(SK, S)] if own_keys else [])
    NC = len(chunks)
    AU = (H // 2) * NC + 1
    P_BUFS = 3
    ctx_rows = d["ctx1"] if own_keys else d["ctx"]
    ctx_cols = d["ctx1T"] if own_keys else d["ctxT"]
    T_LOADS = 2
    N_LOADS = 1 + (1 if own_keys else 0) + (2 if side else 0)
    S_BANK, U_BANK, A_BANK = 0, 4, 6
    todo = [(hp, n) for hp in range(H // 2) for n in range(NC)]
    places = list(range(1, NT - 1))
    plan = {k: todo[len(todo) * m // len(places):len(todo) * (m + 1) // len(places)] for m, k in enumerate(places)}

    def batch(i, j):
        return i * 2 + j

    def rows_loads(i):
        return i * (N_LOADS * DMA) + N_LOADS * DMA

    def p_prior(k):
        if k >= P_BUFS:
            return P_BUFS
        return k + NT - max(t for t in range(NT) if t % P_BUFS == k)

    with ExitStack() as st:
        sb = alloc(c, st)
        ct = sb("ct", [D, NK])
        ct_hi = [sb(f"ct_hi{j}", [D, NKP], F32R) for j in range(2)]
        ct_lo = [sb(f"ct_lo{j}", [D, NKP], F32R) for j in range(2)]
        cn = [sb(f"cn{j}", [KT, NT, D]) for j in range(2)]
        qf = sb("qf", [D, HQ])
        q_hi = [sb(f"q_hi{j}", [D, HQ], F32R) for j in range(2)]
        q_lo = [sb(f"q_lo{j}", [D, HQ], F32R) for j in range(2)]
        part_max = sb("part_max", [TP, H // 2, NC])
        row_max = sb("row_max", [TP, H // 2])
        max_hi = sb("max_hi", [TP, H // 2], F32R)
        max_parts = sb("max_parts", [TP, 2 * (H // 2)])
        neg_max = [sb(f"neg_max{j}", [16, HQ], F32R) for j in range(2)]
        negsel = sb("negsel", [16, H // 2, TP])
        ones_r = sb("ones_r", [16, KT], F32R)
        p_buf = [sb(f"p{n}", [KT, HQ]) for n in range(P_BUFS)]
        p_sum = sb("p_sum", [KT, HQ])
        recip = sb("recip", [D, HQ])
        u_norm = sb("u_norm", [D, H, TP])
        y_sb = sb("y_sb", [TP, D])
        if side:
            side_rows = sb("side_rows", [TP, H // 2, SK])
            side_cols = sb("side_cols", [KT, NT, HQ])
            mask_rows = sb("mask_rows", [2, SK], F32R)
            mask_col = [sb(f"mask_col{j}", [KT, NT]) for j in range(2)]
            scratch = sb("scratch", [TP, 500])

        def emit(run, prologue, pairs_loop):
            prologue()
            with run.Fori(0, PAIRS - 1) as i:
                pairs_loop(i, False)
            pairs_loop(PAIRS - 1, True)

        with nc.Block() as block:
            @block.sync
            def _(sp):
                c.clear_old(sp)
                sp.dma_start(negsel[:], d["negsel"]).then_inc(sg["constants"], DMA)
                if side:
                    sp.dma_start(side_rows[:], d["side_rows"]).then_inc(sg["constants"], DMA)

                def load_t(n):
                    sp.dma_start(ct[:], ctx_cols[n]).then_inc(sg["t_loaded"], DMA)
                    sp.dma_start(qf[:], d["qk"][n]).then_inc(sg["t_loaded"], DMA)

                def load_n(n, j):
                    loaded = sg[f"rows_loaded_{j}"]
                    sp.dma_start(cn[j][:, 0:SK // KT, :],
                                 ctx_rows[n, 0:SK, :].rearrange("(t p) d -> p t d", p=KT)).then_inc(loaded, DMA)
                    if own_keys:
                        sp.dma_start(cn[j][0:S, NT - 1, :], ctx_rows[n, SK:SK + S, :]).then_inc(loaded, DMA)
                    if side:
                        sp.dma_start(mask_rows[:].bitcast(F32), d["mask_parts"][n]).then_inc(loaded, DMA)
                        sp.dma_start(mask_col[j][:], d["mask_col"][n]).then_inc(loaded, DMA)

                def prologue():
                    load_t(0)
                    load_n(0, 0)
                    sp.sem_inc(sg["y_sb_free"], 1)
                    sp.wait_ge(sg["parts_made"], 1)
                    load_t(1)
                    if side:
                        sp.dma_start(side_cols[:], d["side_cols"]).then_inc(sg["side_cols_loaded"], DMA)

                def pair(i, final):
                    for j in range(2):
                        n = batch(i, j)
                        if not (final and j == 1):
                            sp.wait_ge(sg["p_applied"], n * NT + P_BUFS)
                            sp.wait_ge(sg["a_read"], n * AU + AU)
                            load_n(n + 1, 1 - j)
                        if not final:
                            sp.wait_ge(sg["parts_made"], n + 2)
                            load_t(n + 2)
                    sp.wait_ge(sg["y_ready"], i + 2)
                    sp.dma_start(d["y"][i], y_sb[:]).then_inc(sg["y_stored"], DMA)
                    sp.wait_ge(sg["y_stored"], i * DMA + DMA)
                    sp.sem_inc(sg["y_sb_free"], 1)

                emit(sp, prologue, pair)
                sp.wait_ge(sg["y_stored"], PAIRS * DMA)

            @block.tensor
            def _(pe):
                pe.sem_inc(sg["p_applied"], P_BUFS)
                for what in ("sum_read", "u_made", "y_ready", "sum_full", "p_ready") + (("side_added",) if side else ()):
                    pe.sem_inc(sg[what], 1)

                def maxima(n, j, hp, m):
                    k0, kn = chunks[m]
                    use = hp * NC + m
                    bank = A_BANK + (j * AU + use) % 2
                    if not (isinstance(n, int) and n * AU + use < 2):
                        pe.wait_ge(sg["a_read"], n * AU + (use - 1))
                    out = ps[0:TP, bank, 0:kn]
                    last = pe.matmul(out, q_hi[j][:, hp * TP:(hp + 1) * TP], ct_hi[j][:, k0:k0 + kn],
                                     start=True, stop=not side)
                    if side:
                        last = pe.matmul(out, ones_r[0:2, 0:TP], mask_rows[:, k0:k0 + kn], start=False, stop=True)
                    last.then_inc(sg["a_full"], 1)

                def turn_maxima(n, j):
                    use = AU - 1
                    bank = A_BANK + (j * AU + use) % 2
                    pe.wait_ge(sg["a_read"], n * AU + (use - 1))
                    pe.wait_ge(sg["max_parts_ready"], n + 1)
                    pe.transpose(ps[0:16, bank, 0:TP], max_parts[:], c.ident[0:TP, 0:TP]).then_inc(sg["a_full"], 1)

                def score(n, j, k):
                    slot = S_BANK + 2 * (k % 2)
                    if k == 0:
                        pe.wait_ge(sg["parts_made"], n + 1)
                        pe.wait_ge(sg["a_read"], n * AU + AU)
                        pe.wait_ge(sg["sum_read"], n + 1)
                    sem = sg["side_added"] if side else sg["p_ready"]
                    pe.wait_ge(sem, n * NT + max(k, 1))
                    for a in range(2):
                        out = ps[0:KT, slot + a, 0:HALF]
                        cols = slice(a * HALF, (a + 1) * HALF)
                        keys = slice(k * KT, (k + 1) * KT)
                        pe.matmul(out, ct_hi[j][:, keys], q_hi[j][:, cols], start=True, stop=False)
                        pe.matmul(out, ct_hi[j][:, keys], q_lo[j][:, cols], start=False, stop=False)
                        pe.matmul(out, ct_lo[j][:, keys], q_hi[j][:, cols], start=False, stop=False)
                        last = pe.matmul(out, ones_r[:], neg_max[j][:, cols], start=False, stop=True)
                    last.then_inc(sg["scores_full"], 1)

                def apply(n, j, k):
                    kn = widths[k]
                    if k == 0:
                        pe.wait_ge(sg[f"rows_loaded_{j}"], rows_loads(c.pair_of))
                        pe.wait_ge(sg["u_made"], n + 1)
                        if j == 0:
                            pe.wait_ge(sg["y_ready"], c.pair_of + 1)
                    pe.wait_ge(sg["p_ready"], n * NT + (k + 2))
                    for a in range(2):
                        last = pe.matmul(ps[:, U_BANK + a, 0:HALF], cn[j][0:kn, k, :],
                                         p_buf[k % P_BUFS][0:kn, a * HALF:(a + 1) * HALF],
                                         start=(k == 0), stop=(k == NT - 1))
                    last.then_inc(sg["p_applied"], 1)

                def total(n):
                    slot = S_BANK + 2 * (NT % 2)
                    pe.wait_ge(sg["p_summed"], n * NT + (NT + P_BUFS))
                    if NT % 2 != (NT - 1) % 2:
                        pe.wait_ge(sg["side_added"] if side else sg["p_ready"], n * NT + NT)
                    for a in range(2):
                        last = pe.matmul(ps[:, slot + a, 0:HALF], c.ones[0:KT, :], p_sum[:, a * HALF:(a + 1) * HALF],
                                         start=True, stop=True)
                    last.then_inc(sg["sum_full"], 1)

                def project(i):
                    pe.wait_ge(sg["u_made"], i * 2 + 3)
                    for h in range(H):
                        last = pe.matmul(ps[0:TP, U_BANK, 0:D], u_norm[:, h, :], n_in[:, h, :],
                                         start=(h == 0), stop=(h == H - 1))
                    last.then_inc(sg["y_full"], 1)

                def prologue():
                    pe.wait_ge(sg["parts_made"], 1)
                    pe.wait_ge(sg["ones_made"], 1)
                    pe.wait_ge(sg["constants"], (2 if side else 1) * DMA)
                    pe.wait_ge(sg["rows_loaded_0"], N_LOADS * DMA)
                    for hp, m in todo:
                        maxima(0, 0, hp, m)
                    turn_maxima(0, 0)

                def pair(i, final):
                    c.pair_of = i
                    for j in range(2):
                        n = batch(i, j)
                        ahead = not (final and j == 1)
                        for k in range(NT):
                            score(n, j, k)
                            if ahead and k in plan:
                                if k == places[0]:
                                    pe.wait_ge(sg["parts_made"], n + 2)
                                    if side:
                                        pe.wait_ge(sg[f"rows_loaded_{1 - j}"], rows_loads(i + j))
                                for hp, m in plan[k]:
                                    maxima(n + 1, 1 - j, hp, m)
                            if k >= 1:
                                apply(n, j, k - 1)
                        apply(n, j, NT - 1)
                        if ahead:
                            turn_maxima(n + 1, 1 - j)
                        total(n)
                    project(i)

                emit(pe, prologue, pair)

            @block.scalar
            def _(act):
                def split_high(n, j):
                    act.wait_ge(sg["t_loaded"], n * (T_LOADS * DMA) + T_LOADS * DMA)
                    act.activation(ct_hi[j][:, 0:NK], ct[:], ACT.Copy)
                    act.activation(q_hi[j][:], qf[:], ACT.Copy).then_inc(sg["high_made"], 1)

                def pair(i, final):
                    for j in range(2):
                        n = batch(i, j)
                        for k in range(NT):
                            kn = widths[k]
                            p = p_buf[k % P_BUFS][0:kn, :]
                            if side:
                                act.wait_ge(sg["side_added"], n * NT + (k + 2))
                                if k == 0:
                                    act.wait_ge(sg[f"rows_loaded_{j}"], rows_loads(i))
                                act.activation(p, p, ACT.Exp, bias=mask_col[j][:, k:k + 1]).then_inc(sg["p_ready"], 1)
                            else:
                                act.wait_ge(sg["scores_full"], n * NT + (k + 1))
                                free = n * NT + (k + 1 - p_prior(k) + P_BUFS)
                                act.wait_ge(sg["p_applied"], free)
                                act.wait_ge(sg["p_summed"], free)
                                src = ps[0:kn, S_BANK + 2 * (k % 2):S_BANK + 2 * (k % 2) + 2, :]
                                act.activation(two(p), halves(src), ACT.Exp, scale=scale).then_inc(sg["p_ready"], 1)
                            if k == 0 and not (final and j == 1):
                                split_high(n + 1, 1 - j)

                emit(act, lambda: split_high(0, 0), pair)

            @block.gpsimd
            def _(pool):
                pool.sem_inc(sg["p_summed"], P_BUFS)

                def pair(i, final):
                    for j in range(2):
                        n = batch(i, j)
                        for k in range(NT):
                            kn = widths[k]
                            p = p_buf[k % P_BUFS]
                            if k == 0:
                                continue
                            pool.wait_ge(sg["p_ready"], n * NT + (k + 2))
                            if k == 1:
                                pool.wait_ge(sg["sum_full"], n + 1)
                                pool.tensor_tensor(p_sum[:], p_buf[0][:], p[:], ALU.add).then_inc(sg["p_summed"], 2)
                            else:
                                pool.wait_ge(sg["p_summed"], n * NT + (k + P_BUFS))
                                pool.tensor_tensor(p_sum[0:kn, :], p_sum[0:kn, :], p[0:kn, :], ALU.add).then_inc(
                                    sg["p_summed"], 1)

                emit(pool, lambda: None, pair)

            @block.vector
            def _(dve):
                def split_low(n, j):
                    dve.wait_ge(sg["high_made"], n + 1)
                    dve.tensor_tensor(ct_lo[j][:, 0:NK], ct[:], ct_hi[j][:, 0:NK].bitcast(F32), ALU.subtract)
                    dve.tensor_tensor(q_lo[j][:], qf[:], q_hi[j][:].bitcast(F32), ALU.subtract).then_inc(
                        sg["parts_made"], 1)

                def read_maxima(n, j, hp, m):
                    k0, kn = chunks[m]
                    use = hp * NC + m
                    bank = A_BANK + (j * AU + use) % 2
                    dve.wait_ge(sg["a_full"], n * AU + (use + 1))
                    if side:
                        if not (isinstance(n, int) and n * AU + use < 1):
                            dve.wait_ge(sg["a_read"], n * AU + use)
                        dve.sem_inc(sg["chunk_seen"], 1)
                        dve.tensor_tensor_reduce(scratch[:, 0:kn], ps[0:TP, bank, 0:kn], side_rows[:, hp, k0:k0 + kn],
                                                 1.0, -3.0e38, ALU.add, ALU.max,
                                                 part_max[:, hp, m:m + 1]).then_inc(sg["a_read"], 1)
                    else:
                        dve.tensor_reduce(part_max[:, hp, m:m + 1], ps[0:TP, bank, 0:kn], X, ALU.max).then_inc(
                            sg["a_read"], 1)

                def finish_maxima(n, j):
                    bank = A_BANK + (j * AU + AU - 1) % 2
                    dve.wait_ge(sg["a_read"], n * AU + (AU - 1))
                    dve.tensor_reduce(row_max[:], part_max[:], X, ALU.max).then_inc(sg["row_max"], 1)
                    dve.wait_ge(sg["row_max"], n + 1)
                    dve.tensor_copy(max_hi[:], row_max[:]).then_inc(sg["max_hi"], 1)
                    dve.wait_ge(sg["max_hi"], n + 1)
                    dve.tensor_copy(max_parts[:, 0:H // 2], max_hi[:].bitcast(F32))
                    dve.tensor_tensor(max_parts[:, H // 2:H], row_max[:], max_hi[:].bitcast(F32),
                                      ALU.subtract).then_inc(sg["max_parts_ready"], 1)
                    dve.wait_ge(sg["a_full"], n * AU + AU)
                    dve.tensor_tensor(neg_max[j][:].rearrange("p (a c) -> p a c", a=H // 2),
                                      ps[0:16, bank:bank + 1, 0:TP].to_broadcast([16, H // 2, TP]), negsel[:],
                                      ALU.mult).then_inc(sg["a_read"], 1)

                def prologue():
                    for j in range(2):
                        if NKP > NK:
                            dve.memset(ct_hi[j][:, NK:NKP].bitcast(F32), 0.0)
                            dve.memset(ct_lo[j][:, NK:NKP].bitcast(F32), 0.0)
                    dve.memset(ones_r[:].bitcast(F32), 1.0).then_inc(sg["ones_made"], 1)
                    dve.wait_ge(sg["ones_made"], 1)
                    dve.wait_ge(sg["constants"], (2 if side else 1) * DMA)
                    split_low(0, 0)
                    for hp, m in todo:
                        read_maxima(0, 0, hp, m)
                    finish_maxima(0, 0)
                    if side:
                        dve.wait_ge(sg["side_cols_loaded"], DMA)

                def pair(i, final):
                    for j in range(2):
                        n = batch(i, j)
                        ahead = not (final and j == 1)
                        for k in range(NT):
                            if side:
                                free = n * NT + (k + 1 - p_prior(k) + P_BUFS)
                                dve.wait_ge(sg["scores_full"], n * NT + (k + 1))
                                dve.wait_ge(sg["p_applied"], free)
                                dve.wait_ge(sg["p_summed"], free)
                                src = ps[0:KT, S_BANK + 2 * (k % 2):S_BANK + 2 * (k % 2) + 2, :]
                                dve.tensor_tensor(two(p_buf[k % P_BUFS][:]), halves(src), two(side_cols[:, k, :]),
                                                  ALU.add).then_inc(sg["side_added"], 1)
                            if ahead:
                                if k == 0:
                                    split_low(n + 1, 1 - j)
                                for hp, m in plan.get(k, ()):
                                    read_maxima(n + 1, 1 - j, hp, m)
                        if ahead:
                            finish_maxima(n + 1, 1 - j)
                        slot = S_BANK + 2 * (NT % 2)
                        dve.wait_ge(sg["sum_full"], n + 2)
                        dve.reciprocal(two(recip[:]), halves(ps[:, slot:slot + 2, :])).then_inc(sg["sum_read"], 1)
                        dve.wait_ge(sg["sum_read"], n + 2)
                        dve.wait_ge(sg["p_applied"], n * NT + (NT + P_BUFS))
                        dve.tensor_tensor(
                            u_norm[:, :, j * S:(j + 1) * S].rearrange("p (a h) q -> p a h q", a=2),
                            halves(ps[:, U_BANK:U_BANK + 2, :]).rearrange("p a (h q) -> p a h q", q=S),
                            recip[:].rearrange("p (a h q) -> p a h q", a=2, q=S), ALU.mult).then_inc(sg["u_made"], 1)
                    dve.wait_ge(sg["y_full"], i + 1)
                    dve.wait_ge(sg["y_sb_free"], i + 1)
                    dve.tensor_copy(y_sb[:], ps[0:TP, U_BANK, 0:D]).then_inc(sg["y_ready"], 1)

                emit(dve, prologue, pair)


def stage_add_y(c, biased):
    nc, d, sg = c.nc, c.dram, c.stage("addy")
    with nc.sbuf_tensor(f"y_all{c.count}", [TP, PAIRS, D], F32) as y, nc.Block() as block:
        @block.sync
        def _(sp):
            c.clear_old(sp)
            sp.dma_start(y[:], d["y"].rearrange("t p d -> p t d")).then_inc(sg["y_loaded"], DMA)
            sp.wait_ge(sg["y_loaded"], DMA)

        @block.vector
        def _(dve):
            dve.wait_ge(sg["y_loaded"], DMA)
            dve.tensor_tensor(c.x[:], c.x[:], y[:], ALU.add).then_inc(sg["x_added"], 1)
            if biased:
                dve.wait_ge(sg["x_added"], 1)
                dve.tensor_tensor(c.x[:], c.x[:], c.ybias[:].unsqueeze(1).to_broadcast([TP, PAIRS, D]),
                                  ALU.add).then_inc(sg["x_added"], 1)


def stage_store(c):
    nc, d, sg = c.nc, c.dram, c.stage("store")
    with nc.Block() as block:
        @block.sync
        def _(sp):
            c.clear_old(sp)
            sp.dma_start(d["out"].rearrange("(t p) d -> p t d", p=TP), c.x[:]).then_inc(sg["stored"], DMA)
            sp.wait_ge(sg["stored"], DMA)


def stage_own_keys(c, z, zt):
    nc, d, sg = c.nc, c.dram, c.stage("own")
    with nc.Block() as block:
        @block.sync
        def _(sp):
            c.clear_old(sp)
            for j in range(2):
                rows = d["ctx1"][:, SK:SK + S, :].rearrange("(t j) q d -> j q t d", j=2)
                sp.dma_start(rows[j], z[j * S:(j + 1) * S, :, :]).then_inc(sg["stored"], DMA)
            sp.dma_start(d["ctx1T"][:, :, SK:SK + S].rearrange("b p q -> p b q"),
                         zt[:].rearrange("p (b q) -> p b q", q=S)).then_inc(sg["stored"], DMA)
            sp.wait_ge(sg["stored"], 3 * DMA)


def stage_qkv(c, layer, zt, q_t, k_t, v_ext, wo, wo_bias):
    nc, d, sg = c.nc, c.dram, c.stage("qkv")
    ps = c.ps
    with ExitStack() as st:
        sb = alloc(c, st)
        w = {k: sb(k, [D, D]) for k in ("wq", "wk", "wv")}
        bqk = sb("bqk", [D, 2])
        bvo = sb("bvo", [1, 2, D])
        with nc.Block() as block:
            @block.sync
            def _(sp):
                c.clear_old(sp)
                for k in ("wq", "wk", "wv"):
                    sp.dma_start(w[k][:], d[f"f0_{k}"][layer]).then_inc(sg["weights"], DMA)
                sp.dma_start(wo[:], d["f0_wo"][layer]).then_inc(sg["weights"], DMA)
                sp.dma_start(bqk[:], d["f0_bqk"][layer]).then_inc(sg["weights"], DMA)
                sp.dma_start(bvo[:], d["f0_bvo"][layer:layer + 1]).then_inc(sg["weights"], DMA)

            @block.tensor
            def _(pe):
                pe.wait_ge(sg["weights"], 6 * DMA)
                for n, k in enumerate(("wq", "wk")):
                    for a in range(2):
                        last = pe.matmul(ps[:, 2 * n + a, 0:HALF], w[k][:], zt[:, a * HALF:(a + 1) * HALF],
                                         start=True, stop=True)
                    last.then_inc(sg["qk_product"], 1)
                for t in range(PAIRS):
                    out = ps[0:TP, 4 + t // 4, (t % 4) * D:(t % 4 + 1) * D]
                    pe.matmul(out, zt[:, t * TP:(t + 1) * TP], w["wv"][:], start=True, stop=False)
                    last = pe.matmul(out, c.ones[0:1, 0:TP], bvo[:, 0, :], start=False, stop=True)
                last.then_inc(sg["v_product"], 1)
                last = pe.matmul(ps[0:TP, 6, 0:D], c.ones[0:1, 0:TP], bvo[:, 1, :], start=True, stop=True)
                last.then_inc(sg["bo_product"], 1)

            @block.scalar
            def _(act):
                act.wait_ge(sg["weights"], 6 * DMA)
                act.wait_ge(sg["qk_product"], 1)
                act.activation(two(q_t[:]), halves(ps[:, 0:2, :]), ACT.Identity, bias=bqk[:, 0:1]).then_inc(sg["q_ready"], 1)
                act.wait_ge(sg["qk_product"], 2)
                act.activation(two(k_t[:]), halves(ps[:, 2:4, :]), ACT.Identity, bias=bqk[:, 1:2]).then_inc(sg["k_ready"], 1)

            @block.vector
            def _(dve):
                dve.memset(v_ext[:, :, :, 8:9], 1.0)
                dve.wait_ge(sg["v_product"], 1)
                for a in range(2):
                    dve.tensor_copy(v_ext[:, 4 * a:4 * a + 4, :, 0:8],
                                    ps[0:TP, 4 + a, :].rearrange("p (t h e) -> p t h e", t=4, h=H)).then_inc(sg["v_ready"], 1)
                dve.wait_ge(sg["bo_product"], 1)
                dve.tensor_copy(wo_bias[:], ps[0:TP, 6, 0:D]).then_inc(sg["bo_ready"], 1)


def stage_self_attention(c, r, q_t, k_t, v_ext, wo, wo_bias):
    nc, d, sg = c.nc, c.dram, c.stage("self")
    ps = c.ps
    with ExitStack() as st:
        sb = alloc(c, st)
        head_of = sb("head_of", [D, H])
        causal = sb("causal", [TP, TP])
        k_wide = sb("k_wide", [D, H, TP])
        q_now = sb("q_now", [D, TP])
        sc = sb("sc", [TP, H, TP])
        mx = sb("mx", [TP, H])
        p_t = sb("p_t", [TP, H, TP])
        rs = sb("rs", [TP, H])
        o = sb("o", [TP, H, 8])
        o_t = sb("o_t", [D, TP])
        with nc.Block() as block:
            @block.sync
            def _(sp):
                c.clear_old(sp)
                sp.dma_start(head_of[:], d["head_of"]).then_inc(sg["masks"], DMA)
                sp.dma_start(causal[:], d["causal"]).then_inc(sg["masks"], DMA)

            @block.gpsimd
            def _(pool):
                pool.wait_ge(sg["masks"], 2 * DMA)
                pool.sem_inc(sg["k_wide_free"], 1)
                with pool.Fori(0, PAIRS) as i:
                    pool.wait_ge(sg["k_wide_free"], i + 1)
                    pool.tensor_tensor(k_wide[:], k_t[:, bass.ts(i, TP)].unsqueeze(1).to_broadcast([D, H, TP]),
                                       head_of[:].unsqueeze(2).to_broadcast([D, H, TP]), ALU.mult).then_inc(
                        sg["k_wide_made"], 1)

            @block.tensor
            def _(pe):
                with pe.Fori(0, PAIRS) as i:
                    pe.wait_ge(sg["k_wide_made"], i + 1)
                    pe.wait_ge(sg["q_now"], i + 1)
                    for a in range(4):
                        last = pe.matmul(ps[0:TP, a, 0:HALF], q_now[:], k_wide[:, 4 * a:4 * a + 4, :], start=True, stop=True)
                    last.then_inc(sg["k_wide_free"], 1)
                    pe.wait_ge(sg["exp_done"], i + 1)
                    for h in range(H):
                        last = pe.transpose(ps[0:TP, 4 + h // 4, (h % 4) * TP:(h % 4 + 1) * TP], sc[:, h, :],
                                            c.ident[0:TP, 0:TP])
                    last.then_inc(sg["p_turned"], 1)
                    pe.wait_ge(sg["p_t_ready"], i + 1)
                    for h in range(H):
                        last = pe.matmul(ps[0:TP, 0, h * 16:h * 16 + 9], p_t[:, h, :],
                                         v_ext[:, bass.ts(i, 1), h, :], start=True, stop=True)
                    last.then_inc(sg["o_product"], 1)
                    pe.wait_ge(sg["o_ready"], i + 1)
                    pe.transpose(ps[:, 1, 0:TP], o[:].rearrange("p h e -> p (h e)"), c.ident[0:TP, 0:TP]).then_inc(
                        sg["o_turned"], 1)
                    pe.wait_ge(sg["o_t_ready"], i + 1)
                    pe.matmul(ps[0:TP, 2, 0:D], o_t[:], wo[:], start=True, stop=True).then_inc(sg["y_product"], 1)

            @block.scalar
            def _(act):
                with act.Fori(0, PAIRS) as i:
                    act.wait_ge(sg["y_added_or_start"], i + 1)
                    act.activation(q_now[:], q_t[:, bass.ts(i, TP)], ACT.Copy).then_inc(sg["q_now"], 1)
                    act.wait_ge(sg["less_max"], i + 1)
                    act.activation(sc[:], sc[:], ACT.Exp).then_inc(sg["exp_done"], 1)
                    act.wait_ge(sg["p_turned"], i + 1)
                    act.activation(p_t[:].rearrange("p (a h) q -> p a (h q)", a=4), ps[0:TP, 4:8, 0:HALF], ACT.Copy).then_inc(
                        sg["p_t_ready"], 1)
                    act.wait_ge(sg["o_turned"], i + 1)
                    act.activation(o_t[:], ps[:, 1, 0:TP], ACT.Copy).then_inc(sg["o_t_ready"], 1)

            @block.vector
            def _(dve):
                dve.wait_ge(sg["masks"], 2 * DMA)
                dve.tensor_tensor(r[:], r[:], wo_bias[:].unsqueeze(1).to_broadcast([TP, PAIRS, D]), ALU.add).then_inc(
                    sg["y_added_or_start"], 1)
                with dve.Fori(0, PAIRS) as i:
                    dve.wait_ge(sg["k_wide_free"], i + 2)
                    for a in range(4):
                        last = dve.scalar_tensor_tensor(
                            sc[:, 4 * a:4 * a + 4, :], ps[0:TP, a, 0:HALF].rearrange("p (h q) -> p h q", q=TP), 8 ** -0.5,
                            causal[:].unsqueeze(1).to_broadcast([TP, 4, TP]), ALU.mult, ALU.add)
                    last.then_inc(sg["masked"], 1)
                    dve.wait_ge(sg["masked"], i + 1)
                    dve.tensor_reduce(mx[:], sc[:], X, ALU.max).then_inc(sg["mx"], 1)
                    dve.wait_ge(sg["mx"], i + 1)
                    dve.tensor_tensor(sc[:], sc[:], mx[:].unsqueeze(2).to_broadcast([TP, H, TP]), ALU.subtract).then_inc(
                        sg["less_max"], 1)
                    dve.wait_ge(sg["o_product"], i + 1)
                    o_ps = ps[0:TP, 0, 0:256].rearrange("p (h e) -> p h e", h=H)
                    dve.reciprocal(rs[:].unsqueeze(2), o_ps[:, :, 8:9]).then_inc(sg["rs"], 1)
                    dve.wait_ge(sg["rs"], i + 1)
                    dve.tensor_tensor(o[:], o_ps[:, :, 0:8], rs[:].unsqueeze(2).to_broadcast([TP, H, 8]), ALU.mult).then_inc(
                        sg["o_ready"], 1)
                    dve.wait_ge(sg["y_product"], i + 1)
                    rt = r[:, bass.ts(i, 1), :]
                    dve.tensor_tensor(rt, rt, ps[0:TP, 2:3, 0:D], ALU.add).then_inc(sg["y_added_or_start"], 1)


def stage_top2(c, ht, gate_w, gate_b, cw, of_batch_mean):
    nc, d, sg = c.nc, c.dram, c.stage("top2")
    ps = c.ps
    with ExitStack() as st:
        sb = alloc(c, st)
        gw = sb("gw", [D, E])
        gb = sb("gb", [1, E])
        earlier = sb("earlier", [TP, E, E])
        sums = sb("sums", [D, B])
        mean = sb("mean", [D, TOK])
        lg = sb("lg", [TP, PAIRS, E])
        gt = sb("gt", [TP, PAIRS, E, E])
        eq = sb("eq", [TP, PAIRS, E, E])
        rank = sb("rank", [TP, PAIRS, E])
        mx = sb("mx", [TP, PAIRS])
        ex = sb("ex", [TP, PAIRS, E])
        tot = sb("tot", [TP, PAIRS])
        src = mean if of_batch_mean else ht
        with nc.Block() as block:
            @block.sync
            def _(sp):
                c.clear_old(sp)
                sp.dma_start(gw[:], gate_w).then_inc(sg["weights"], DMA)
                sp.dma_start(gb[:], gate_b).then_inc(sg["weights"], DMA)
                sp.dma_start(earlier[:], d["earlier"]).then_inc(sg["weights"], DMA)

            @block.tensor
            def _(pe):
                pe.wait_ge(sg["weights"], 3 * DMA)
                if of_batch_mean:
                    pe.wait_ge(sg["mean_ready"], 1)
                for t in range(PAIRS):
                    out = ps[0:TP, 0, t * E:(t + 1) * E]
                    pe.matmul(out, src[:, t * TP:(t + 1) * TP], gw[:], start=True, stop=False)
                    last = pe.matmul(out, c.ones[0:1, 0:TP], gb[:], start=False, stop=True)
                last.then_inc(sg["logits"], 1)

            @block.scalar
            def _(act):
                act.wait_ge(sg["less_max"], 1)
                act.activation(ex[:], ex[:], ACT.Exp).then_inc(sg["exp_done"], 1)

            @block.vector
            def _(dve):
                link = Link(dve, sg["dve_chain"])
                if of_batch_mean:
                    link(dve.tensor_reduce(sums[:], ht[:].rearrange("p (b q) -> p b q", q=S), X, ALU.add))
                    dve.tensor_scalar(mean[:].rearrange("p (b q) -> p b q", q=S),
                                      sums[:].unsqueeze(2).to_broadcast([D, B, S]), 1.0 / S, None,
                                      ALU.mult).then_inc(sg["mean_ready"], 1)
                dve.wait_ge(sg["weights"], 3 * DMA)
                dve.wait_ge(sg["logits"], 1)
                link(dve.tensor_copy(lg[:], ps[0:TP, 0, 0:PAIRS * E].rearrange("p (t e) -> p t e", e=E)))
                other = lg[:].unsqueeze(2).to_broadcast([TP, PAIRS, E, E])
                mine = lg[:].unsqueeze(3).to_broadcast([TP, PAIRS, E, E])
                link(dve.tensor_reduce(mx[:], lg[:], X, ALU.max))
                dve.tensor_tensor(ex[:], lg[:], mx[:].unsqueeze(2).to_broadcast([TP, PAIRS, E]), ALU.subtract).then_inc(
                    sg["less_max"], 1)
                link(dve.tensor_tensor(gt[:], other, mine, ALU.is_gt))
                link(dve.tensor_tensor(eq[:], other, mine, ALU.is_equal))
                link(dve.tensor_tensor(eq[:], eq[:], earlier[:].unsqueeze(1).to_broadcast([TP, PAIRS, E, E]), ALU.mult))
                link(dve.tensor_tensor(gt[:], gt[:], eq[:], ALU.add))
                link(dve.tensor_reduce(rank[:], gt[:], X, ALU.add))
                dve.wait_ge(sg["exp_done"], 1)
                link(dve.scalar_tensor_tensor(ex[:], rank[:], 2.0, ex[:], ALU.is_lt, ALU.mult))
                link(dve.tensor_reduce(tot[:], ex[:], X, ALU.add))
                link(dve.reciprocal(tot[:], tot[:]))
                dve.tensor_tensor(cw[:].rearrange("p e t -> p t e"), ex[:],
                                  tot[:].unsqueeze(2).to_broadcast([TP, PAIRS, E]), ALU.mult).then_inc(sg["cw_ready"], 1)


def stage_capacity(c, zt, cw):
    nc, d, sg = c.nc, c.dram, c.stage("cap")
    ps = c.ps
    with ExitStack() as st:
        sb = alloc(c, st)
        gw = sb("gw", [D, E])
        same = sb("same", [TP, TP])
        before = sb("before", [TP, TP])
        pr = sb("pr", [TP, PAIRS, E])
        mx = sb("mx", [TP, PAIRS])
        tot = sb("tot", [TP, PAIRS])
        diag = sb("diag", [TP, 2, E, TP])
        gt = sb("gt", [TP, E, TP])
        eq = sb("eq", [TP, E, TP])
        rank = sb("rank", [TP, PAIRS, E])

        def over_t(ap):
            return ap.unsqueeze(1).to_broadcast([TP, E, TP])

        with nc.Block() as block:
            @block.sync
            def _(sp):
                c.clear_old(sp)
                sp.dma_start(gw[:], d["f2_gate_w"]).then_inc(sg["weights"], DMA)
                sp.dma_start(same[:], d["same"]).then_inc(sg["weights"], DMA)
                sp.dma_start(before[:], d["before"]).then_inc(sg["weights"], DMA)

            @block.tensor
            def _(pe):
                pe.wait_ge(sg["weights"], 3 * DMA)
                for t in range(PAIRS):
                    last = pe.matmul(ps[0:TP, 0, t * E:(t + 1) * E], zt[:, t * TP:(t + 1) * TP], gw[:],
                                     start=True, stop=True)
                last.then_inc(sg["scores"], 1)
                with pe.Fori(0, PAIRS // 2) as i:
                    for j in range(2):
                        pe.wait_ge(sg["diag_made"], i * 2 + (j + 1))
                        for a in range(2):
                            last = pe.matmul(ps[0:TP, 2 + 2 * j + a, 0:HALF], c.ones[0:TP, 0:TP],
                                             diag[:, j, 4 * a:4 * a + 4, :], start=True, stop=True)
                        last.then_inc(sg["spread"], 1)

            @block.scalar
            def _(act):
                act.wait_ge(sg["less_max"], 1)
                act.activation(pr[:], pr[:], ACT.Exp).then_inc(sg["exp_done"], 1)

            @block.vector
            def _(dve):
                link = Link(dve, sg["dve_chain"])
                dve.wait_ge(sg["weights"], 3 * DMA)
                dve.wait_ge(sg["scores"], 1)
                scores = ps[0:TP, 0, 0:PAIRS * E].rearrange("p (t e) -> p t e", e=E)
                link(dve.tensor_reduce(mx[:], scores, X, ALU.max))
                dve.tensor_tensor(pr[:], scores, mx[:].unsqueeze(2).to_broadcast([TP, PAIRS, E]), ALU.subtract).then_inc(
                    sg["less_max"], 1)
                dve.wait_ge(sg["exp_done"], 1)
                link(dve.tensor_reduce(tot[:], pr[:], X, ALU.add))
                link(dve.reciprocal(tot[:], tot[:]))
                link(dve.tensor_tensor(pr[:], pr[:], tot[:].unsqueeze(2).to_broadcast([TP, PAIRS, E]), ALU.mult))
                with dve.Fori(0, PAIRS // 2) as i:
                    for j in range(2):
                        mine = pr[:, i * 2 + j, :].unsqueeze(2).to_broadcast([TP, E, TP])
                        dve.tensor_tensor(diag[:, j, :, :], over_t(c.ident[0:TP, 0:TP]), mine, ALU.mult).then_inc(
                            sg["diag_made"], 1)
                        dve.wait_ge(sg["spread"], i * 2 + (j + 1))
                        theirs = ps[0:TP, 2 + 2 * j:4 + 2 * j, 0:HALF].rearrange("p a (e t) -> p a e t", t=TP)
                        mine4 = pr[:, i * 2 + j, :].rearrange("p (a e) -> p a e", a=2).unsqueeze(3).to_broadcast([TP, 2, E // 2, TP])
                        gt4 = gt[:].rearrange("p (a e) t -> p a e t", a=2)
                        eq4 = eq[:].rearrange("p (a e) t -> p a e t", a=2)
                        dve.tensor_tensor(gt4, theirs, mine4, ALU.is_gt)
                        dve.tensor_tensor(eq4, theirs, mine4, ALU.is_equal).then_inc(sg["compared"], 1)
                        dve.wait_ge(sg["compared"], i * 2 + (j + 1))
                        dve.tensor_tensor(gt[:], gt[:], over_t(same[:]), ALU.mult)
                        dve.tensor_tensor(eq[:], eq[:], over_t(before[:]), ALU.mult).then_inc(sg["kept"], 1)
                        dve.wait_ge(sg["kept"], i * 2 + (j + 1))
                        dve.tensor_tensor(gt[:], gt[:], eq[:], ALU.add).then_inc(sg["before_me"], 1)
                        dve.wait_ge(sg["before_me"], i * 2 + (j + 1))
                        dve.tensor_reduce(rank[:, i * 2 + j, :], gt[:], X, ALU.add).then_inc(sg["rank"], 1)
                dve.wait_ge(sg["rank"], PAIRS)
                dve.scalar_tensor_tensor(cw[:].rearrange("p e t -> p t e"), rank[:], float(CAP), pr[:], ALU.is_lt,
                                         ALU.mult).then_inc(sg["cw_ready"], 1)


def stage_experts(c, ht, acc, cw, w1, w2, b1=None, b2=None):
    nc, d, sg = c.nc, c.dram, c.stage("experts")
    ps = c.ps
    F = DFF // 128
    with ExitStack() as st:
        sb = alloc(c, st)
        w1s = [sb(f"w1_{j}", [D, DFF]) for j in range(2)]
        w2s = [sb(f"w2_{j}", [128, F, D]) for j in range(2)]
        g = sb("g", [128, 2, F, TOK])
        if b1 is not None:
            b1s = sb("b1", [128, E, F])
            b2s = sb("b2", [E, D])
            cw_t = sb("cw_t", [E, PAIRS, TP])
        UP, DOWN = 0, 4

        def emit(run, before, step):
            before()
            with run.Fori(0, E // 2 - 1) as i:
                for j in range(2):
                    step(i, j, True, True)
            for j in range(2):
                step(E // 2 - 1, j, False, j == 0)

        with nc.Block() as block:
            @block.sync
            def _(sp):
                c.clear_old(sp)

                def before():
                    if b1 is not None:
                        sp.dma_start(b1s[:], b1).then_inc(sg["biases"], DMA)
                        sp.dma_start(b2s[:], b2).then_inc(sg["biases"], DMA)
                    for j in range(2):
                        sp.dma_start(w1s[j][:], w1[:, j, :]).then_inc(sg[f"w1_{j}"], DMA)
                        sp.dma_start(w2s[j][:], w2[:, j, :, :]).then_inc(sg[f"w2_{j}"], DMA)

                def step(i, j, two_more, one_more):
                    if two_more:
                        sp.wait_ge(sg["up_full"], i * 8 + 4 * (j + 1))
                        sp.dma_start(w1s[j][:], w1[:, i * 2 + (j + 2), :]).then_inc(sg[f"w1_{j}"], DMA)
                        sp.wait_ge(sg["down_full"], i * 2 + (j + 3))
                        sp.dma_start(w2s[j][:], w2[:, i * 2 + (j + 2), :, :]).then_inc(sg[f"w2_{j}"], DMA)

                emit(sp, before, step)

            @block.tensor
            def _(pe):
                def up(i, j):
                    pe.wait_ge(sg[f"w1_{j}"], i * DMA + DMA)
                    for f in range(F):
                        bank = UP + 2 * (f % 2)
                        pe.wait_ge(sg["gelu_done"], i * 8 + (4 * j + f + 1))
                        for a in range(2):
                            last = pe.matmul(ps[:, bank + a, 0:HALF], w1s[j][:, f * 128:(f + 1) * 128],
                                             ht[:, a * HALF:(a + 1) * HALF], start=True, stop=True)
                        last.then_inc(sg["up_full"], 1)

                def down(i, j):
                    pe.wait_ge(sg[f"w2_{j}"], i * DMA + DMA)
                    pe.wait_ge(sg["combined"], i * 2 + (j + 1))
                    pe.wait_ge(sg["gelu_done"], i * 8 + (4 * (j + 1) + 2))
                    for t in range(PAIRS):
                        for f in range(F):
                            last = pe.matmul(ps[0:TP, DOWN + 2 * j + t // 4, (t % 4) * D:(t % 4 + 1) * D],
                                             g[:, j, f, t * TP:(t + 1) * TP], w2s[j][:, f, :],
                                             start=(f == 0), stop=(f == F - 1))
                    last.then_inc(sg["down_full"], 1)

                def before():
                    pe.sem_inc(sg["gelu_done"], 2)
                    pe.sem_inc(sg["combined"], 2)
                    pe.sem_inc(sg["down_full"], 2)
                    if b1 is not None:
                        for t in range(PAIRS):
                            last = pe.transpose(ps[0:E, t // 4, (t % 4) * TP:(t % 4 + 1) * TP], cw[:, :, t],
                                                c.ident[0:TP, 0:TP])
                        last.then_inc(sg["cw_turned"], 1)
                        pe.wait_ge(sg["cw_t_ready"], 1)
                        pe.wait_ge(sg["biases"], 2 * DMA)
                        for t in range(PAIRS):
                            last = pe.matmul(ps[0:TP, 2 + t // 4, (t % 4) * D:(t % 4 + 1) * D], cw_t[:, t, :], b2s[:],
                                             start=True, stop=True)
                        last.then_inc(sg["b2_product"], 1)
                        pe.wait_ge(sg["b2_added"], 1)
                    up(0, 0)

                def step(i, j, two_more, one_more):
                    if one_more:
                        up(i + j, 1 - j)
                    down(i, j)

                emit(pe, before, step)

            @block.scalar
            def _(act):
                def before():
                    if b1 is not None:
                        act.wait_ge(sg["biases"], 2 * DMA)

                def step(i, j, two_more, one_more):
                    act.wait_ge(sg["down_full"], i * 2 + (j + 1))
                    for f in range(F):
                        act.wait_ge(sg["up_full"], i * 8 + (4 * j + f + 1))
                        src = halves(ps[:, UP + 2 * (f % 2):UP + 2 * (f % 2) + 2, :])
                        bias = b1s[:, i * 2 + j, f:f + 1] if b1 is not None else 0.0
                        act.activation(two(g[:, j, f, :]), src, ACT.Gelu, bias=bias).then_inc(sg["gelu_done"], 1)

                emit(act, before, step)

            @block.vector
            def _(dve):
                def before():
                    if b1 is not None:
                        dve.wait_ge(sg["cw_turned"], 1)
                        dve.tensor_copy(cw_t[:].rearrange("e (a t) q -> e a (t q)", a=2), ps[0:E, 0:2, 0:HALF]).then_inc(
                            sg["cw_t_ready"], 1)
                        dve.wait_ge(sg["b2_product"], 1)
                        dve.tensor_tensor(acc[:].rearrange("p (a t) d -> p a (t d)", a=2),
                                          acc[:].rearrange("p (a t) d -> p a (t d)", a=2), ps[0:TP, 2:4, :],
                                          ALU.add).then_inc(sg["b2_added"], 1)
                        dve.wait_ge(sg["b2_added"], 1)

                def step(i, j, two_more, one_more):
                    dve.wait_ge(sg["down_full"], i * 2 + (j + 3))
                    dve.wait_ge(sg["combined"], i * 2 + (j + 2))
                    for t in range(PAIRS):
                        last = dve.scalar_tensor_tensor(
                            acc[:, t, :], ps[0:TP, DOWN + 2 * j + t // 4, (t % 4) * D:(t % 4 + 1) * D],
                            cw[:, i * 2 + j, t:t + 1], acc[:, t, :], ALU.mult, ALU.add)
                    last.then_inc(sg["combined"], 1)

                emit(dve, before, step)


def stage_add(c, dst, src):
    nc, sg = c.nc, c.stage("add")
    with nc.Block() as block:
        @block.sync
        def _(sp):
            c.clear_old(sp)

        @block.vector
        def _(dve):
            dve.tensor_tensor(dst[:], dst[:], src[:], ALU.add).then_inc(sg["added"], 1)


def layer0_ffn(c):
    d = c.dram
    with ExitStack() as st:
        sb = alloc(c, st)
        r = sb("r", [TP, PAIRS, D])
        z = sb("z", [TP, PAIRS, D])
        zt = sb("zt", [D, TOK])
        cw = sb("cw", [TP, E, PAIRS])
        stage_norm(c, c.x, r)
        for layer in range(2):
            stage_norm(c, r, z, zt, affine=(d["ln1_w"][layer], d["ln1_b"][layer]))
            with ExitStack() as inner:
                sb = alloc(c, inner)
                q_t, k_t = sb("q_t", [D, TOK]), sb("k_t", [D, TOK])
                v_ext = sb("v_ext", [TP, PAIRS, H, 9])
                wo, wo_bias = sb("wo", [D, D]), sb("wo_bias", [TP, D])
                stage_qkv(c, layer, zt, q_t, k_t, v_ext, wo, wo_bias)
                stage_self_attention(c, r, q_t, k_t, v_ext, wo, wo_bias)
            stage_norm(c, r, z, zt, affine=(d["ln2_w"][layer], d["ln2_b"][layer]))
            stage_top2(c, zt, d["f0_gate_w"][layer], d["f0_gate_b"][layer], cw, of_batch_mean=(layer == 1))
            stage_experts(c, zt, r, cw, d["f0_w1"][layer], d["f0_w2"][layer], d["f0_b1"][layer], d["f0_b2"][layer])
        stage_add(c, c.x, r)


def layer1_ffn(c):
    with ExitStack() as st:
        sb = alloc(c, st)
        z = sb("z", [TP, PAIRS, D])
        zt = sb("zt", [D, TOK])
        stage_norm(c, c.x, z, zt)
        nc, d, sg = c.nc, c.dram, c.stage("ternary")
        ps = c.ps
        F = 4
        w = [sb(f"w{n}", [128, 512]) for n in range(2)]
        t0 = [sb(f"t{n}", [128, 512]) for n in range(2)]
        b1 = sb("b1", [128, F])
        b2 = sb("b2", [1, D])
        mag = sb("mag", [128, 2])
        thr = sb("thr", [128, 2, 2])
        g = sb("g", [128, F, TOK])
        with nc.Block() as block:
            @block.sync
            def _(sp):
                c.clear_old(sp)
                sp.dma_start(w[0][:], d["f1_w1T"]).then_inc(sg["weights"], DMA)
                sp.dma_start(w[1][:], d["f1_w2T"].rearrange("p f d -> p (f d)")).then_inc(sg["weights"], DMA)
                sp.dma_start(b1[:], d["f1_b1"]).then_inc(sg["weights"], DMA)
                sp.dma_start(b2[:], d["f1_b2"]).then_inc(sg["weights"], DMA)

            @block.vector
            def _(dve):
                link = Link(dve, sg["dve_chain"])
                dve.wait_ge(sg["weights"], 4 * DMA)
                for n in range(2):
                    last = dve.tensor_reduce(mag[:, n:n + 1], w[n][:], X, ALU.add, apply_absolute_value=True)
                last.then_inc(sg["magnitudes"], 1)
                dve.wait_ge(sg["magnitudes_summed"], 1)
                link(dve.tensor_scalar(thr[:, 0, :], ps[:, 0, 0:2], 1.0 / (128 * 512), 1e-8, ALU.mult, ALU.max))
                link(dve.tensor_scalar(thr[:, 0, :], thr[:, 0, :], 0.5, None, ALU.mult))
                link(dve.tensor_scalar(thr[:, 1, :], thr[:, 0, :], -1.0, None, ALU.mult))
                for n in range(2):
                    link(dve.tensor_scalar(t0[n][:], w[n][:], thr[:, 1, n:n + 1], None, ALU.is_lt))
                    link(dve.scalar_tensor_tensor(t0[n][:], w[n][:], thr[:, 0, n:n + 1], t0[n][:], ALU.is_gt, ALU.subtract))
                    link(dve.tensor_tensor(t0[n][:], t0[n][:], w[n][:], ALU.subtract))
                    link(dve.tensor_tensor(w[n][:], w[n][:], t0[n][:], ALU.add))
                dve.engine_nop().then_inc(sg["ternary_made"], 1)
                dve.wait_ge(sg["y_product"], 1)
                x2 = c.x[:].rearrange("p (a t) d -> p a (t d)", a=2)
                dve.tensor_tensor(x2, x2, ps[0:TP, 6:8, :], ALU.add).then_inc(sg["x_added"], 1)

            @block.tensor
            def _(pe):
                pe.wait_ge(sg["magnitudes"], 1)
                pe.matmul(ps[:, 0, 0:2], c.ones[:], mag[:], start=True, stop=True).then_inc(sg["magnitudes_summed"], 1)
                pe.wait_ge(sg["ternary_made"], 1)
                for f in range(F):
                    bank = 2 * (f % 3)
                    if f >= 3:
                        pe.wait_ge(sg["gelu_done"], f - 2)
                    for a in range(2):
                        last = pe.matmul(ps[:, bank + a, 0:HALF], w[0][:, f * 128:(f + 1) * 128],
                                         zt[:, a * HALF:(a + 1) * HALF], start=True, stop=True)
                    last.then_inc(sg["up_full"], 1)
                pe.wait_ge(sg["gelu_done"], F)
                for t in range(PAIRS):
                    out = ps[0:TP, 6 + t // 4, (t % 4) * D:(t % 4 + 1) * D]
                    for f in range(F):
                        pe.matmul(out, g[:, f, t * TP:(t + 1) * TP], w[1][:, f * D:(f + 1) * D],
                                  start=(f == 0), stop=False)
                    last = pe.matmul(out, c.ones[0:1, 0:TP], b2[:], start=False, stop=True)
                last.then_inc(sg["y_product"], 1)

            @block.scalar
            def _(act):
                act.wait_ge(sg["weights"], 4 * DMA)
                for f in range(F):
                    act.wait_ge(sg["up_full"], f + 1)
                    bank = 2 * (f % 3)
                    act.activation(two(g[:, f, :]), halves(ps[:, bank:bank + 2, :]), ACT.Gelu,
                                   bias=b1[:, f:f + 1]).then_inc(sg["gelu_done"], 1)


def layer2_attention(c):
    with ExitStack() as st:
        sb = alloc(c, st)
        z = sb("z", [TP, PAIRS, D])
        zt = sb("zt", [D, TOK])
        stage_norm(c, c.x, z, zt)
        nc, d, sg = c.nc, c.dram, c.stage("a2")
        ps = c.ps
        k_rows = sb("k_rows", [TP, PAIRS, D])
        k_cols = sb("k_cols", [D, TOK])
        causal = sb("causal", [TP, TP])
        sc = sb("sc", [TP, PAIRS, TP])
        mx = sb("mx", [TP, PAIRS])
        tot = sb("tot", [TP, PAIRS])
        p_t = sb("p_t", [TP, PAIRS, TP])

        def slot(bank, t, n=TP):
            return ps[0:TP, bank + t // 4, (t % 4) * n:(t % 4 + 1) * n]

        with nc.Block() as block:
            @block.sync
            def _(sp):
                c.clear_old(sp)
                sp.dma_start(k_rows[:], d["own_rows"]).then_inc(sg["loaded"], DMA)
                sp.dma_start(k_cols[:], d["own_cols"]).then_inc(sg["loaded"], DMA)
                sp.dma_start(causal[:], d["causal"]).then_inc(sg["loaded"], DMA)

            @block.tensor
            def _(pe):
                pe.wait_ge(sg["loaded"], 3 * DMA)
                for t in range(PAIRS):
                    last = pe.matmul(slot(0, t), zt[:, t * TP:(t + 1) * TP], k_cols[:, t * TP:(t + 1) * TP],
                                     start=True, stop=True)
                last.then_inc(sg["scores"], 1)
                pe.wait_ge(sg["p_ready"], 1)
                for t in range(PAIRS):
                    last = pe.transpose(slot(2, t), sc[:, t, :], c.ident[0:TP, 0:TP])
                last.then_inc(sg["p_turned"], 1)
                pe.wait_ge(sg["p_t_ready"], 1)
                for t in range(PAIRS):
                    last = pe.matmul(slot(4, t, D), p_t[:, t, :], k_rows[:, t, :], start=True, stop=True)
                last.then_inc(sg["y_product"], 1)

            @block.scalar
            def _(act):
                act.wait_ge(sg["less_max"], 1)
                act.activation(sc[:], sc[:], ACT.Exp).then_inc(sg["exp_done"], 1)
                act.wait_ge(sg["p_turned"], 1)
                act.activation(p_t[:].rearrange("p (a t) k -> p a (t k)", a=2), ps[0:TP, 2:4, 0:HALF], ACT.Copy).then_inc(
                    sg["p_t_ready"], 1)

            @block.vector
            def _(dve):
                link = Link(dve, sg["dve_chain"])
                dve.wait_ge(sg["loaded"], 3 * DMA)
                dve.wait_ge(sg["scores"], 1)
                for a in range(2):
                    last = dve.scalar_tensor_tensor(
                        sc[:, 4 * a:4 * a + 4, :], ps[0:TP, a, 0:HALF].rearrange("p (t k) -> p t k", k=TP), D ** -0.5,
                        causal[:].unsqueeze(1).to_broadcast([TP, 4, TP]), ALU.mult, ALU.add)
                link(last)
                link(dve.tensor_reduce(mx[:], sc[:], X, ALU.max))
                dve.tensor_tensor(sc[:], sc[:], mx[:].unsqueeze(2).to_broadcast([TP, PAIRS, TP]), ALU.subtract).then_inc(
                    sg["less_max"], 1)
                dve.wait_ge(sg["exp_done"], 1)
                link(dve.tensor_reduce(tot[:], sc[:], X, ALU.add))
                link(dve.reciprocal(tot[:], tot[:]))
                dve.tensor_tensor(sc[:], sc[:], tot[:].unsqueeze(2).to_broadcast([TP, PAIRS, TP]), ALU.mult).then_inc(
                    sg["p_ready"], 1)
                dve.wait_ge(sg["y_product"], 1)
                x2 = c.x[:].rearrange("p (a t) d -> p a (t d)", a=2)
                dve.tensor_tensor(x2, x2, ps[0:TP, 4:6, :], ALU.add).then_inc(sg["x_added"], 1)


def layer2_ffn(c):
    d = c.dram
    with ExitStack() as st:
        sb = alloc(c, st)
        z = sb("z", [TP, PAIRS, D])
        zt = sb("zt", [D, TOK])
        cw = sb("cw", [TP, E, PAIRS])
        stage_norm(c, c.x, z, zt)
        stage_capacity(c, zt, cw)
        stage_experts(c, zt, c.x, cw, d["f2_w1"], d["f2_w2"])


def stage_mask(c):
    nc, d, sg = c.nc, c.dram, c.stage("mask")
    with ExitStack() as st:
        sb = alloc(c, st)
        m = sb("m", [B, SK])
        hi = sb("hi", [B, SK], F32R)
        lo = sb("lo", [B, SK], F32R)
        with nc.Block() as block:
            @block.sync
            def _(sp):
                c.clear_old(sp)
                sp.dma_start(m[:], d["mask"]).then_inc(sg["loaded"], DMA)
                sp.wait_ge(sg["low"], 1)
                sp.dma_start(d["mask_parts"][:, 0, :], hi[:].bitcast(F32)).then_inc(sg["stored"], DMA)
                sp.dma_start(d["mask_parts"][:, 1, :], lo[:].bitcast(F32)).then_inc(sg["stored"], DMA)
                sp.wait_ge(sg["stored"], 2 * DMA)

            @block.vector
            def _(dve):
                dve.wait_ge(sg["loaded"], DMA)
                dve.tensor_copy(hi[:], m[:]).then_inc(sg["high"], 1)
                dve.wait_ge(sg["high"], 1)
                dve.tensor_tensor(lo[:], m[:], hi[:].bitcast(F32), ALU.subtract).then_inc(sg["low"], 1)


TINY = 1.17549435e-38
ERFC = [-1.26551223, 1.00002368, 0.37409196, 0.09678418, -0.18628806, 0.27886807, -1.13520398, 1.48851587,
        -0.82215223, 0.17087277]


def layer3_ffn(c):
    with ExitStack() as st:
        sb = alloc(c, st)
        z = sb("z", [TP, PAIRS, D])
        stage_norm(c, c.x, z)
        nc, d, sg = c.nc, c.dram, c.stage("tree")
        W = PAIRS * TREE_P
        RI, RO = 8, 8
        ROW = FAN * D + FAN
        node = sb("node", [TP, PAIRS, TREE_P])
        index = sb("index", [TP, 2, PAIRS, TREE_P], U32)
        platform = sb("platform", [TP, PAIRS, TREE_P])
        fan_less = sb("fan_less", [TP, W, FAN])
        row_in = sb("row_in", [TP, RI, ROW])
        row_out = sb("row_out", [TP, RO, FAN * D])
        prod = sb("prod", [TP, FAN, D])
        logit = sb("logit", [TP, W, FAN])
        gel = sb("gel", [TP, 2, W, FAN])
        mag, frac, poly, half_sq = (sb(k, [TP, W, FAN]) for k in ("mag", "frac", "poly", "half_sq"))
        best = sb("best", [TP, W])
        eq = sb("eq", [TP, W, FAN])
        move = sb("move", [TP, PAIRS, TREE_P])
        levels = range(DEPTH + 1)
        first = [sum(FAN ** k for k in range(n)) for n in levels]
        with nc.Block() as block:
            @block.sync
            def _(sp):
                c.clear_old(sp)
                sp.dma_start(platform[:], d["platform"]).then_inc(sg["constants"], DMA)
                sp.dma_start(fan_less[:], d["fan_less"]).then_inc(sg["constants"], DMA)

            def fetch_out(pool, level, w):
                t, p = w // TREE_P, w % TREE_P
                use = level * W + w
                if use >= RO:
                    pool.wait_ge(sg["row_out_used"], use - RO + 1)
                pool.indirect_dma_start(
                    row_out[:, use % RO, :], None, d["tree_out"],
                    bass.IndirectOffsetOnAxis(ap=index[:, level % 2, t, p:p + 1], axis=0)).then_inc(
                    sg[f"row_out_{use % RO}"], DMA)

            @block.gpsimd
            def _(pool):
                for level in levels:
                    pool.wait_ge(sg["index_ready"], level + 1)
                    for w in range(W):
                        t, p = w // TREE_P, w % TREE_P
                        use = level * W + w
                        if use >= RI:
                            pool.wait_ge(sg["row_in_used"], use - RI + 1)
                        pool.indirect_dma_start(
                            row_in[:, use % RI, :], None, d["tree_in"],
                            bass.IndirectOffsetOnAxis(ap=index[:, level % 2, t, p:p + 1], axis=0)).then_inc(
                            sg[f"row_in_{use % RI}"], DMA)
                        if level >= 1:
                            fetch_out(pool, level - 1, w)
                for w in range(W):
                    fetch_out(pool, DEPTH, w)

            @block.scalar
            def _(act):
                for level in levels:
                    act.wait_ge(sg["exponent"], level + 1)
                    act.activation(poly[:], poly[:], ACT.Exp).then_inc(sg["exp_done"], 1)

            @block.vector
            def _(dve):
                link = Link(dve, sg["dve_chain"])

                def add_out(level, w):
                    t = w // TREE_P
                    use = level * W + w
                    dve.wait_ge(sg[f"row_out_{use % RO}"], DMA * (use // RO + 1))
                    for f in range(FAN):
                        link(dve.scalar_tensor_tensor(c.x[:, t, :], row_out[:, use % RO, f * D:(f + 1) * D],
                                                      gel[:, level % 2, w, f:f + 1], c.x[:, t, :], ALU.mult, ALU.add))
                    dve.engine_nop().then_inc(sg["row_out_used"], 1)

                def gelu(level):
                    link(dve.scalar_tensor_tensor(mag[:], logit[:], -1.0, logit[:], ALU.mult, ALU.max))
                    link(dve.tensor_scalar(frac[:], mag[:], 0.5 * 0.5 ** 0.5, 1.0, ALU.mult, ALU.add))
                    link(dve.reciprocal(frac[:], frac[:]))
                    link(dve.tensor_scalar(poly[:], frac[:], ERFC[-1], None, ALU.mult))
                    for coefficient in reversed(ERFC[1:-1]):
                        link(dve.scalar_tensor_tensor(poly[:], poly[:], coefficient, frac[:], ALU.add, ALU.mult))
                    link(dve.scalar_tensor_tensor(half_sq[:], mag[:], 0.5, mag[:], ALU.mult, ALU.mult))
                    dve.scalar_tensor_tensor(poly[:], poly[:], ERFC[0], half_sq[:], ALU.add, ALU.subtract).then_inc(
                        sg["exponent"], 1)
                    dve.wait_ge(sg["exp_done"], level + 1)
                    link(dve.tensor_tensor(poly[:], poly[:], frac[:], ALU.mult))
                    link(dve.scalar_tensor_tensor(poly[:], poly[:], TINY, poly[:], ALU.is_ge, ALU.mult))
                    link(dve.scalar_tensor_tensor(poly[:], mag[:], 0.5, poly[:], ALU.mult, ALU.mult))
                    link(dve.scalar_tensor_tensor(gel[:, level % 2, :, :], logit[:], 0.0, poly[:], ALU.max, ALU.subtract))

                dve.wait_ge(sg["constants"], 2 * DMA)
                link(dve.memset(node[:], 0.0))
                for level in levels:
                    dve.tensor_tensor(index[:, level % 2, :, :], node[:], platform[:], ALU.add).then_inc(sg["index_ready"], 1)
                    for w in range(W):
                        t = w // TREE_P
                        use = level * W + w
                        dve.wait_ge(sg[f"row_in_{use % RI}"], DMA * (use // RI + 1))
                        row = row_in[:, use % RI, :]
                        link(dve.tensor_tensor(prod[:], row[:, 0:FAN * D].rearrange("p (f d) -> p f d", f=FAN),
                                               z[:, t:t + 1, :].to_broadcast([TP, FAN, D]), ALU.mult))
                        link(dve.tensor_reduce(logit[:, w, :], prod[:], X, ALU.add))
                        dve.tensor_tensor(logit[:, w, :], logit[:, w, :], row[:, FAN * D:ROW], ALU.add).then_inc(
                            sg["row_in_used"], 1)
                        if level >= 1:
                            add_out(level - 1, w)
                    dve.wait_ge(sg["row_in_used"], (level + 1) * W)
                    gelu(level)
                    if level < DEPTH:
                        ge = gel[:, level % 2, :, :]
                        link(dve.tensor_reduce(best[:], ge, X, ALU.max))
                        link(dve.tensor_tensor(eq[:], ge, best[:].unsqueeze(2).to_broadcast([TP, W, FAN]), ALU.is_equal))
                        link(dve.tensor_tensor(eq[:], eq[:], fan_less[:], ALU.mult))
                        link(dve.tensor_reduce(move[:].rearrange("p t f -> p (t f)"), eq[:], X, ALU.min))
                        link(dve.tensor_scalar(node[:], node[:], float(FAN),
                                               float(9 + first[level + 1] - FAN * first[level]), ALU.mult, ALU.add))
                        link(dve.tensor_tensor(node[:], node[:], move[:], ALU.add))
                for w in range(W):
                    add_out(DEPTH, w)


LAST = 8


def program(nc, d):
    with ExitStack() as st:
        c = Core(nc, d)
        sb = alloc(c, st)
        c.x = sb("x", [TP, PAIRS, D])
        c.ident = sb("ident", [128, 128])
        c.ones = sb("ones", [128, 128])
        c.ybias = sb("ybias", [TP, D])
        c.ps = st.enter_context(nc.psum_tensor("ps", [128, 8, 512], F32))
        stage_load(c)

        def attend(name, hd, scale, latents=False, side=False):
            with ExitStack() as inner:
                n_prod = alloc(c, inner)(f"n_{name}", [D, H, D])
                with ExitStack() as prep:
                    z = alloc(c, prep)(f"z_{name}", [TP, PAIRS, D])
                    zt = alloc(c, prep)(f"zt_{name}", [D, TOK])
                    if latents:
                        stage_norm(c, c.x, z, None)
                        stage_norm(c, z, z, zt, affine=(d["ln_l_g"], d["ln_l_b"]))
                        stage_own_keys(c, z, zt)
                    else:
                        stage_norm(c, c.x, z, zt)
                    stage_fold(c, name, hd, zt, n_prod, biased=(name == "a0"))
                stage_attention(c, name, n_prod, scale, latents, side)
            stage_add_y(c, biased=(name == "a0"))

        attend("a0", D // H, (D // H) ** -0.5)
        if LAST >= 2:
            layer0_ffn(c)
        if LAST >= 3:
            stage_context_norm(c)
            attend("a1", 64, 64 ** -0.5, latents=True)
        if LAST >= 4:
            layer1_ffn(c)
        if LAST >= 5:
            layer2_attention(c)
        if LAST >= 6:
            layer2_ffn(c)
        if LAST >= 7:
            stage_mask(c)
            attend("a3", 64, 1.0, side=True)
        if LAST >= 8:
            layer3_ffn(c)
        stage_store(c)


def kernel(**a):
    import numpy as np
    import concourse.bacc as bacc
    from concourse import mybir as _mybir
    from concourse.bass_utils import run_bass_kernel_spmd

    a = {k: np.asarray(v) for k, v in a.items()}
    f32 = np.float32
    ins = {}

    def put(name, array):
        ins[name] = np.ascontiguousarray(array)

    def heads_t(w, hd):
        return w.reshape(D, H, hd).transpose(2, 1, 0)

    def heads(w, hd):
        return w.reshape(H, hd, D).transpose(1, 0, 2)

    ctx = a["ctx_1024"]
    put("x", a["x"].reshape(TOK, D))
    put("ctx", ctx)
    put("ctxT", ctx.transpose(0, 2, 1))
    wkv = a["L0_xattn_Wkv"]
    put("a0_wqT", heads_t(a["L0_xattn_Wq"], 8))
    put("a0_wkT", heads_t(wkv[:, :D], 8))
    put("a0_wvT", heads_t(wkv[:, D:], 8))
    put("a0_wo", heads(a["L0_xattn_Wo"], 8))
    put("a0_bq", a["L0_xattn_bq"].reshape(H, 8).T)
    put("a0_bv", np.broadcast_to(a["L0_xattn_bkv"][D:].reshape(H, 8).T[:, :, None], (8, H, TP)))
    put("a0_bo", a["L0_xattn_bo"][None])
    inner = H * 64
    wkv = a["L1_xattn_Wkv"]
    put("a1_wqT", heads_t(a["L1_xattn_Wq"], 64))
    put("a1_wkT", heads_t(wkv[:, :inner], 64))
    put("a1_wvT", heads_t(wkv[:, inner:], 64))
    put("a1_wo", heads(a["L1_xattn_Wout"], 64))
    put("ln_m_col", np.stack([a["L1_xattn_ln_m_g"], a["L1_xattn_ln_m_b"]], 1))
    put("ln_m_row", np.broadcast_to(np.stack([a["L1_xattn_ln_m_g"], a["L1_xattn_ln_m_b"]])[None], (KT, 2, D)))
    for k in ("ln_l_g", "ln_l_b"):
        put(k, np.broadcast_to(a[f"L1_xattn_{k}"][None], (TP, D)))
    for k, name in (("wqT", "Wq"), ("wkT", "Wk"), ("wvT", "Wv")):
        put(f"a3_{k}", heads_t(a[f"L3_xattn_{name}"], 64))
    put("a3_wo", heads(a["L3_xattn_Wo"], 64))
    side = a["fside_1x16xSxS2_0"]
    put("side_rows", side.reshape(H // 2, TP, SK).transpose(1, 0, 2))
    put("side_cols", side.reshape(HQ, SK // KT, KT).transpose(2, 1, 0))
    mask = a["mask_Bx1x1xS2_ff0"].reshape(B, SK)
    put("mask", mask)
    put("mask_col", mask.reshape(B, SK // KT, KT).transpose(0, 2, 1))
    for k in ("ln1_w", "ln1_b", "ln2_w", "ln2_b"):
        put(k, np.broadcast_to(a[f"L0_ffn_{k}"][:, None, :], (2, TP, D)))
    put("f0_wq", a["L0_ffn_wq"])
    put("f0_wk", a["L0_ffn_wk"])
    put("f0_wv", a["L0_ffn_wv"])
    put("f0_wo", a["L0_ffn_wo"])
    put("f0_bqk", np.stack([a["L0_ffn_bq"], a["L0_ffn_bk"]], -1))
    put("f0_bvo", np.stack([a["L0_ffn_bv"], a["L0_ffn_bo"]], 1))
    put("f0_gate_w", a["L0_ffn_gate_w"])
    put("f0_gate_b", a["L0_ffn_gate_b"][:, None, :])
    put("f0_w1", a["L0_ffn_e_w1"].transpose(0, 2, 1, 3))
    put("f0_b1", a["L0_ffn_e_b1"].reshape(2, E, 4, 128).transpose(0, 3, 1, 2))
    put("f0_w2", a["L0_ffn_e_w2"].reshape(2, E, 4, 128, D).transpose(0, 3, 1, 2, 4))
    put("f0_b2", a["L0_ffn_e_b2"])
    put("f1_w1T", a["L1_ffn_W1"].T)
    put("f1_b1", a["L1_ffn_b1"].reshape(4, 128).T)
    put("f1_w2T", a["L1_ffn_W2"].T.reshape(4, 128, D).transpose(1, 0, 2))
    put("f1_b2", a["L1_ffn_b2"][None])
    own = ctx[:, :S, :]
    put("own_rows", own.reshape(PAIRS, TP, D).transpose(1, 0, 2))
    put("own_cols", own.reshape(TOK, D).T)
    put("f2_gate_w", a["L2_ffn_gate_w"])
    put("f2_w1", a["L2_ffn_w1"].transpose(1, 0, 2))
    put("f2_w2", a["L2_ffn_w2"].reshape(E, 4, 128, D).transpose(2, 0, 1, 3))
    nodes = TREE_P * G
    put("tree_in", np.concatenate([a["L3_ffn_W_in"].reshape(nodes, FAN * D), a["L3_ffn_b_in"].reshape(nodes, FAN)], 1))
    put("tree_out", a["L3_ffn_W_out"].T.reshape(nodes, FAN * D))
    put("ident", np.eye(128, dtype=f32))
    put("ones", np.ones((128, 128), f32))
    p16 = np.arange(16)[:, None, None]
    put("negsel", np.broadcast_to(np.where(p16 % 8 == np.arange(8)[None, :, None], f32(-1), f32(0)), (16, 8, TP)))
    r = np.arange(TP)
    same = (r[:, None] // S) == (r[None, :] // S)
    before = same & (r[None, :] < r[:, None])
    put("causal", np.where(same & (r[None, :] <= r[:, None]), f32(0), f32(-1e30)))
    put("same", same.astype(f32))
    put("before", before.astype(f32))
    put("head_of", (np.arange(128)[:, None] // 8 == np.arange(16)[None, :]).astype(f32))
    e8 = np.arange(8)
    put("earlier", np.broadcast_to((e8[None, :] < e8[:, None]).astype(f32)[None], (TP, 8, 8)))
    put("platform", np.broadcast_to(np.arange(4, dtype=f32)[None, None, :] * f32(G), (TP, PAIRS, 4)))
    put("fan_less", np.broadcast_to(np.arange(4, dtype=f32)[None, None, :] - f32(9), (TP, 32, 4)))

    nc = bacc.Bacc("TRN2", target_bir_lowering=False, num_devices=1)
    dram = {k: nc.dram_tensor(k, v.shape, _mybir.dt.from_np(v.dtype), kind="ExternalInput").ap() for k, v in ins.items()}
    dram["qk"] = nc.dram_tensor("qk", (B, D, HQ), F32, kind="Internal").ap()
    dram["y"] = nc.dram_tensor("y", (PAIRS, TP, D), F32, kind="Internal").ap()
    dram["ctx1"] = nc.dram_tensor("ctx1", (B, SK + S, D), F32, kind="Internal").ap()
    dram["ctx1T"] = nc.dram_tensor("ctx1T", (B, D, SK + S), F32, kind="Internal").ap()
    dram["mask_parts"] = nc.dram_tensor("mask_parts", (B, 2, SK), F32, kind="Internal").ap()
    dram["out"] = nc.dram_tensor("out", (TOK, D), F32, kind="ExternalOutput").ap()
    program(nc, dram)
    got = run_bass_kernel_spmd(nc, [ins], core_ids=[0])
    return got.results[0]["out"].reshape(B, S, D)
```

```python
from contextlib import ExitStack

import concourse.bass as bass
from concourse import mybir

F32 = mybir.dt.float32
F32R = mybir.dt.float32r
U32 = mybir.dt.uint32
ALU = mybir.AluOpType
ACT = mybir.ActivationFunctionType
X = mybir.AxisListType.X

B, S, D, SK = 16, 56, 128, 1500
H = 16
PAIRS, TP = B // 2, 2 * S
TOK = B * S
HALF = TOK // 2
HQ = H * S
KT = 125
E, DFF = 8, 512
CAP = 2 * S // E
TREE_P, FAN, DEPTH = 4, 4, 5
G = (FAN ** (DEPTH + 1) - 1) // 3
LN_EPS = 1e-5
DMA = 16


class Signals:

    def __init__(self, nc, stage):
        self.nc, self.stage, self.stack, self.by_name = nc, stage, ExitStack(), {}

    def __getitem__(self, what):
        if what not in self.by_name:
            self.by_name[what] = self.stack.enter_context(self.nc.semaphore(f"{self.stage}_{what}"))
        return self.by_name[what]


class Core:

    def __init__(self, nc, dram):
        self.nc, self.dram = nc, dram
        self.old = None
        self.now = None
        self.count = 0

    def stage(self, name):
        if self.old is not None:
            self.old.stack.close()
        self.old, self.now = self.now, Signals(self.nc, f"s{self.count}_{name}")
        self.count += 1
        return self.now

    def clear_old(self, eng):
        if self.old is not None:
            for sem in self.old.by_name.values():
                eng.sem_clear(sem)


class Link:

    def __init__(self, eng, sem):
        self.eng, self.sem, self.n = eng, sem, 0

    def __call__(self, ins):
        self.n += 1
        ins.then_inc(self.sem, 1)
        self.eng.wait_ge(self.sem, self.n)


def halves(psum_two_banks):
    return psum_two_banks[:, :, 0:HALF]


def two(ap):
    return ap.rearrange("p (a c) -> p a c", a=2)


def alloc(c, stack):
    def sb(name, shape, dt=F32):
        return stack.enter_context(c.nc.sbuf_tensor(f"sb{c.count}_{name}", shape, dt))
    return sb


def stage_load(c):
    nc, d, sg = c.nc, c.dram, c.stage("load")
    with nc.Block() as block:
        @block.sync
        def _(sp):
            sp.dma_start(c.x[:], d["x"].rearrange("(t p) d -> p t d", p=TP)).then_inc(sg["loaded"], DMA)
            sp.dma_start(c.ident[:], d["ident"]).then_inc(sg["loaded"], DMA)
            sp.dma_start(c.ones[:], d["ones"]).then_inc(sg["loaded"], DMA)
            sp.wait_ge(sg["loaded"], 3 * DMA)


def stage_norm(c, src, dst, dst_t=None, affine=None):
    nc, d, sg = c.nc, c.dram, c.stage("norm")
    ps = c.ps
    with ExitStack() as st:
        sb = alloc(c, st)
        stats = sb(f"stats{c.count}", [TP, PAIRS, 6])
        mv = sb(f"mv{c.count}", [TP, PAIRS, 2])
        var = sb(f"var{c.count}", [TP, PAIRS])
        std = sb(f"std{c.count}", [TP, PAIRS])
        rstd = sb(f"rstd{c.count}", [TP, PAIRS])
        gb = sb(f"gb{c.count}", [TP, 2, D]) if affine else None
        with nc.Block() as block:
            @block.sync
            def _(sp):
                c.clear_old(sp)
                if affine:
                    for n, name in enumerate(affine):
                        sp.dma_start(gb[:, n, :], name).then_inc(sg["affine_loaded"], DMA)
                    sp.wait_ge(sg["affine_loaded"], 2 * DMA)

            @block.vector
            def _(dve):
                link = Link(dve, sg["dve_chain"])
                for t in range(PAIRS):
                    last = dve.bn_stats(stats[:, t, :], src[:, t, :])
                link(last)
                for t in range(PAIRS):
                    last = dve.bn_aggr(mv[:, t, :], stats[:, t, :])
                link(last)
                dve.tensor_scalar(var[:], mv[:, :, 1], LN_EPS, None, ALU.add).then_inc(sg["var_ready"], 1)
                dve.wait_ge(sg["std_ready"], 1)
                link(dve.reciprocal(rstd[:], std[:]))
                for t in range(PAIRS):
                    last = dve.tensor_scalar(dst[:, t, :], src[:, t, :], mv[:, t, 0:1], rstd[:, t:t + 1],
                                             ALU.subtract, ALU.mult)
                if affine:
                    link(last)
                    dve.wait_ge(sg["affine_loaded"], 2 * DMA)
                    link(dve.tensor_tensor(dst[:], dst[:], gb[:, 0:1, :].to_broadcast([TP, PAIRS, D]), ALU.mult))
                    last = dve.tensor_tensor(dst[:], dst[:], gb[:, 1:2, :].to_broadcast([TP, PAIRS, D]), ALU.add)
                last.then_inc(sg["dst_ready"], 1)
                if dst_t is not None:
                    dve.wait_ge(sg["transposed"], 1)
                    dve.tensor_copy(two(dst_t[:]), halves(ps[:, 0:2, :])).then_inc(sg["dst_t_ready"], 1)

            @block.scalar
            def _(act):
                act.wait_ge(sg["var_ready"], 1)
                act.activation(std[:], var[:], ACT.Sqrt).then_inc(sg["std_ready"], 1)

            if dst_t is not None:
                @block.tensor
                def _(pe):
                    pe.wait_ge(sg["dst_ready"], 1)
                    for t in range(PAIRS):
                        last = pe.transpose(ps[:, t // 4, (t % 4) * TP:(t % 4 + 1) * TP], dst[:, t, :],
                                            c.ident[0:TP, 0:TP])
                    last.then_inc(sg["transposed"], 1)


def stage_fold(c, name, hd, zt, n_out, biased):
    nc, d, sg = c.nc, c.dram, c.stage("fold")
    ps = c.ps
    with ExitStack() as st:
        sb = alloc(c, st)
        w = {k: sb(f"{k}_{name}", [hd, H, D]) for k in ("wqT", "wkT", "wvT", "wo")}
        m = sb(f"m_{name}", [D, H, D])
        qk = sb(f"qk_{name}", [D, B, H, S])
        if biased:
            bq = sb(f"bq_{name}", [hd, H])
            bv = sb(f"bv_{name}", [hd, H, TP])
            bo = sb(f"bo_{name}", [1, D])
            wb = sb(f"wb_{name}", [D, H])
        with nc.Block() as block:
            @block.sync
            def _(sp):
                c.clear_old(sp)
                for k in ("wqT", "wkT", "wvT", "wo"):
                    sp.dma_start(w[k][:], d[f"{name}_{k}"]).then_inc(sg["weights"], DMA)
                if biased:
                    sp.dma_start(bq[:], d[f"{name}_bq"]).then_inc(sg["weights"], DMA)
                    sp.dma_start(bv[:], d[f"{name}_bv"]).then_inc(sg["weights"], DMA)
                    sp.dma_start(bo[:], d[f"{name}_bo"]).then_inc(sg["weights"], DMA)
                sp.wait_ge(sg["q_folded"], H)
                sp.dma_start(d["qk"].rearrange("b p n -> p b n"), qk[:].rearrange("p b h q -> p b (h q)")).then_inc(
                    sg["stored"], DMA)
                sp.wait_ge(sg["stored"], DMA)

            @block.tensor
            def _(pe):
                pe.wait_ge(sg["weights"], (7 if biased else 4) * DMA)
                for h in range(H):
                    last = pe.matmul(ps[:, h // 4, (h % 4) * D:(h % 4 + 1) * D], w["wqT"][:, h, :], w["wkT"][:, h, :],
                                     start=True, stop=True)
                last.then_inc(sg["m_product"], 1)
                for h in range(H):
                    last = pe.matmul(ps[:, 4 + h // 4, (h % 4) * D:(h % 4 + 1) * D], w["wvT"][:, h, :],
                                     w["wo"][:, h, :], start=True, stop=True)
                last.then_inc(sg["n_product"], 1)
                if biased:
                    pe.wait_ge(sg["n_ready"], 1)
                    for h in range(H):
                        last = pe.matmul(ps[:, 4, h:h + 1], w["wkT"][:, h, :], bq[:, h:h + 1], start=True, stop=True)
                    last.then_inc(sg["wb_product"], 1)
                    for h in range(H):
                        pe.matmul(ps[0:TP, 5, 0:D], bv[:, h, :], w["wo"][:, h, :], start=(h == 0), stop=False)
                    pe.matmul(ps[0:TP, 5, 0:D], c.ones[0:1, 0:TP], bo[:], start=False, stop=True).then_inc(
                        sg["ybias_product"], 1)
                pe.wait_ge(sg["m_ready"], 1)
                for h in range(H):
                    slot = 2 * (h % 2)
                    if h >= 2:
                        pe.wait_ge(sg["q_folded"], h - 1)
                    for a in range(2):
                        last = pe.matmul(ps[:, slot + a, 0:HALF], m[:, h, :], zt[:, a * HALF:(a + 1) * HALF],
                                         start=True, stop=True)
                    last.then_inc(sg["q_product"], 1)

            @block.scalar
            def _(act):
                act.wait_ge(sg["m_product"], 1)
                act.activation(m[:].rearrange("p (a h) d -> p a (h d)", a=4), ps[:, 0:4, :], ACT.Copy).then_inc(
                    sg["m_ready"], 1)
                if biased:
                    act.wait_ge(sg["wb_ready"], 1)
                for h in range(H):
                    slot = 2 * (h % 2)
                    act.wait_ge(sg["q_product"], h + 1)
                    src = halves(ps[:, slot:slot + 2, :]).rearrange("p a (b q) -> p a b q", b=B // 2)
                    dst = qk[:, :, h, :].rearrange("p (a b) q -> p a b q", a=2)
                    if biased:
                        act.activation(dst, src, ACT.Identity, bias=wb[:, h:h + 1]).then_inc(sg["q_folded"], 1)
                    else:
                        act.activation(dst, src, ACT.Copy).then_inc(sg["q_folded"], 1)

            @block.vector
            def _(dve):
                dve.wait_ge(sg["n_product"], 1)
                dve.tensor_copy(n_out[:].rearrange("p (a h) d -> p a (h d)", a=4), ps[:, 4:8, :]).then_inc(
                    sg["n_ready"], 1)
                if biased:
                    dve.wait_ge(sg["wb_product"], 1)
                    dve.tensor_copy(wb[:], ps[:, 4, 0:H]).then_inc(sg["wb_ready"], 1)
                    dve.wait_ge(sg["ybias_product"], 1)
                    dve.tensor_copy(c.ybias[:], ps[0:TP, 5, 0:D]).then_inc(sg["ybias_ready"], 1)


def stage_context_norm(c):
    nc, d, sg = c.nc, c.dram, c.stage("ctxnorm")
    ps = c.ps
    NT = SK // KT
    with ExitStack() as st:
        sb = alloc(c, st)
        raw = sb("cn_raw", [KT, 2, NT, D])
        z = sb("cn_z", [KT, 2, NT, D])
        zt = sb("cn_zt", [D, 2, SK])
        stats = sb("cn_stats", [KT, NT, 6])
        mv = sb("cn_mv", [KT, NT, 2])
        var = sb("cn_var", [KT, NT])
        std = sb("cn_std", [KT, NT])
        rstd = sb("cn_rstd", [KT, NT])
        shift = sb("cn_shift", [KT, 2, NT])
        scale = sb("cn_scale", [KT, 2, NT])
        gb = sb("cn_gb", [D, 2])
        waiter = sb("cn_waiter", [D, 1])
        gbrow = sb("cn_gbrow", [KT, 2, D])
        src = d["ctx"].rearrange("b (t p) d -> b p t d", p=KT)
        dst = d["ctx1"][:, 0:SK, :].rearrange("b (t p) d -> b p t d", p=KT)
        with nc.Block() as block:
            @block.sync
            def _(sp):
                c.clear_old(sp)
                sp.dma_start(gb[:], d["ln_m_col"]).then_inc(sg["affine"], DMA)
                sp.dma_start(gbrow[:], d["ln_m_row"]).then_inc(sg["affine"], DMA)
                for j in range(2):
                    sp.dma_start(raw[:, j, :, :], src[j]).then_inc(sg[f"raw_loaded_{j}"], DMA)
                with sp.Fori(0, PAIRS) as i:
                    for j in range(2):
                        sp.wait_ge(sg["rows_ready"], i * 2 + (j + 1))
                        sp.dma_start(dst[i * 2 + j], z[:, j, :, :]).then_inc(sg["rows_stored"], DMA)
                        sp.wait_ge(sg["zt_ready"], i * 8 + 4 * (j + 1))
                        sp.dma_start(d["ctx1T"][i * 2 + j, :, 0:SK], zt[:, j, :]).then_inc(sg["zt_stored"], DMA)
                sp.wait_ge(sg["rows_stored"], B * DMA)
                sp.wait_ge(sg["zt_stored"], B * DMA)

            @block.vector
            def _(dve):
                dve.wait_ge(sg["affine"], 2 * DMA)
                with dve.Fori(0, PAIRS) as i:
                    for j in range(2):
                        dve.wait_ge(sg[f"raw_loaded_{j}"], i * DMA + DMA)
                        for t in range(NT):
                            last = dve.bn_stats(stats[:, t, :], raw[:, j, t, :])
                        last.then_inc(sg["stats"], 1)
                        dve.wait_ge(sg["stats"], i * 2 + (j + 1))
                        dve.tensor_copy(waiter[:], gb[:, 0:1])
                        for t in range(NT):
                            last = dve.bn_aggr(mv[:, t, :], stats[:, t, :])
                        last.then_inc(sg["aggr"], 1)
                        dve.wait_ge(sg["aggr"], i * 2 + (j + 1))
                        dve.tensor_scalar(var[:], mv[:, :, 1], LN_EPS, None, ALU.add).then_inc(sg["var"], 1)
                        dve.wait_ge(sg["std"], i * 2 + (j + 1))
                        dve.reciprocal(scale[:, j, :], std[:]).then_inc(sg["rstd"], 1)
                        dve.wait_ge(sg["rstd"], i * 2 + (j + 1))
                        dve.scalar_tensor_tensor(shift[:, j, :], mv[:, :, 0], -1.0, scale[:, j, :], ALU.mult,
                                                 ALU.mult).then_inc(sg["shift"], 1)
                        dve.wait_ge(sg["normalised"], i * 2 + (j + 1))
                        dve.wait_ge(sg["transposed"], i * 8 + 4 * (j + 1))
                        dve.tensor_tensor(z[:, j, :, :], z[:, j, :, :],
                                          gbrow[:, 0:1, :].to_broadcast([KT, NT, D]), ALU.mult).then_inc(sg["times_g"], 1)
                        dve.wait_ge(sg["times_g"], i * 2 + (j + 1))
                        dve.tensor_tensor(z[:, j, :, :], z[:, j, :, :],
                                          gbrow[:, 1:2, :].to_broadcast([KT, NT, D]), ALU.add).then_inc(sg["rows_ready"], 1)

            @block.scalar
            def _(act):
                act.wait_ge(sg["affine"], 2 * DMA)

                def pair(i, final):
                    for j in range(2):
                        act.wait_ge(sg["var"], i * 2 + (j + 1))
                        act.activation(std[:], var[:], ACT.Sqrt).then_inc(sg["std"], 1)
                        act.wait_ge(sg["shift"], i * 2 + (j + 1))
                        act.wait_ge(sg["z_free"], i * 2 + (j + 1))
                        for t in range(NT):
                            last = act.activation(z[:, j, t, :], raw[:, j, t, :], ACT.Identity,
                                                  scale=scale[:, j, t:t + 1], bias=shift[:, j, t:t + 1])
                        last.then_inc(sg["normalised"], 1)
                        for q in range(4):
                            act.wait_ge(sg["transposed"], i * 8 + (4 * j + q + 1))
                            act.activation(zt[:, j, q * 375:(q + 1) * 375], ps[:, 4 * j + q, 0:375], ACT.Identity,
                                           scale=gb[:, 0:1], bias=gb[:, 1:2]).then_inc(sg["zt_ready"], 1)
                        if not final:
                            act.dma_start(raw[:, j, :, :], src[i * 2 + (j + 2)]).then_inc(sg[f"raw_loaded_{j}"], DMA)

                with act.Fori(0, PAIRS - 1) as i:
                    pair(i, False)
                pair(PAIRS - 1, True)

            @block.tensor
            def _(pe):
                pe.sem_inc(sg["z_free"], 2)
                with pe.Fori(0, PAIRS) as i:
                    for j in range(2):
                        pe.wait_ge(sg["normalised"], i * 2 + (j + 1))
                        for q in range(4):
                            for k in range(3):
                                last = pe.transpose(ps[:, 4 * j + q, k * KT:(k + 1) * KT], z[:, j, 3 * q + k, :],
                                                    c.ident[0:KT, 0:KT])
                            last.then_inc(sg["transposed"], 1)
                        pe.wait_ge(sg["rows_stored"], i * 2 * DMA + (j + 1) * DMA)
                        pe.wait_ge(sg["zt_stored"], i * 2 * DMA + (j + 1) * DMA)
                        pe.sem_inc(sg["z_free"], 1)


def stage_attention(c, name, n_in, scale, own_keys, side):
    nc, d, sg = c.nc, c.dram, c.stage(name)
    ps = c.ps
    widths = [KT] * (SK // KT) + ([S] if own_keys else [])
    NT = len(widths)
    NK = sum(widths)
    NKP = KT * NT
    chunks = [(k, 500) for k in range(0, SK, 500)] + ([(SK, S)] if own_keys else [])
    NC = len(chunks)
    P_BUFS = 3
    T_LOADS = 2
    N_LOADS = 1 + (1 if own_keys else 0) + (2 if side else 0)
    S_BANK, U_BANK, A_BANK = 0, 4, 6
    ctx_rows = d["ctx1"] if own_keys else d["ctx"]
    ctx_cols = d["ctx1T"] if own_keys else d["ctxT"]

    CH = (H // 2) * NC
    PAIR_USES = 2 * (2 + CH + 1) + 2
    GRANTED = 4

    def use_of(i, j, u):
        return i * PAIR_USES + (CH + 1 + j * (5 + CH) + u)

    def bank_of(j, u):
        return A_BANK + (CH + 1 + j * (5 + CH) + u) % 2

    def first_chunk(j):
        return 4 if j == 0 else 2

    todo = [(hp, m) for hp in range(H // 2) for m in range(NC)]
    NORM_AT, Y_AT = 3, 4

    def spread(first):
        places = range(first, NT - 1)
        return {k: range(CH * n // len(places), CH * (n + 1) // len(places)) for n, k in enumerate(places)}

    plan = [spread(Y_AT), spread(NORM_AT)]

    def batch(i, j):
        return i * 2 + j

    def rows_loads(i):
        return i * (N_LOADS * DMA) + N_LOADS * DMA

    def slot_of(j, k):
        return S_BANK + 2 * ((j * NT + k) % 2)

    def buf_of(j, k):
        return (j * NT + k) % P_BUFS

    def p_free(n, j, k):
        m = j * NT + k
        back = P_BUFS if m >= P_BUFS else m + 2 * NT - max(t for t in range(2 * NT) if t % P_BUFS == m)
        return n * NT + (k + 1 - back + P_BUFS)

    with ExitStack() as st:
        sb = alloc(c, st)
        ct = sb("ct", [D, NK])
        ct_hi = [sb(f"ct_hi{j}", [D, NKP], F32R) for j in range(2)]
        ct_lo = [sb(f"ct_lo{j}", [D, NKP], F32R) for j in range(2)]
        cn = [sb(f"cn{j}", [KT, NT, D]) for j in range(2)]
        qf = sb("qf", [D, HQ])
        q_hi = [sb(f"q_hi{j}", [D, HQ], F32R) for j in range(2)]
        q_lo = [sb(f"q_lo{j}", [D, HQ], F32R) for j in range(2)]
        part_max = sb("part_max", [TP, H // 2, NC])
        row_max = sb("row_max", [TP, H // 2])
        max_hi = sb("max_hi", [TP, H // 2], F32R)
        max_parts = sb("max_parts", [TP, 2 * (H // 2)])
        neg_max = [sb(f"neg_max{j}", [16, HQ], F32R) for j in range(2)]
        negsel = sb("negsel", [16, H // 2, TP])
        ones_r = sb("ones_r", [16, KT], F32R)
        p_buf = [sb(f"p{n}", [KT, HQ]) for n in range(P_BUFS)]
        p_sum = sb("p_sum", [KT, HQ])
        recip = sb("recip", [D, HQ])
        u_norm = sb("u_norm", [D, H, TP])
        y_sb = sb("y_sb", [TP, D])
        if side:
            side_rows = sb("side_rows", [TP, H // 2, SK])
            side_cols = sb("side_cols", [KT, NT, HQ])
            mask_rows = sb("mask_rows", [2, SK], F32R)
            mask_col = [sb(f"mask_col{j}", [KT, NT]) for j in range(2)]
            scratch = sb("scratch", [TP, 500])

        def emit(run, prologue, pair, epilogue):
            prologue()
            pair(0, True, False)
            with run.Fori(1, PAIRS - 1) as i:
                pair(i, False, False)
            pair(PAIRS - 1, False, True)
            epilogue()

        with nc.Block() as block:
            @block.sync
            def _(sp):
                c.clear_old(sp)
                sp.dma_start(negsel[:], d["negsel"]).then_inc(sg["constants"], DMA)

                def load_t(n):
                    sp.dma_start(ct[:], ctx_cols[n]).then_inc(sg["t_loaded"], DMA)
                    sp.dma_start(qf[:], d["qk"][n]).then_inc(sg["t_loaded"], DMA)

                def load_n(n, j):
                    loaded = sg[f"rows_loaded_{j}"]
                    sp.dma_start(cn[j][:, 0:SK // KT, :],
                                 ctx_rows[n, 0:SK, :].rearrange("(t p) d -> p t d", p=KT)).then_inc(loaded, DMA)
                    if own_keys:
                        sp.dma_start(cn[j][0:S, NT - 1, :], ctx_rows[n, SK:SK + S, :]).then_inc(loaded, DMA)
                    if side:
                        sp.dma_start(mask_rows[:].bitcast(F32), d["mask_parts"][n]).then_inc(loaded, DMA)
                        sp.dma_start(mask_col[j][:], d["mask_col"][n]).then_inc(loaded, DMA)

                def store_y(i):
                    sp.wait_ge(sg["a_read"], use_of(i, 0, 4))
                    sp.sem_inc(sg["sp_seen"], 1)
                    sp.dma_start(d["y"][i - 1], y_sb[:]).then_inc(sg["y_stored"], DMA)
                    sp.wait_ge(sg["y_stored"], i * DMA)
                    sp.sem_inc(sg["y_sb_free"], 1)

                def prologue():
                    load_t(0)
                    load_n(0, 0)
                    if side:
                        sp.dma_start(side_rows[:], d["side_rows"]).then_inc(sg["constants"], DMA)
                    sp.sem_inc(sg["y_sb_free"], 1)
                    sp.wait_ge(sg["parts_made"], 1)
                    load_t(1)
                    if side:
                        sp.dma_start(side_cols[:], d["side_cols"]).then_inc(sg["side_cols_loaded"], DMA)

                def pair(i, first, final):
                    for j in range(2):
                        n = batch(i, j)
                        if not (final and j == 1):
                            sp.wait_ge(sg["p_applied"], n * NT + P_BUFS)
                            sp.sem_inc(sg["sp_seen"], 1)
                            sp.wait_ge(sg["a_read"], use_of(i, j, GRANTED if first and j == 0 else 0))
                            sp.sem_inc(sg["sp_seen"], 1)
                            load_n(n + 1, 1 - j)
                        if j == 0 and not first:
                            store_y(i)
                        if not final:
                            sp.wait_ge(sg["parts_made"], n + 2)
                            sp.sem_inc(sg["sp_seen"], 1)
                            load_t(n + 2)

                emit(sp, prologue, pair, lambda: store_y(PAIRS))

            @block.tensor
            def _(pe):
                pe.sem_inc(sg["p_applied"], P_BUFS)
                pe.sem_inc(sg["a_full"], GRANTED)
                pe.sem_inc(sg["a_read"], GRANTED)
                for what in ("u_read", "sum_full", "p_ready", "u_made") + (("side_added",) if side else ()):
                    pe.sem_inc(sg[what], 1)

                def maxima(i, j, u, nj, hp, m):
                    k0, kn = chunks[m]
                    pe.wait_ge(sg["a_read"], use_of(i, j, u - 1))
                    out = ps[0:TP, bank_of(j, u), 0:kn]
                    last = pe.matmul(out, q_hi[nj][:, hp * TP:(hp + 1) * TP], ct_hi[nj][:, k0:k0 + kn],
                                     start=True, stop=not side)
                    if side:
                        last = pe.matmul(out, ones_r[0:2, 0:TP], mask_rows[:, k0:k0 + kn], start=False, stop=True)
                    last.then_inc(sg["a_full"], 1)

                def turn_maxima(i, j, u, n):
                    pe.wait_ge(sg["max_parts_ready"], n + 1)
                    pe.wait_ge(sg["a_read"], use_of(i, j, u - 1))
                    pe.transpose(ps[0:16, bank_of(j, u), 0:TP], max_parts[:], c.ident[0:TP, 0:TP]).then_inc(sg["a_full"], 1)

                def score(i, j, k, first):
                    n = batch(i, j)
                    slot = slot_of(j, k)
                    if k == 0:
                        pe.wait_ge(sg["parts_made"], n + 1)
                    if not (first and j == 0 and k < 2):
                        pe.wait_ge(sg["side_added"] if side else sg["p_ready"], n * NT + k)
                    for a in range(2):
                        out = ps[0:KT, slot + a, 0:HALF]
                        cols = slice(a * HALF, (a + 1) * HALF)
                        keys = slice(k * KT, (k + 1) * KT)
                        pe.matmul(out, ct_hi[j][:, keys], q_hi[j][:, cols], start=True, stop=False)
                        pe.matmul(out, ct_hi[j][:, keys], q_lo[j][:, cols], start=False, stop=False)
                        pe.matmul(out, ct_lo[j][:, keys], q_hi[j][:, cols], start=False, stop=False)
                        if k == 0 and a == 0:
                            pe.wait_ge(sg["a_read"], use_of(i, j, GRANTED if first and j == 0 else 0))
                        last = pe.matmul(out, ones_r[:], neg_max[j][:, cols], start=False, stop=True)
                    last.then_inc(sg["scores_full"], 1)

                def apply(i, j, k):
                    n = batch(i, j)
                    kn = widths[k]
                    if k == 0:
                        pe.wait_ge(sg[f"rows_loaded_{j}"], rows_loads(i))
                        pe.wait_ge(sg["u_read"], n + 1)
                    pe.wait_ge(sg["p_ready"], n * NT + (k + 2))
                    for a in range(2):
                        last = pe.matmul(ps[:, U_BANK + a, 0:HALF], cn[j][0:kn, k, :],
                                         p_buf[buf_of(j, k)][0:kn, a * HALF:(a + 1) * HALF],
                                         start=(k == 0), stop=(k == NT - 1))
                    last.then_inc(sg["p_applied"], 1)

                def total(i, j, n):
                    pe.wait_ge(sg["p_summed"], n * NT + P_BUFS)
                    pe.wait_ge(sg["a_read"], use_of(i, j, 0))
                    for a in range(2):
                        pe.matmul(ps[:, bank_of(j, a), 0:HALF], c.ones[0:KT, :], p_sum[:, a * HALF:(a + 1) * HALF],
                                  start=True, stop=True).then_inc(sg["a_full"], 1)

                def project(i):
                    pe.wait_ge(sg["u_made"], i * 2 + 1)
                    pe.wait_ge(sg["a_read"], use_of(i, 0, 2))
                    for a in range(2):
                        for h in range(H):
                            last = pe.matmul(ps[0:TP, bank_of(0, 2 + a), 0:64], u_norm[:, h, :],
                                             n_in[:, h, a * 64:(a + 1) * 64], start=(h == 0), stop=(h == H - 1))
                        last.then_inc(sg["a_full"], 1)

                def prologue():
                    pe.wait_ge(sg["high_made"], 1)
                    pe.wait_ge(sg["ones_made"], 1)
                    pe.wait_ge(sg["constants"], (2 if side else 1) * DMA)
                    pe.wait_ge(sg["rows_loaded_0"], N_LOADS * DMA)
                    for u, (hp, m) in enumerate(todo):
                        maxima(0, 0, u + GRANTED - (CH + 1), 0, hp, m)
                    turn_maxima(0, 0, CH + GRANTED - (CH + 1), 0)

                def pair(i, first, final):
                    for j in range(2):
                        n = batch(i, j)
                        start, ahead = first and j == 0, not (final and j == 1)
                        for k in range(NT):
                            score(i, j, k, first)
                            if k == 1 and not start:
                                total(i, j, n)
                            if k == Y_AT and j == 0 and not first:
                                project(i)
                            if ahead and k in plan[j]:
                                if k == min(plan[j]):
                                    pe.wait_ge(sg["high_made"], n + 2)
                                    pe.wait_ge(sg["a_read"], use_of(i, j, first_chunk(j)))
                                    if side:
                                        pe.wait_ge(sg[f"rows_loaded_{1 - j}"], rows_loads(i + j))
                                for x in plan[j][k]:
                                    maxima(i, j, first_chunk(j) + x, 1 - j, *todo[x])
                            if k == NT - 1 and ahead:
                                turn_maxima(i, j, first_chunk(j) + CH, n + 1)
                            if k >= 1:
                                apply(i, j, k - 1)
                            elif j == 1:
                                apply(i, 0, NT - 1)
                            elif not first:
                                apply(i - 1, 1, NT - 1)

                def epilogue():
                    apply(PAIRS - 1, 1, NT - 1)
                    pe.wait_ge(sg["a_read"], use_of(PAIRS - 1, 1, 2))
                    pe.sem_inc(sg["a_full"], CH + 1)
                    pe.sem_inc(sg["a_read"], CH + 1)
                    total(PAIRS, 0, B)
                    project(PAIRS)

                emit(pe, prologue, pair, epilogue)

            @block.scalar
            def _(act):
                def split_high(n, j):
                    act.wait_ge(sg["t_loaded"], n * (T_LOADS * DMA) + T_LOADS * DMA)
                    act.activation(ct_hi[j][:, 0:NK], ct[:], ACT.Copy)
                    act.activation(q_hi[j][:], qf[:], ACT.Copy).then_inc(sg["high_made"], 1)

                def copy_u(i, j, n):
                    act.wait_ge(sg["p_applied"], n * NT + P_BUFS)
                    if j == 1:
                        act.wait_ge(sg["a_full"], use_of(i, 0, 4))
                    act.activation(
                        u_norm[:, :, (1 - j) * S:(2 - j) * S].rearrange("p (a h) q -> p a h q", a=2),
                        halves(ps[:, U_BANK:U_BANK + 2, :]).rearrange("p a (h q) -> p a h q", q=S),
                        ACT.Copy).then_inc(sg["u_read"], 1)

                def copy_sum(i, j, n):
                    if not (isinstance(n, int) and n == 1):
                        act.wait_ge(sg["u_made"], n)
                    for a in range(2):
                        act.wait_ge(sg["a_full"], use_of(i, j, a + 1))
                        act.activation(recip[:, a * HALF:(a + 1) * HALF], ps[:, bank_of(j, a), 0:HALF],
                                       ACT.Copy).then_inc(sg["a_read"], 1)

                def pair(i, first, final):
                    for j in range(2):
                        n = batch(i, j)
                        start, ahead = first and j == 0, not (final and j == 1)
                        for k in range(NT):
                            kn = widths[k]
                            p = p_buf[buf_of(j, k)][0:kn, :]
                            if side:
                                if k == 0:
                                    act.wait_ge(sg[f"rows_loaded_{j}"], rows_loads(i))
                                act.wait_ge(sg["side_added"], n * NT + (k + 2))
                                act.activation(p, p, ACT.Exp, bias=mask_col[j][:, k:k + 1]).then_inc(sg["p_ready"], 1)
                            else:
                                act.wait_ge(sg["scores_full"], n * NT + (k + 1))
                                act.wait_ge(sg["p_applied"], p_free(n, j, k))
                                act.wait_ge(sg["p_summed"], p_free(n, j, k))
                                src = ps[0:kn, slot_of(j, k):slot_of(j, k) + 2, :]
                                act.activation(two(p), halves(src), ACT.Exp, scale=scale).then_inc(sg["p_ready"], 1)
                            if k == 0 and not start:
                                copy_u(i, j, n)
                            if k == 1 and not start:
                                copy_sum(i, j, n)
                            if k == 2 and ahead:
                                split_high(n + 1, 1 - j)

                def epilogue():
                    copy_u(PAIRS, 0, B)
                    copy_sum(PAIRS, 0, B)

                emit(act, lambda: split_high(0, 0), pair, epilogue)

            @block.gpsimd
            def _(pool):
                pool.sem_inc(sg["p_summed"], P_BUFS)

                def pair(i, first, final):
                    for j in range(2):
                        n = batch(i, j)
                        for k in range(1, NT):
                            kn = widths[k]
                            p = p_buf[buf_of(j, k)]
                            pool.wait_ge(sg["p_ready"], n * NT + (k + 2))
                            if k == 1:
                                if not (first and j == 0):
                                    pool.wait_ge(sg["a_full"], use_of(i, j, 2))
                                pool.tensor_tensor(p_sum[:], p_buf[buf_of(j, 0)][:], p[:], ALU.add).then_inc(
                                    sg["p_summed"], 2)
                            else:
                                pool.wait_ge(sg["p_summed"], n * NT + (k + P_BUFS))
                                pool.tensor_tensor(p_sum[0:kn, :], p_sum[0:kn, :], p[0:kn, :], ALU.add).then_inc(
                                    sg["p_summed"], 1)

                emit(pool, lambda: None, pair, lambda: None)

            @block.vector
            def _(dve):
                def split_low(n, j):
                    dve.wait_ge(sg["high_made"], n + 1)
                    dve.tensor_tensor(ct_lo[j][:, 0:NK], ct[:], ct_hi[j][:, 0:NK].bitcast(F32), ALU.subtract)
                    dve.tensor_tensor(q_lo[j][:], qf[:], q_hi[j][:].bitcast(F32), ALU.subtract).then_inc(
                        sg["parts_made"], 1)

                def read_maxima(i, j, u, hp, m):
                    k0, kn = chunks[m]
                    bank = bank_of(j, u)
                    dve.wait_ge(sg["a_full"], use_of(i, j, u + 1))
                    if side:
                        dve.wait_ge(sg["a_read"], use_of(i, j, u))
                        dve.sem_inc(sg["chunk_seen"], 1)
                        dve.tensor_tensor_reduce(scratch[:, 0:kn], ps[0:TP, bank, 0:kn], side_rows[:, hp, k0:k0 + kn],
                                                 1.0, -3.0e38, ALU.add, ALU.max,
                                                 part_max[:, hp, m:m + 1]).then_inc(sg["a_read"], 1)
                    else:
                        dve.tensor_reduce(part_max[:, hp, m:m + 1], ps[0:TP, bank, 0:kn], X, ALU.max).then_inc(
                            sg["a_read"], 1)

                def finish_maxima(i, j, u, n, nj):
                    dve.wait_ge(sg["a_read"], use_of(i, j, u))
                    dve.tensor_reduce(row_max[:], part_max[:], X, ALU.max).then_inc(sg["row_max"], 1)
                    dve.wait_ge(sg["row_max"], n + 1)
                    dve.tensor_copy(max_hi[:], row_max[:]).then_inc(sg["max_hi"], 1)
                    dve.wait_ge(sg["max_hi"], n + 1)
                    dve.tensor_copy(max_parts[:, 0:H // 2], max_hi[:].bitcast(F32))
                    dve.tensor_tensor(max_parts[:, H // 2:H], row_max[:], max_hi[:].bitcast(F32),
                                      ALU.subtract).then_inc(sg["max_parts_ready"], 1)
                    bank = bank_of(j, u)
                    dve.wait_ge(sg["a_full"], use_of(i, j, u + 1))
                    dve.tensor_tensor(neg_max[nj][:].rearrange("p (a c) -> p a c", a=H // 2),
                                      ps[0:16, bank:bank + 1, 0:TP].to_broadcast([16, H // 2, TP]), negsel[:],
                                      ALU.mult).then_inc(sg["a_read"], 1)

                def invert(i, j, n, quarter):
                    if quarter == 0:
                        dve.wait_ge(sg["a_read"], use_of(i, j, 2))
                    cols = slice(quarter * HQ // 4, (quarter + 1) * HQ // 4)
                    dve.reciprocal(recip[:, cols], recip[:, cols]).then_inc(sg["inverted"], 1)

                def normalise(j, n):
                    dve.wait_ge(sg["inverted"], n * 4)
                    dve.wait_ge(sg["u_read"], n + 1)
                    u = u_norm[:, :, (1 - j) * S:(2 - j) * S]
                    dve.tensor_tensor(u, u, recip[:].rearrange("p (h q) -> p h q", q=S), ALU.mult).then_inc(
                        sg["u_made"], 1)

                def read_y(i):
                    dve.wait_ge(sg["y_sb_free"], i)
                    for a in range(2):
                        dve.wait_ge(sg["a_full"], use_of(i, 0, 3 + a))
                        dve.tensor_copy(y_sb[:, a * 64:(a + 1) * 64], ps[0:TP, bank_of(0, 2 + a), 0:64]).then_inc(
                            sg["a_read"], 1)

                def prologue():
                    for j in range(2):
                        if NKP > NK:
                            dve.memset(ct_hi[j][:, NK:NKP].bitcast(F32), 0.0)
                            dve.memset(ct_lo[j][:, NK:NKP].bitcast(F32), 0.0)
                    dve.memset(ones_r[:].bitcast(F32), 1.0).then_inc(sg["ones_made"], 1)
                    dve.wait_ge(sg["ones_made"], 1)
                    split_low(0, 0)
                    dve.wait_ge(sg["constants"], (2 if side else 1) * DMA)
                    for u, (hp, m) in enumerate(todo):
                        read_maxima(0, 0, u + GRANTED - (CH + 1), hp, m)
                    finish_maxima(0, 0, CH + GRANTED - (CH + 1), 0, 0)
                    if side:
                        dve.wait_ge(sg["side_cols_loaded"], DMA)

                def pair(i, first, final):
                    for j in range(2):
                        n = batch(i, j)
                        start, ahead = first and j == 0, not (final and j == 1)
                        for k in range(NT):
                            if side:
                                dve.wait_ge(sg["scores_full"], n * NT + (k + 1))
                                dve.wait_ge(sg["p_applied"], p_free(n, j, k))
                                dve.wait_ge(sg["p_summed"], p_free(n, j, k))
                                src = ps[0:KT, slot_of(j, k):slot_of(j, k) + 2, :]
                                dve.tensor_tensor(two(p_buf[buf_of(j, k)][:]), halves(src), two(side_cols[:, k, :]),
                                                  ALU.add).then_inc(sg["side_added"], 1)
                            if k in (1, 2) and not start:
                                invert(i, j, n, 2 * k - 2)
                                invert(i, j, n, 2 * k - 1)
                            if k == NORM_AT:
                                if not start:
                                    normalise(j, n)
                                if ahead:
                                    split_low(n + 1, 1 - j)
                            if k == Y_AT and j == 0 and not first:
                                read_y(i)
                            if ahead:
                                for x in plan[j].get(k, ()):
                                    read_maxima(i, j, first_chunk(j) + x, *todo[x])
                                if k == NT - 1:
                                    finish_maxima(i, j, first_chunk(j) + CH, n + 1, 1 - j)

                def epilogue():
                    for quarter in range(4):
                        invert(PAIRS, 0, B, quarter)
                    normalise(0, B)
                    read_y(PAIRS)

                emit(dve, prologue, pair, epilogue)


def stage_add_y(c, biased):
    nc, d, sg = c.nc, c.dram, c.stage("addy")
    with nc.sbuf_tensor(f"y_all{c.count}", [TP, PAIRS, D], F32) as y, nc.Block() as block:
        @block.sync
        def _(sp):
            c.clear_old(sp)
            sp.dma_start(y[:], d["y"].rearrange("t p d -> p t d")).then_inc(sg["y_loaded"], DMA)
            sp.wait_ge(sg["y_loaded"], DMA)

        @block.vector
        def _(dve):
            dve.wait_ge(sg["y_loaded"], DMA)
            dve.tensor_tensor(c.x[:], c.x[:], y[:], ALU.add).then_inc(sg["x_added"], 1)
            if biased:
                dve.wait_ge(sg["x_added"], 1)
                dve.tensor_tensor(c.x[:], c.x[:], c.ybias[:].unsqueeze(1).to_broadcast([TP, PAIRS, D]),
                                  ALU.add).then_inc(sg["x_added"], 1)


def stage_store(c):
    nc, d, sg = c.nc, c.dram, c.stage("store")
    with nc.Block() as block:
        @block.sync
        def _(sp):
            c.clear_old(sp)
            sp.dma_start(d["out"].rearrange("(t p) d -> p t d", p=TP), c.x[:]).then_inc(sg["stored"], DMA)
            sp.wait_ge(sg["stored"], DMA)


def stage_own_keys(c, z, zt):
    nc, d, sg = c.nc, c.dram, c.stage("own")
    with nc.Block() as block:
        @block.sync
        def _(sp):
            c.clear_old(sp)
            for j in range(2):
                rows = d["ctx1"][:, SK:SK + S, :].rearrange("(t j) q d -> j q t d", j=2)
                sp.dma_start(rows[j], z[j * S:(j + 1) * S, :, :]).then_inc(sg["stored"], DMA)
            sp.dma_start(d["ctx1T"][:, :, SK:SK + S].rearrange("b p q -> p b q"),
                         zt[:].rearrange("p (b q) -> p b q", q=S)).then_inc(sg["stored"], DMA)
            sp.wait_ge(sg["stored"], 3 * DMA)


def stage_qkv(c, layer, zt, q_t, k_t, v_ext, wo, wo_bias):
    nc, d, sg = c.nc, c.dram, c.stage("qkv")
    ps = c.ps
    with ExitStack() as st:
        sb = alloc(c, st)
        w = {k: sb(k, [D, D]) for k in ("wq", "wk", "wv")}
        bqk = sb("bqk", [D, 2])
        bvo = sb("bvo", [1, 2, D])
        with nc.Block() as block:
            @block.sync
            def _(sp):
                c.clear_old(sp)
                for k in ("wq", "wk", "wv"):
                    sp.dma_start(w[k][:], d[f"f0_{k}"][layer]).then_inc(sg["weights"], DMA)
                sp.dma_start(wo[:], d["f0_wo"][layer]).then_inc(sg["weights"], DMA)
                sp.dma_start(bqk[:], d["f0_bqk"][layer]).then_inc(sg["weights"], DMA)
                sp.dma_start(bvo[:], d["f0_bvo"][layer:layer + 1]).then_inc(sg["weights"], DMA)

            @block.tensor
            def _(pe):
                pe.wait_ge(sg["weights"], 6 * DMA)
                for n, k in enumerate(("wq", "wk")):
                    for a in range(2):
                        last = pe.matmul(ps[:, 2 * n + a, 0:HALF], w[k][:], zt[:, a * HALF:(a + 1) * HALF],
                                         start=True, stop=True)
                    last.then_inc(sg["qk_product"], 1)
                for t in range(PAIRS):
                    out = ps[0:TP, 4 + t // 4, (t % 4) * D:(t % 4 + 1) * D]
                    pe.matmul(out, zt[:, t * TP:(t + 1) * TP], w["wv"][:], start=True, stop=False)
                    last = pe.matmul(out, c.ones[0:1, 0:TP], bvo[:, 0, :], start=False, stop=True)
                last.then_inc(sg["v_product"], 1)
                last = pe.matmul(ps[0:TP, 6, 0:D], c.ones[0:1, 0:TP], bvo[:, 1, :], start=True, stop=True)
                last.then_inc(sg["bo_product"], 1)

            @block.scalar
            def _(act):
                act.wait_ge(sg["weights"], 6 * DMA)
                act.wait_ge(sg["qk_product"], 1)
                act.activation(two(q_t[:]), halves(ps[:, 0:2, :]), ACT.Identity, bias=bqk[:, 0:1]).then_inc(sg["q_ready"], 1)
                act.wait_ge(sg["qk_product"], 2)
                act.activation(two(k_t[:]), halves(ps[:, 2:4, :]), ACT.Identity, bias=bqk[:, 1:2]).then_inc(sg["k_ready"], 1)

            @block.vector
            def _(dve):
                dve.memset(v_ext[:, :, :, 8:9], 1.0)
                dve.wait_ge(sg["v_product"], 1)
                for a in range(2):
                    dve.tensor_copy(v_ext[:, 4 * a:4 * a + 4, :, 0:8],
                                    ps[0:TP, 4 + a, :].rearrange("p (t h e) -> p t h e", t=4, h=H)).then_inc(sg["v_ready"], 1)
                dve.wait_ge(sg["bo_product"], 1)
                dve.tensor_copy(wo_bias[:], ps[0:TP, 6, 0:D]).then_inc(sg["bo_ready"], 1)


def stage_self_attention(c, r, q_t, k_t, v_ext, wo, wo_bias):
    nc, d, sg = c.nc, c.dram, c.stage("self")
    ps = c.ps
    with ExitStack() as st:
        sb = alloc(c, st)
        head_of = sb("head_of", [D, H])
        causal = sb("causal", [TP, TP])
        k_wide = sb("k_wide", [D, H, TP])
        q_now = sb("q_now", [D, TP])
        sc = sb("sc", [TP, H, TP])
        mx = sb("mx", [TP, H])
        p_t = sb("p_t", [TP, H, TP])
        rs = sb("rs", [TP, H])
        o = sb("o", [TP, H, 8])
        o_t = sb("o_t", [D, TP])
        with nc.Block() as block:
            @block.sync
            def _(sp):
                c.clear_old(sp)
                sp.dma_start(head_of[:], d["head_of"]).then_inc(sg["masks"], DMA)
                sp.dma_start(causal[:], d["causal"]).then_inc(sg["masks"], DMA)

            @block.gpsimd
            def _(pool):
                pool.wait_ge(sg["masks"], 2 * DMA)
                pool.sem_inc(sg["k_wide_free"], 1)
                with pool.Fori(0, PAIRS) as i:
                    pool.wait_ge(sg["k_wide_free"], i + 1)
                    pool.tensor_tensor(k_wide[:], k_t[:, bass.ts(i, TP)].unsqueeze(1).to_broadcast([D, H, TP]),
                                       head_of[:].unsqueeze(2).to_broadcast([D, H, TP]), ALU.mult).then_inc(
                        sg["k_wide_made"], 1)

            @block.tensor
            def _(pe):
                with pe.Fori(0, PAIRS) as i:
                    pe.wait_ge(sg["k_wide_made"], i + 1)
                    pe.wait_ge(sg["q_now"], i + 1)
                    for a in range(4):
                        last = pe.matmul(ps[0:TP, a, 0:HALF], q_now[:], k_wide[:, 4 * a:4 * a + 4, :], start=True, stop=True)
                    last.then_inc(sg["k_wide_free"], 1)
                    pe.wait_ge(sg["exp_done"], i + 1)
                    for h in range(H):
                        last = pe.transpose(ps[0:TP, 4 + h // 4, (h % 4) * TP:(h % 4 + 1) * TP], sc[:, h, :],
                                            c.ident[0:TP, 0:TP])
                    last.then_inc(sg["p_turned"], 1)
                    pe.wait_ge(sg["p_t_ready"], i + 1)
                    for h in range(H):
                        last = pe.matmul(ps[0:TP, 0, h * 16:h * 16 + 9], p_t[:, h, :],
                                         v_ext[:, bass.ts(i, 1), h, :], start=True, stop=True)
                    last.then_inc(sg["o_product"], 1)
                    pe.wait_ge(sg["o_ready"], i + 1)
                    pe.transpose(ps[:, 1, 0:TP], o[:].rearrange("p h e -> p (h e)"), c.ident[0:TP, 0:TP]).then_inc(
                        sg["o_turned"], 1)
                    pe.wait_ge(sg["o_t_ready"], i + 1)
                    pe.matmul(ps[0:TP, 2, 0:D], o_t[:], wo[:], start=True, stop=True).then_inc(sg["y_product"], 1)

            @block.scalar
            def _(act):
                with act.Fori(0, PAIRS) as i:
                    act.wait_ge(sg["y_added_or_start"], i + 1)
                    act.activation(q_now[:], q_t[:, bass.ts(i, TP)], ACT.Copy).then_inc(sg["q_now"], 1)
                    act.wait_ge(sg["less_max"], i + 1)
                    act.activation(sc[:], sc[:], ACT.Exp).then_inc(sg["exp_done"], 1)
                    act.wait_ge(sg["p_turned"], i + 1)
                    act.activation(p_t[:].rearrange("p (a h) q -> p a (h q)", a=4), ps[0:TP, 4:8, 0:HALF], ACT.Copy).then_inc(
                        sg["p_t_ready"], 1)
                    act.wait_ge(sg["o_turned"], i + 1)
                    act.activation(o_t[:], ps[:, 1, 0:TP], ACT.Copy).then_inc(sg["o_t_ready"], 1)

            @block.vector
            def _(dve):
                dve.wait_ge(sg["masks"], 2 * DMA)
                dve.tensor_tensor(r[:], r[:], wo_bias[:].unsqueeze(1).to_broadcast([TP, PAIRS, D]), ALU.add).then_inc(
                    sg["y_added_or_start"], 1)
                with dve.Fori(0, PAIRS) as i:
                    dve.wait_ge(sg["k_wide_free"], i + 2)
                    for a in range(4):
                        last = dve.scalar_tensor_tensor(
                            sc[:, 4 * a:4 * a + 4, :], ps[0:TP, a, 0:HALF].rearrange("p (h q) -> p h q", q=TP), 8 ** -0.5,
                            causal[:].unsqueeze(1).to_broadcast([TP, 4, TP]), ALU.mult, ALU.add)
                    last.then_inc(sg["masked"], 1)
                    dve.wait_ge(sg["masked"], i + 1)
                    dve.tensor_reduce(mx[:], sc[:], X, ALU.max).then_inc(sg["mx"], 1)
                    dve.wait_ge(sg["mx"], i + 1)
                    dve.tensor_tensor(sc[:], sc[:], mx[:].unsqueeze(2).to_broadcast([TP, H, TP]), ALU.subtract).then_inc(
                        sg["less_max"], 1)
                    dve.wait_ge(sg["o_product"], i + 1)
                    o_ps = ps[0:TP, 0, 0:256].rearrange("p (h e) -> p h e", h=H)
                    dve.reciprocal(rs[:].unsqueeze(2), o_ps[:, :, 8:9]).then_inc(sg["rs"], 1)
                    dve.wait_ge(sg["rs"], i + 1)
                    dve.tensor_tensor(o[:], o_ps[:, :, 0:8], rs[:].unsqueeze(2).to_broadcast([TP, H, 8]), ALU.mult).then_inc(
                        sg["o_ready"], 1)
                    dve.wait_ge(sg["y_product"], i + 1)
                    rt = r[:, bass.ts(i, 1), :]
                    dve.tensor_tensor(rt, rt, ps[0:TP, 2:3, 0:D], ALU.add).then_inc(sg["y_added_or_start"], 1)


def stage_top2(c, ht, gate_w, gate_b, cw, of_batch_mean):
    nc, d, sg = c.nc, c.dram, c.stage("top2")
    ps = c.ps
    with ExitStack() as st:
        sb = alloc(c, st)
        gw = sb("gw", [D, E])
        gb = sb("gb", [1, E])
        earlier = sb("earlier", [TP, E, E])
        sums = sb("sums", [D, B])
        mean = sb("mean", [D, TOK])
        lg = sb("lg", [TP, PAIRS, E])
        gt = sb("gt", [TP, PAIRS, E, E])
        eq = sb("eq", [TP, PAIRS, E, E])
        rank = sb("rank", [TP, PAIRS, E])
        mx = sb("mx", [TP, PAIRS])
        ex = sb("ex", [TP, PAIRS, E])
        tot = sb("tot", [TP, PAIRS])
        src = mean if of_batch_mean else ht
        with nc.Block() as block:
            @block.sync
            def _(sp):
                c.clear_old(sp)
                sp.dma_start(gw[:], gate_w).then_inc(sg["weights"], DMA)
                sp.dma_start(gb[:], gate_b).then_inc(sg["weights"], DMA)
                sp.dma_start(earlier[:], d["earlier"]).then_inc(sg["weights"], DMA)

            @block.tensor
            def _(pe):
                pe.wait_ge(sg["weights"], 3 * DMA)
                if of_batch_mean:
                    pe.wait_ge(sg["mean_ready"], 1)
                for t in range(PAIRS):
                    out = ps[0:TP, 0, t * E:(t + 1) * E]
                    pe.matmul(out, src[:, t * TP:(t + 1) * TP], gw[:], start=True, stop=False)
                    last = pe.matmul(out, c.ones[0:1, 0:TP], gb[:], start=False, stop=True)
                last.then_inc(sg["logits"], 1)

            @block.scalar
            def _(act):
                act.wait_ge(sg["less_max"], 1)
                act.activation(ex[:], ex[:], ACT.Exp).then_inc(sg["exp_done"], 1)

            @block.vector
            def _(dve):
                link = Link(dve, sg["dve_chain"])
                if of_batch_mean:
                    link(dve.tensor_reduce(sums[:], ht[:].rearrange("p (b q) -> p b q", q=S), X, ALU.add))
                    dve.tensor_scalar(mean[:].rearrange("p (b q) -> p b q", q=S),
                                      sums[:].unsqueeze(2).to_broadcast([D, B, S]), 1.0 / S, None,
                                      ALU.mult).then_inc(sg["mean_ready"], 1)
                dve.wait_ge(sg["weights"], 3 * DMA)
                dve.wait_ge(sg["logits"], 1)
                link(dve.tensor_copy(lg[:], ps[0:TP, 0, 0:PAIRS * E].rearrange("p (t e) -> p t e", e=E)))
                other = lg[:].unsqueeze(2).to_broadcast([TP, PAIRS, E, E])
                mine = lg[:].unsqueeze(3).to_broadcast([TP, PAIRS, E, E])
                link(dve.tensor_reduce(mx[:], lg[:], X, ALU.max))
                dve.tensor_tensor(ex[:], lg[:], mx[:].unsqueeze(2).to_broadcast([TP, PAIRS, E]), ALU.subtract).then_inc(
                    sg["less_max"], 1)
                link(dve.tensor_tensor(gt[:], other, mine, ALU.is_gt))
                link(dve.tensor_tensor(eq[:], other, mine, ALU.is_equal))
                link(dve.tensor_tensor(eq[:], eq[:], earlier[:].unsqueeze(1).to_broadcast([TP, PAIRS, E, E]), ALU.mult))
                link(dve.tensor_tensor(gt[:], gt[:], eq[:], ALU.add))
                link(dve.tensor_reduce(rank[:], gt[:], X, ALU.add))
                dve.wait_ge(sg["exp_done"], 1)
                link(dve.scalar_tensor_tensor(ex[:], rank[:], 2.0, ex[:], ALU.is_lt, ALU.mult))
                link(dve.tensor_reduce(tot[:], ex[:], X, ALU.add))
                link(dve.reciprocal(tot[:], tot[:]))
                dve.tensor_tensor(cw[:].rearrange("p e t -> p t e"), ex[:],
                                  tot[:].unsqueeze(2).to_broadcast([TP, PAIRS, E]), ALU.mult).then_inc(sg["cw_ready"], 1)


def stage_capacity(c, zt, cw):
    nc, d, sg = c.nc, c.dram, c.stage("cap")
    ps = c.ps
    with ExitStack() as st:
        sb = alloc(c, st)
        gw = sb("gw", [D, E])
        same = sb("same", [TP, TP])
        before = sb("before", [TP, TP])
        pr = sb("pr", [TP, PAIRS, E])
        mx = sb("mx", [TP, PAIRS])
        tot = sb("tot", [TP, PAIRS])
        diag = sb("diag", [TP, 2, E, TP])
        gt = sb("gt", [TP, E, TP])
        eq = sb("eq", [TP, E, TP])
        rank = sb("rank", [TP, PAIRS, E])

        def over_t(ap):
            return ap.unsqueeze(1).to_broadcast([TP, E, TP])

        with nc.Block() as block:
            @block.sync
            def _(sp):
                c.clear_old(sp)
                sp.dma_start(gw[:], d["f2_gate_w"]).then_inc(sg["weights"], DMA)
                sp.dma_start(same[:], d["same"]).then_inc(sg["weights"], DMA)
                sp.dma_start(before[:], d["before"]).then_inc(sg["weights"], DMA)

            @block.tensor
            def _(pe):
                pe.wait_ge(sg["weights"], 3 * DMA)
                for t in range(PAIRS):
                    last = pe.matmul(ps[0:TP, 0, t * E:(t + 1) * E], zt[:, t * TP:(t + 1) * TP], gw[:],
                                     start=True, stop=True)
                last.then_inc(sg["scores"], 1)
                with pe.Fori(0, PAIRS // 2) as i:
                    for j in range(2):
                        pe.wait_ge(sg["diag_made"], i * 2 + (j + 1))
                        for a in range(2):
                            last = pe.matmul(ps[0:TP, 2 + 2 * j + a, 0:HALF], c.ones[0:TP, 0:TP],
                                             diag[:, j, 4 * a:4 * a + 4, :], start=True, stop=True)
                        last.then_inc(sg["spread"], 1)

            @block.scalar
            def _(act):
                act.wait_ge(sg["less_max"], 1)
                act.activation(pr[:], pr[:], ACT.Exp).then_inc(sg["exp_done"], 1)

            @block.vector
            def _(dve):
                link = Link(dve, sg["dve_chain"])
                dve.wait_ge(sg["weights"], 3 * DMA)
                dve.wait_ge(sg["scores"], 1)
                scores = ps[0:TP, 0, 0:PAIRS * E].rearrange("p (t e) -> p t e", e=E)
                link(dve.tensor_reduce(mx[:], scores, X, ALU.max))
                dve.tensor_tensor(pr[:], scores, mx[:].unsqueeze(2).to_broadcast([TP, PAIRS, E]), ALU.subtract).then_inc(
                    sg["less_max"], 1)
                dve.wait_ge(sg["exp_done"], 1)
                link(dve.tensor_reduce(tot[:], pr[:], X, ALU.add))
                link(dve.reciprocal(tot[:], tot[:]))
                link(dve.tensor_tensor(pr[:], pr[:], tot[:].unsqueeze(2).to_broadcast([TP, PAIRS, E]), ALU.mult))
                with dve.Fori(0, PAIRS // 2) as i:
                    for j in range(2):
                        mine = pr[:, i * 2 + j, :].unsqueeze(2).to_broadcast([TP, E, TP])
                        dve.tensor_tensor(diag[:, j, :, :], over_t(c.ident[0:TP, 0:TP]), mine, ALU.mult).then_inc(
                            sg["diag_made"], 1)
                        dve.wait_ge(sg["spread"], i * 2 + (j + 1))
                        theirs = ps[0:TP, 2 + 2 * j:4 + 2 * j, 0:HALF].rearrange("p a (e t) -> p a e t", t=TP)
                        mine4 = pr[:, i * 2 + j, :].rearrange("p (a e) -> p a e", a=2).unsqueeze(3).to_broadcast([TP, 2, E // 2, TP])
                        gt4 = gt[:].rearrange("p (a e) t -> p a e t", a=2)
                        eq4 = eq[:].rearrange("p (a e) t -> p a e t", a=2)
                        dve.tensor_tensor(gt4, theirs, mine4, ALU.is_gt)
                        dve.tensor_tensor(eq4, theirs, mine4, ALU.is_equal).then_inc(sg["compared"], 1)
                        dve.wait_ge(sg["compared"], i * 2 + (j + 1))
                        dve.tensor_tensor(gt[:], gt[:], over_t(same[:]), ALU.mult)
                        dve.tensor_tensor(eq[:], eq[:], over_t(before[:]), ALU.mult).then_inc(sg["kept"], 1)
                        dve.wait_ge(sg["kept"], i * 2 + (j + 1))
                        dve.tensor_tensor(gt[:], gt[:], eq[:], ALU.add).then_inc(sg["before_me"], 1)
                        dve.wait_ge(sg["before_me"], i * 2 + (j + 1))
                        dve.tensor_reduce(rank[:, i * 2 + j, :], gt[:], X, ALU.add).then_inc(sg["rank"], 1)
                dve.wait_ge(sg["rank"], PAIRS)
                dve.scalar_tensor_tensor(cw[:].rearrange("p e t -> p t e"), rank[:], float(CAP), pr[:], ALU.is_lt,
                                         ALU.mult).then_inc(sg["cw_ready"], 1)


def stage_experts(c, ht, acc, cw, w1, w2, b1=None, b2=None):
    nc, d, sg = c.nc, c.dram, c.stage("experts")
    ps = c.ps
    F = DFF // 128
    with ExitStack() as st:
        sb = alloc(c, st)
        w1s = [sb(f"w1_{j}", [D, DFF]) for j in range(2)]
        w2s = [sb(f"w2_{j}", [128, F, D]) for j in range(2)]
        g = sb("g", [128, 2, F, TOK])
        if b1 is not None:
            b1s = sb("b1", [128, E, F])
            b2s = sb("b2", [E, D])
            cw_t = sb("cw_t", [E, PAIRS, TP])
        UP, DOWN = 0, 4

        def emit(run, before, step):
            before()
            with run.Fori(0, E // 2 - 1) as i:
                for j in range(2):
                    step(i, j, True, True)
            for j in range(2):
                step(E // 2 - 1, j, False, j == 0)

        with nc.Block() as block:
            @block.sync
            def _(sp):
                c.clear_old(sp)

                def before():
                    if b1 is not None:
                        sp.dma_start(b1s[:], b1).then_inc(sg["biases"], DMA)
                        sp.dma_start(b2s[:], b2).then_inc(sg["biases"], DMA)
                    for j in range(2):
                        sp.dma_start(w1s[j][:], w1[:, j, :]).then_inc(sg[f"w1_{j}"], DMA)
                        sp.dma_start(w2s[j][:], w2[:, j, :, :]).then_inc(sg[f"w2_{j}"], DMA)

                def step(i, j, two_more, one_more):
                    if two_more:
                        sp.wait_ge(sg["up_full"], i * 8 + 4 * (j + 1))
                        sp.dma_start(w1s[j][:], w1[:, i * 2 + (j + 2), :]).then_inc(sg[f"w1_{j}"], DMA)
                        sp.wait_ge(sg["down_full"], i * 2 + (j + 3))
                        sp.dma_start(w2s[j][:], w2[:, i * 2 + (j + 2), :, :]).then_inc(sg[f"w2_{j}"], DMA)

                emit(sp, before, step)

            @block.tensor
            def _(pe):
                def up(i, j):
                    pe.wait_ge(sg[f"w1_{j}"], i * DMA + DMA)
                    for f in range(F):
                        bank = UP + 2 * (f % 2)
                        pe.wait_ge(sg["gelu_done"], i * 8 + (4 * j + f + 1))
                        for a in range(2):
                            last = pe.matmul(ps[:, bank + a, 0:HALF], w1s[j][:, f * 128:(f + 1) * 128],
                                             ht[:, a * HALF:(a + 1) * HALF], start=True, stop=True)
                        last.then_inc(sg["up_full"], 1)

                def down(i, j):
                    pe.wait_ge(sg[f"w2_{j}"], i * DMA + DMA)
                    pe.wait_ge(sg["combined"], i * 2 + (j + 1))
                    pe.wait_ge(sg["gelu_done"], i * 8 + (4 * (j + 1) + 2))
                    for t in range(PAIRS):
                        for f in range(F):
                            last = pe.matmul(ps[0:TP, DOWN + 2 * j + t // 4, (t % 4) * D:(t % 4 + 1) * D],
                                             g[:, j, f, t * TP:(t + 1) * TP], w2s[j][:, f, :],
                                             start=(f == 0), stop=(f == F - 1))
                    last.then_inc(sg["down_full"], 1)

                def before():
                    pe.sem_inc(sg["gelu_done"], 2)
                    pe.sem_inc(sg["combined"], 2)
                    pe.sem_inc(sg["down_full"], 2)
                    if b1 is not None:
                        for t in range(PAIRS):
                            last = pe.transpose(ps[0:E, t // 4, (t % 4) * TP:(t % 4 + 1) * TP], cw[:, :, t],
                                                c.ident[0:TP, 0:TP])
                        last.then_inc(sg["cw_turned"], 1)
                        pe.wait_ge(sg["cw_t_ready"], 1)
                        pe.wait_ge(sg["biases"], 2 * DMA)
                        for t in range(PAIRS):
                            last = pe.matmul(ps[0:TP, 2 + t // 4, (t % 4) * D:(t % 4 + 1) * D], cw_t[:, t, :], b2s[:],
                                             start=True, stop=True)
                        last.then_inc(sg["b2_product"], 1)
                        pe.wait_ge(sg["b2_added"], 1)
                    up(0, 0)

                def step(i, j, two_more, one_more):
                    if one_more:
                        up(i + j, 1 - j)
                    down(i, j)

                emit(pe, before, step)

            @block.scalar
            def _(act):
                def before():
                    if b1 is not None:
                        act.wait_ge(sg["biases"], 2 * DMA)

                def step(i, j, two_more, one_more):
                    act.wait_ge(sg["down_full"], i * 2 + (j + 1))
                    for f in range(F):
                        act.wait_ge(sg["up_full"], i * 8 + (4 * j + f + 1))
                        src = halves(ps[:, UP + 2 * (f % 2):UP + 2 * (f % 2) + 2, :])
                        bias = b1s[:, i * 2 + j, f:f + 1] if b1 is not None else 0.0
                        act.activation(two(g[:, j, f, :]), src, ACT.Gelu, bias=bias).then_inc(sg["gelu_done"], 1)

                emit(act, before, step)

            @block.vector
            def _(dve):
                def before():
                    if b1 is not None:
                        dve.wait_ge(sg["cw_turned"], 1)
                        dve.tensor_copy(cw_t[:].rearrange("e (a t) q -> e a (t q)", a=2), ps[0:E, 0:2, 0:HALF]).then_inc(
                            sg["cw_t_ready"], 1)
                        dve.wait_ge(sg["b2_product"], 1)
                        dve.tensor_tensor(acc[:].rearrange("p (a t) d -> p a (t d)", a=2),
                                          acc[:].rearrange("p (a t) d -> p a (t d)", a=2), ps[0:TP, 2:4, :],
                                          ALU.add).then_inc(sg["b2_added"], 1)
                        dve.wait_ge(sg["b2_added"], 1)

                def step(i, j, two_more, one_more):
                    dve.wait_ge(sg["down_full"], i * 2 + (j + 3))
                    dve.wait_ge(sg["combined"], i * 2 + (j + 2))
                    for t in range(PAIRS):
                        last = dve.scalar_tensor_tensor(
                            acc[:, t, :], ps[0:TP, DOWN + 2 * j + t // 4, (t % 4) * D:(t % 4 + 1) * D],
                            cw[:, i * 2 + j, t:t + 1], acc[:, t, :], ALU.mult, ALU.add)
                    last.then_inc(sg["combined"], 1)

                emit(dve, before, step)


def stage_add(c, dst, src):
    nc, sg = c.nc, c.stage("add")
    with nc.Block() as block:
        @block.sync
        def _(sp):
            c.clear_old(sp)

        @block.vector
        def _(dve):
            dve.tensor_tensor(dst[:], dst[:], src[:], ALU.add).then_inc(sg["added"], 1)


def layer0_ffn(c):
    d = c.dram
    with ExitStack() as st:
        sb = alloc(c, st)
        r = sb("r", [TP, PAIRS, D])
        z = sb("z", [TP, PAIRS, D])
        zt = sb("zt", [D, TOK])
        cw = sb("cw", [TP, E, PAIRS])
        stage_norm(c, c.x, r)
        for layer in range(2):
            stage_norm(c, r, z, zt, affine=(d["ln1_w"][layer], d["ln1_b"][layer]))
            with ExitStack() as inner:
                sb = alloc(c, inner)
                q_t, k_t = sb("q_t", [D, TOK]), sb("k_t", [D, TOK])
                v_ext = sb("v_ext", [TP, PAIRS, H, 9])
                wo, wo_bias = sb("wo", [D, D]), sb("wo_bias", [TP, D])
                stage_qkv(c, layer, zt, q_t, k_t, v_ext, wo, wo_bias)
                stage_self_attention(c, r, q_t, k_t, v_ext, wo, wo_bias)
            stage_norm(c, r, z, zt, affine=(d["ln2_w"][layer], d["ln2_b"][layer]))
            stage_top2(c, zt, d["f0_gate_w"][layer], d["f0_gate_b"][layer], cw, of_batch_mean=(layer == 1))
            stage_experts(c, zt, r, cw, d["f0_w1"][layer], d["f0_w2"][layer], d["f0_b1"][layer], d["f0_b2"][layer])
        stage_add(c, c.x, r)


def layer1_ffn(c):
    with ExitStack() as st:
        sb = alloc(c, st)
        z = sb("z", [TP, PAIRS, D])
        zt = sb("zt", [D, TOK])
        stage_norm(c, c.x, z, zt)
        nc, d, sg = c.nc, c.dram, c.stage("ternary")
        ps = c.ps
        F = 4
        w = [sb(f"w{n}", [128, 512]) for n in range(2)]
        t0 = [sb(f"t{n}", [128, 512]) for n in range(2)]
        b1 = sb("b1", [128, F])
        b2 = sb("b2", [1, D])
        mag = sb("mag", [128, 2])
        thr = sb("thr", [128, 2, 2])
        g = sb("g", [128, F, TOK])
        with nc.Block() as block:
            @block.sync
            def _(sp):
                c.clear_old(sp)
                sp.dma_start(w[0][:], d["f1_w1T"]).then_inc(sg["weights"], DMA)
                sp.dma_start(w[1][:], d["f1_w2T"].rearrange("p f d -> p (f d)")).then_inc(sg["weights"], DMA)
                sp.dma_start(b1[:], d["f1_b1"]).then_inc(sg["weights"], DMA)
                sp.dma_start(b2[:], d["f1_b2"]).then_inc(sg["weights"], DMA)

            @block.vector
            def _(dve):
                link = Link(dve, sg["dve_chain"])
                dve.wait_ge(sg["weights"], 4 * DMA)
                for n in range(2):
                    last = dve.tensor_reduce(mag[:, n:n + 1], w[n][:], X, ALU.add, apply_absolute_value=True)
                last.then_inc(sg["magnitudes"], 1)
                dve.wait_ge(sg["magnitudes_summed"], 1)
                link(dve.tensor_scalar(thr[:, 0, :], ps[:, 0, 0:2], 1.0 / (128 * 512), 1e-8, ALU.mult, ALU.max))
                link(dve.tensor_scalar(thr[:, 0, :], thr[:, 0, :], 0.5, None, ALU.mult))
                link(dve.tensor_scalar(thr[:, 1, :], thr[:, 0, :], -1.0, None, ALU.mult))
                for n in range(2):
                    link(dve.tensor_scalar(t0[n][:], w[n][:], thr[:, 1, n:n + 1], None, ALU.is_lt))
                    link(dve.scalar_tensor_tensor(t0[n][:], w[n][:], thr[:, 0, n:n + 1], t0[n][:], ALU.is_gt, ALU.subtract))
                    link(dve.tensor_tensor(t0[n][:], t0[n][:], w[n][:], ALU.subtract))
                    link(dve.tensor_tensor(w[n][:], w[n][:], t0[n][:], ALU.add))
                dve.engine_nop().then_inc(sg["ternary_made"], 1)
                dve.wait_ge(sg["y_product"], 1)
                x2 = c.x[:].rearrange("p (a t) d -> p a (t d)", a=2)
                dve.tensor_tensor(x2, x2, ps[0:TP, 6:8, :], ALU.add).then_inc(sg["x_added"], 1)

            @block.tensor
            def _(pe):
                pe.wait_ge(sg["magnitudes"], 1)
                pe.matmul(ps[:, 0, 0:2], c.ones[:], mag[:], start=True, stop=True).then_inc(sg["magnitudes_summed"], 1)
                pe.wait_ge(sg["ternary_made"], 1)
                for f in range(F):
                    bank = 2 * (f % 3)
                    if f >= 3:
                        pe.wait_ge(sg["gelu_done"], f - 2)
                    for a in range(2):
                        last = pe.matmul(ps[:, bank + a, 0:HALF], w[0][:, f * 128:(f + 1) * 128],
                                         zt[:, a * HALF:(a + 1) * HALF], start=True, stop=True)
                    last.then_inc(sg["up_full"], 1)
                pe.wait_ge(sg["gelu_done"], F)
                for t in range(PAIRS):
                    out = ps[0:TP, 6 + t // 4, (t % 4) * D:(t % 4 + 1) * D]
                    for f in range(F):
                        pe.matmul(out, g[:, f, t * TP:(t + 1) * TP], w[1][:, f * D:(f + 1) * D],
                                  start=(f == 0), stop=False)
                    last = pe.matmul(out, c.ones[0:1, 0:TP], b2[:], start=False, stop=True)
                last.then_inc(sg["y_product"], 1)

            @block.scalar
            def _(act):
                act.wait_ge(sg["weights"], 4 * DMA)
                for f in range(F):
                    act.wait_ge(sg["up_full"], f + 1)
                    bank = 2 * (f % 3)
                    act.activation(two(g[:, f, :]), halves(ps[:, bank:bank + 2, :]), ACT.Gelu,
                                   bias=b1[:, f:f + 1]).then_inc(sg["gelu_done"], 1)


def layer2_attention(c):
    with ExitStack() as st:
        sb = alloc(c, st)
        z = sb("z", [TP, PAIRS, D])
        zt = sb("zt", [D, TOK])
        stage_norm(c, c.x, z, zt)
        nc, d, sg = c.nc, c.dram, c.stage("a2")
        ps = c.ps
        k_rows = sb("k_rows", [TP, PAIRS, D])
        k_cols = sb("k_cols", [D, TOK])
        causal = sb("causal", [TP, TP])
        sc = sb("sc", [TP, PAIRS, TP])
        mx = sb("mx", [TP, PAIRS])
        tot = sb("tot", [TP, PAIRS])
        p_t = sb("p_t", [TP, PAIRS, TP])

        def slot(bank, t, n=TP):
            return ps[0:TP, bank + t // 4, (t % 4) * n:(t % 4 + 1) * n]

        with nc.Block() as block:
            @block.sync
            def _(sp):
                c.clear_old(sp)
                sp.dma_start(k_rows[:], d["own_rows"]).then_inc(sg["loaded"], DMA)
                sp.dma_start(k_cols[:], d["own_cols"]).then_inc(sg["loaded"], DMA)
                sp.dma_start(causal[:], d["causal"]).then_inc(sg["loaded"], DMA)

            @block.tensor
            def _(pe):
                pe.wait_ge(sg["loaded"], 3 * DMA)
                for t in range(PAIRS):
                    last = pe.matmul(slot(0, t), zt[:, t * TP:(t + 1) * TP], k_cols[:, t * TP:(t + 1) * TP],
                                     start=True, stop=True)
                last.then_inc(sg["scores"], 1)
                pe.wait_ge(sg["p_ready"], 1)
                for t in range(PAIRS):
                    last = pe.transpose(slot(2, t), sc[:, t, :], c.ident[0:TP, 0:TP])
                last.then_inc(sg["p_turned"], 1)
                pe.wait_ge(sg["p_t_ready"], 1)
                for t in range(PAIRS):
                    last = pe.matmul(slot(4, t, D), p_t[:, t, :], k_rows[:, t, :], start=True, stop=True)
                last.then_inc(sg["y_product"], 1)

            @block.scalar
            def _(act):
                act.wait_ge(sg["less_max"], 1)
                act.activation(sc[:], sc[:], ACT.Exp).then_inc(sg["exp_done"], 1)
                act.wait_ge(sg["p_turned"], 1)
                act.activation(p_t[:].rearrange("p (a t) k -> p a (t k)", a=2), ps[0:TP, 2:4, 0:HALF], ACT.Copy).then_inc(
                    sg["p_t_ready"], 1)

            @block.vector
            def _(dve):
                link = Link(dve, sg["dve_chain"])
                dve.wait_ge(sg["loaded"], 3 * DMA)
                dve.wait_ge(sg["scores"], 1)
                for a in range(2):
                    last = dve.scalar_tensor_tensor(
                        sc[:, 4 * a:4 * a + 4, :], ps[0:TP, a, 0:HALF].rearrange("p (t k) -> p t k", k=TP), D ** -0.5,
                        causal[:].unsqueeze(1).to_broadcast([TP, 4, TP]), ALU.mult, ALU.add)
                link(last)
                link(dve.tensor_reduce(mx[:], sc[:], X, ALU.max))
                dve.tensor_tensor(sc[:], sc[:], mx[:].unsqueeze(2).to_broadcast([TP, PAIRS, TP]), ALU.subtract).then_inc(
                    sg["less_max"], 1)
                dve.wait_ge(sg["exp_done"], 1)
                link(dve.tensor_reduce(tot[:], sc[:], X, ALU.add))
                link(dve.reciprocal(tot[:], tot[:]))
                dve.tensor_tensor(sc[:], sc[:], tot[:].unsqueeze(2).to_broadcast([TP, PAIRS, TP]), ALU.mult).then_inc(
                    sg["p_ready"], 1)
                dve.wait_ge(sg["y_product"], 1)
                x2 = c.x[:].rearrange("p (a t) d -> p a (t d)", a=2)
                dve.tensor_tensor(x2, x2, ps[0:TP, 4:6, :], ALU.add).then_inc(sg["x_added"], 1)


def layer2_ffn(c):
    d = c.dram
    with ExitStack() as st:
        sb = alloc(c, st)
        z = sb("z", [TP, PAIRS, D])
        zt = sb("zt", [D, TOK])
        cw = sb("cw", [TP, E, PAIRS])
        stage_norm(c, c.x, z, zt)
        stage_capacity(c, zt, cw)
        stage_experts(c, zt, c.x, cw, d["f2_w1"], d["f2_w2"])


def stage_mask(c):
    nc, d, sg = c.nc, c.dram, c.stage("mask")
    with ExitStack() as st:
        sb = alloc(c, st)
        m = sb("m", [B, SK])
        hi = sb("hi", [B, SK], F32R)
        lo = sb("lo", [B, SK], F32R)
        with nc.Block() as block:
            @block.sync
            def _(sp):
                c.clear_old(sp)
                sp.dma_start(m[:], d["mask"]).then_inc(sg["loaded"], DMA)
                sp.wait_ge(sg["low"], 1)
                sp.dma_start(d["mask_parts"][:, 0, :], hi[:].bitcast(F32)).then_inc(sg["stored"], DMA)
                sp.dma_start(d["mask_parts"][:, 1, :], lo[:].bitcast(F32)).then_inc(sg["stored"], DMA)
                sp.wait_ge(sg["stored"], 2 * DMA)

            @block.vector
            def _(dve):
                dve.wait_ge(sg["loaded"], DMA)
                dve.tensor_copy(hi[:], m[:]).then_inc(sg["high"], 1)
                dve.wait_ge(sg["high"], 1)
                dve.tensor_tensor(lo[:], m[:], hi[:].bitcast(F32), ALU.subtract).then_inc(sg["low"], 1)


TINY = 1.17549435e-38
ERFC = [-1.26551223, 1.00002368, 0.37409196, 0.09678418, -0.18628806, 0.27886807, -1.13520398, 1.48851587,
        -0.82215223, 0.17087277]


def layer3_ffn(c):
    with ExitStack() as st:
        sb = alloc(c, st)
        z = sb("z", [TP, PAIRS, D])
        stage_norm(c, c.x, z)
        nc, d, sg = c.nc, c.dram, c.stage("tree")
        W = PAIRS * TREE_P
        RI, RO = 8, 8
        ROW = FAN * D + FAN
        node = sb("node", [TP, PAIRS, TREE_P])
        index = sb("index", [TP, 2, PAIRS, TREE_P], U32)
        platform = sb("platform", [TP, PAIRS, TREE_P])
        fan_less = sb("fan_less", [TP, W, FAN])
        row_in = sb("row_in", [TP, RI, ROW])
        row_out = sb("row_out", [TP, RO, FAN * D])
        prod = sb("prod", [TP, FAN, D])
        logit = sb("logit", [TP, W, FAN])
        gel = sb("gel", [TP, 2, W, FAN])
        mag, frac, poly, half_sq = (sb(k, [TP, W, FAN]) for k in ("mag", "frac", "poly", "half_sq"))
        best = sb("best", [TP, W])
        eq = sb("eq", [TP, W, FAN])
        move = sb("move", [TP, PAIRS, TREE_P])
        levels = range(DEPTH + 1)
        first = [sum(FAN ** k for k in range(n)) for n in levels]
        with nc.Block() as block:
            @block.sync
            def _(sp):
                c.clear_old(sp)
                sp.dma_start(platform[:], d["platform"]).then_inc(sg["constants"], DMA)
                sp.dma_start(fan_less[:], d["fan_less"]).then_inc(sg["constants"], DMA)

            def fetch_out(pool, level, w):
                t, p = w // TREE_P, w % TREE_P
                use = level * W + w
                if use >= RO:
                    pool.wait_ge(sg["row_out_used"], use - RO + 1)
                pool.indirect_dma_start(
                    row_out[:, use % RO, :], None, d["tree_out"],
                    bass.IndirectOffsetOnAxis(ap=index[:, level % 2, t, p:p + 1], axis=0)).then_inc(
                    sg[f"row_out_{use % RO}"], DMA)

            @block.gpsimd
            def _(pool):
                for level in levels:
                    pool.wait_ge(sg["index_ready"], level + 1)
                    for w in range(W):
                        t, p = w // TREE_P, w % TREE_P
                        use = level * W + w
                        if use >= RI:
                            pool.wait_ge(sg["row_in_used"], use - RI + 1)
                        pool.indirect_dma_start(
                            row_in[:, use % RI, :], None, d["tree_in"],
                            bass.IndirectOffsetOnAxis(ap=index[:, level % 2, t, p:p + 1], axis=0)).then_inc(
                            sg[f"row_in_{use % RI}"], DMA)
                        if level >= 1:
                            fetch_out(pool, level - 1, w)
                for w in range(W):
                    fetch_out(pool, DEPTH, w)

            @block.scalar
            def _(act):
                for level in levels:
                    act.wait_ge(sg["exponent"], level + 1)
                    act.activation(poly[:], poly[:], ACT.Exp).then_inc(sg["exp_done"], 1)

            @block.vector
            def _(dve):
                link = Link(dve, sg["dve_chain"])

                def add_out(level, w):
                    t = w // TREE_P
                    use = level * W + w
                    dve.wait_ge(sg[f"row_out_{use % RO}"], DMA * (use // RO + 1))
                    for f in range(FAN):
                        link(dve.scalar_tensor_tensor(c.x[:, t, :], row_out[:, use % RO, f * D:(f + 1) * D],
                                                      gel[:, level % 2, w, f:f + 1], c.x[:, t, :], ALU.mult, ALU.add))
                    dve.engine_nop().then_inc(sg["row_out_used"], 1)

                def gelu(level):
                    link(dve.scalar_tensor_tensor(mag[:], logit[:], -1.0, logit[:], ALU.mult, ALU.max))
                    link(dve.tensor_scalar(frac[:], mag[:], 0.5 * 0.5 ** 0.5, 1.0, ALU.mult, ALU.add))
                    link(dve.reciprocal(frac[:], frac[:]))
                    link(dve.tensor_scalar(poly[:], frac[:], ERFC[-1], None, ALU.mult))
                    for coefficient in reversed(ERFC[1:-1]):
                        link(dve.scalar_tensor_tensor(poly[:], poly[:], coefficient, frac[:], ALU.add, ALU.mult))
                    link(dve.scalar_tensor_tensor(half_sq[:], mag[:], 0.5, mag[:], ALU.mult, ALU.mult))
                    dve.scalar_tensor_tensor(poly[:], poly[:], ERFC[0], half_sq[:], ALU.add, ALU.subtract).then_inc(
                        sg["exponent"], 1)
                    dve.wait_ge(sg["exp_done"], level + 1)
                    link(dve.tensor_tensor(poly[:], poly[:], frac[:], ALU.mult))
                    link(dve.scalar_tensor_tensor(poly[:], poly[:], TINY, poly[:], ALU.is_ge, ALU.mult))
                    link(dve.scalar_tensor_tensor(poly[:], mag[:], 0.5, poly[:], ALU.mult, ALU.mult))
                    link(dve.scalar_tensor_tensor(gel[:, level % 2, :, :], logit[:], 0.0, poly[:], ALU.max, ALU.subtract))

                dve.wait_ge(sg["constants"], 2 * DMA)
                link(dve.memset(node[:], 0.0))
                for level in levels:
                    dve.tensor_tensor(index[:, level % 2, :, :], node[:], platform[:], ALU.add).then_inc(sg["index_ready"], 1)
                    for w in range(W):
                        t = w // TREE_P
                        use = level * W + w
                        dve.wait_ge(sg[f"row_in_{use % RI}"], DMA * (use // RI + 1))
                        row = row_in[:, use % RI, :]
                        link(dve.tensor_tensor(prod[:], row[:, 0:FAN * D].rearrange("p (f d) -> p f d", f=FAN),
                                               z[:, t:t + 1, :].to_broadcast([TP, FAN, D]), ALU.mult))
                        link(dve.tensor_reduce(logit[:, w, :], prod[:], X, ALU.add))
                        dve.tensor_tensor(logit[:, w, :], logit[:, w, :], row[:, FAN * D:ROW], ALU.add).then_inc(
                            sg["row_in_used"], 1)
                        if level >= 1:
                            add_out(level - 1, w)
                    dve.wait_ge(sg["row_in_used"], (level + 1) * W)
                    gelu(level)
                    if level < DEPTH:
                        ge = gel[:, level % 2, :, :]
                        link(dve.tensor_reduce(best[:], ge, X, ALU.max))
                        link(dve.tensor_tensor(eq[:], ge, best[:].unsqueeze(2).to_broadcast([TP, W, FAN]), ALU.is_equal))
                        link(dve.tensor_tensor(eq[:], eq[:], fan_less[:], ALU.mult))
                        link(dve.tensor_reduce(move[:].rearrange("p t f -> p (t f)"), eq[:], X, ALU.min))
                        link(dve.tensor_scalar(node[:], node[:], float(FAN),
                                               float(9 + first[level + 1] - FAN * first[level]), ALU.mult, ALU.add))
                        link(dve.tensor_tensor(node[:], node[:], move[:], ALU.add))
                for w in range(W):
                    add_out(DEPTH, w)


LAST = 8


def program(nc, d):
    with ExitStack() as st:
        c = Core(nc, d)
        sb = alloc(c, st)
        c.x = sb("x", [TP, PAIRS, D])
        c.ident = sb("ident", [128, 128])
        c.ones = sb("ones", [128, 128])
        c.ybias = sb("ybias", [TP, D])
        c.ps = st.enter_context(nc.psum_tensor("ps", [128, 8, 512], F32))
        stage_load(c)

        def attend(name, hd, scale, latents=False, side=False):
            with ExitStack() as inner:
                n_prod = alloc(c, inner)(f"n_{name}", [D, H, D])
                with ExitStack() as prep:
                    z = alloc(c, prep)(f"z_{name}", [TP, PAIRS, D])
                    zt = alloc(c, prep)(f"zt_{name}", [D, TOK])
                    if latents:
                        stage_norm(c, c.x, z, None)
                        stage_norm(c, z, z, zt, affine=(d["ln_l_g"], d["ln_l_b"]))
                        stage_own_keys(c, z, zt)
                    else:
                        stage_norm(c, c.x, z, zt)
                    stage_fold(c, name, hd, zt, n_prod, biased=(name == "a0"))
                stage_attention(c, name, n_prod, scale, latents, side)
            stage_add_y(c, biased=(name == "a0"))

        attend("a0", D // H, (D // H) ** -0.5)
        if LAST >= 2:
            layer0_ffn(c)
        if LAST >= 3:
            stage_context_norm(c)
            attend("a1", 64, 64 ** -0.5, latents=True)
        if LAST >= 4:
            layer1_ffn(c)
        if LAST >= 5:
            layer2_attention(c)
        if LAST >= 6:
            layer2_ffn(c)
        if LAST >= 7:
            stage_mask(c)
            attend("a3", 64, 1.0, side=True)
        if LAST >= 8:
            layer3_ffn(c)
        stage_store(c)


def kernel(**a):
    import numpy as np
    import concourse.bacc as bacc
    from concourse import mybir as _mybir
    from concourse.bass_utils import run_bass_kernel_spmd

    a = {k: np.asarray(v) for k, v in a.items()}
    f32 = np.float32
    ins = {}

    def put(name, array):
        ins[name] = np.ascontiguousarray(array)

    def heads_t(w, hd):
        return w.reshape(D, H, hd).transpose(2, 1, 0)

    def heads(w, hd):
        return w.reshape(H, hd, D).transpose(1, 0, 2)

    ctx = a["ctx_1024"]
    put("x", a["x"].reshape(TOK, D))
    put("ctx", ctx)
    put("ctxT", ctx.transpose(0, 2, 1))
    wkv = a["L0_xattn_Wkv"]
    put("a0_wqT", heads_t(a["L0_xattn_Wq"], 8))
    put("a0_wkT", heads_t(wkv[:, :D], 8))
    put("a0_wvT", heads_t(wkv[:, D:], 8))
    put("a0_wo", heads(a["L0_xattn_Wo"], 8))
    put("a0_bq", a["L0_xattn_bq"].reshape(H, 8).T)
    put("a0_bv", np.broadcast_to(a["L0_xattn_bkv"][D:].reshape(H, 8).T[:, :, None], (8, H, TP)))
    put("a0_bo", a["L0_xattn_bo"][None])
    inner = H * 64
    wkv = a["L1_xattn_Wkv"]
    put("a1_wqT", heads_t(a["L1_xattn_Wq"], 64))
    put("a1_wkT", heads_t(wkv[:, :inner], 64))
    put("a1_wvT", heads_t(wkv[:, inner:], 64))
    put("a1_wo", heads(a["L1_xattn_Wout"], 64))
    put("ln_m_col", np.stack([a["L1_xattn_ln_m_g"], a["L1_xattn_ln_m_b"]], 1))
    put("ln_m_row", np.broadcast_to(np.stack([a["L1_xattn_ln_m_g"], a["L1_xattn_ln_m_b"]])[None], (KT, 2, D)))
    for k in ("ln_l_g", "ln_l_b"):
        put(k, np.broadcast_to(a[f"L1_xattn_{k}"][None], (TP, D)))
    for k, name in (("wqT", "Wq"), ("wkT", "Wk"), ("wvT", "Wv")):
        put(f"a3_{k}", heads_t(a[f"L3_xattn_{name}"], 64))
    put("a3_wo", heads(a["L3_xattn_Wo"], 64))
    side = a["fside_1x16xSxS2_0"]
    put("side_rows", side.reshape(H // 2, TP, SK).transpose(1, 0, 2))
    put("side_cols", side.reshape(HQ, SK // KT, KT).transpose(2, 1, 0))
    mask = a["mask_Bx1x1xS2_ff0"].reshape(B, SK)
    put("mask", mask)
    put("mask_col", mask.reshape(B, SK // KT, KT).transpose(0, 2, 1))
    for k in ("ln1_w", "ln1_b", "ln2_w", "ln2_b"):
        put(k, np.broadcast_to(a[f"L0_ffn_{k}"][:, None, :], (2, TP, D)))
    put("f0_wq", a["L0_ffn_wq"])
    put("f0_wk", a["L0_ffn_wk"])
    put("f0_wv", a["L0_ffn_wv"])
    put("f0_wo", a["L0_ffn_wo"])
    put("f0_bqk", np.stack([a["L0_ffn_bq"], a["L0_ffn_bk"]], -1))
    put("f0_bvo", np.stack([a["L0_ffn_bv"], a["L0_ffn_bo"]], 1))
    put("f0_gate_w", a["L0_ffn_gate_w"])
    put("f0_gate_b", a["L0_ffn_gate_b"][:, None, :])
    put("f0_w1", a["L0_ffn_e_w1"].transpose(0, 2, 1, 3))
    put("f0_b1", a["L0_ffn_e_b1"].reshape(2, E, 4, 128).transpose(0, 3, 1, 2))
    put("f0_w2", a["L0_ffn_e_w2"].reshape(2, E, 4, 128, D).transpose(0, 3, 1, 2, 4))
    put("f0_b2", a["L0_ffn_e_b2"])
    put("f1_w1T", a["L1_ffn_W1"].T)
    put("f1_b1", a["L1_ffn_b1"].reshape(4, 128).T)
    put("f1_w2T", a["L1_ffn_W2"].T.reshape(4, 128, D).transpose(1, 0, 2))
    put("f1_b2", a["L1_ffn_b2"][None])
    own = ctx[:, :S, :]
    put("own_rows", own.reshape(PAIRS, TP, D).transpose(1, 0, 2))
    put("own_cols", own.reshape(TOK, D).T)
    put("f2_gate_w", a["L2_ffn_gate_w"])
    put("f2_w1", a["L2_ffn_w1"].transpose(1, 0, 2))
    put("f2_w2", a["L2_ffn_w2"].reshape(E, 4, 128, D).transpose(2, 0, 1, 3))
    nodes = TREE_P * G
    put("tree_in", np.concatenate([a["L3_ffn_W_in"].reshape(nodes, FAN * D), a["L3_ffn_b_in"].reshape(nodes, FAN)], 1))
    put("tree_out", a["L3_ffn_W_out"].T.reshape(nodes, FAN * D))
    put("ident", np.eye(128, dtype=f32))
    put("ones", np.ones((128, 128), f32))
    p16 = np.arange(16)[:, None, None]
    put("negsel", np.broadcast_to(np.where(p16 % 8 == np.arange(8)[None, :, None], f32(-1), f32(0)), (16, 8, TP)))
    r = np.arange(TP)
    same = (r[:, None] // S) == (r[None, :] // S)
    before = same & (r[None, :] < r[:, None])
    put("causal", np.where(same & (r[None, :] <= r[:, None]), f32(0), f32(-1e30)))
    put("same", same.astype(f32))
    put("before", before.astype(f32))
    put("head_of", (np.arange(128)[:, None] // 8 == np.arange(16)[None, :]).astype(f32))
    e8 = np.arange(8)
    put("earlier", np.broadcast_to((e8[None, :] < e8[:, None]).astype(f32)[None], (TP, 8, 8)))
    put("platform", np.broadcast_to(np.arange(4, dtype=f32)[None, None, :] * f32(G), (TP, PAIRS, 4)))
    put("fan_less", np.broadcast_to(np.arange(4, dtype=f32)[None, None, :] - f32(9), (TP, 32, 4)))

    nc = bacc.Bacc("TRN2", target_bir_lowering=False, num_devices=1)
    dram = {k: nc.dram_tensor(k, v.shape, _mybir.dt.from_np(v.dtype), kind="ExternalInput").ap() for k, v in ins.items()}
    dram["qk"] = nc.dram_tensor("qk", (B, D, HQ), F32, kind="Internal").ap()
    dram["y"] = nc.dram_tensor("y", (PAIRS, TP, D), F32, kind="Internal").ap()
    dram["ctx1"] = nc.dram_tensor("ctx1", (B, SK + S, D), F32, kind="Internal").ap()
    dram["ctx1T"] = nc.dram_tensor("ctx1T", (B, D, SK + S), F32, kind="Internal").ap()
    dram["mask_parts"] = nc.dram_tensor("mask_parts", (B, 2, SK), F32, kind="Internal").ap()
    dram["out"] = nc.dram_tensor("out", (TOK, D), F32, kind="ExternalOutput").ap()
    program(nc, dram)
    got = run_bass_kernel_spmd(nc, [ins], core_ids=[0])
    return got.results[0]["out"].reshape(B, S, D)
```

```python
from contextlib import ExitStack

import concourse.bass as bass
from concourse import mybir

F32 = mybir.dt.float32
F32R = mybir.dt.float32r
U32 = mybir.dt.uint32
ALU = mybir.AluOpType
ACT = mybir.ActivationFunctionType
X = mybir.AxisListType.X

B, S, D, SK = 16, 56, 128, 1500
H = 16
PAIRS, TP = B // 2, 2 * S
TOK = B * S
HALF = TOK // 2
HQ = H * S
KT = 125
E, DFF = 8, 512
CAP = 2 * S // E
TREE_P, FAN, DEPTH = 4, 4, 5
G = (FAN ** (DEPTH + 1) - 1) // 3
LN_EPS = 1e-5
DMA = 16


class Signals:

    def __init__(self, nc, stage):
        self.nc, self.stage, self.stack, self.by_name = nc, stage, ExitStack(), {}

    def __getitem__(self, what):
        if what not in self.by_name:
            self.by_name[what] = self.stack.enter_context(self.nc.semaphore(f"{self.stage}_{what}"))
        return self.by_name[what]


class Core:

    def __init__(self, nc, dram):
        self.nc, self.dram = nc, dram
        self.old = None
        self.now = None
        self.count = 0

    def stage(self, name):
        if self.old is not None:
            self.old.stack.close()
        self.old, self.now = self.now, Signals(self.nc, f"s{self.count}_{name}")
        self.count += 1
        return self.now

    def clear_old(self, eng):
        if self.old is not None:
            for sem in self.old.by_name.values():
                eng.sem_clear(sem)


class Link:

    def __init__(self, eng, sem):
        self.eng, self.sem, self.n = eng, sem, 0
        self.start = 0

    def __call__(self, ins):
        self.n += 1
        ins.then_inc(self.sem, 1)
        self.eng.wait_ge(self.sem, self.start + self.n)


def halves(psum_two_banks):
    return psum_two_banks[:, :, 0:HALF]


def two(ap):
    return ap.rearrange("p (a c) -> p a c", a=2)


def alloc(c, stack):
    def sb(name, shape, dt=F32):
        return stack.enter_context(c.nc.sbuf_tensor(f"sb{c.count}_{name}", shape, dt))
    return sb


def stage_load(c):
    nc, d, sg = c.nc, c.dram, c.stage("load")
    with nc.Block() as block:
        @block.sync
        def _(sp):
            sp.dma_start(c.x[:], d["x"].rearrange("(t p) d -> p t d", p=TP)).then_inc(sg["loaded"], DMA)
            sp.dma_start(c.ident[:], d["ident"]).then_inc(sg["loaded"], DMA)
            sp.dma_start(c.ones[:], d["ones"]).then_inc(sg["loaded"], DMA)
            sp.wait_ge(sg["loaded"], 3 * DMA)


def stage_norm(c, src, dst, dst_t=None, affine=None):
    nc, d, sg = c.nc, c.dram, c.stage("norm")
    ps = c.ps
    with ExitStack() as st:
        sb = alloc(c, st)
        stats = sb(f"stats{c.count}", [TP, PAIRS, 6])
        mv = sb(f"mv{c.count}", [TP, PAIRS, 2])
        var = sb(f"var{c.count}", [TP, PAIRS])
        std = sb(f"std{c.count}", [TP, PAIRS])
        rstd = sb(f"rstd{c.count}", [TP, PAIRS])
        gb = sb(f"gb{c.count}", [TP, 2, D]) if affine else None
        with nc.Block() as block:
            @block.sync
            def _(sp):
                c.clear_old(sp)
                if affine:
                    for n, name in enumerate(affine):
                        sp.dma_start(gb[:, n, :], name).then_inc(sg["affine_loaded"], DMA)
                    sp.wait_ge(sg["affine_loaded"], 2 * DMA)

            @block.vector
            def _(dve):
                link = Link(dve, sg["dve_chain"])
                for t in range(PAIRS):
                    last = dve.bn_stats(stats[:, t, :], src[:, t, :])
                link(last)
                for t in range(PAIRS):
                    last = dve.bn_aggr(mv[:, t, :], stats[:, t, :])
                link(last)
                dve.tensor_scalar(var[:], mv[:, :, 1], LN_EPS, None, ALU.add).then_inc(sg["var_ready"], 1)
                dve.wait_ge(sg["std_ready"], 1)
                link(dve.reciprocal(rstd[:], std[:]))
                for t in range(PAIRS):
                    last = dve.tensor_scalar(dst[:, t, :], src[:, t, :], mv[:, t, 0:1], rstd[:, t:t + 1],
                                             ALU.subtract, ALU.mult)
                if affine:
                    link(last)
                    dve.wait_ge(sg["affine_loaded"], 2 * DMA)
                    link(dve.tensor_tensor(dst[:], dst[:], gb[:, 0:1, :].to_broadcast([TP, PAIRS, D]), ALU.mult))
                    last = dve.tensor_tensor(dst[:], dst[:], gb[:, 1:2, :].to_broadcast([TP, PAIRS, D]), ALU.add)
                last.then_inc(sg["dst_ready"], 1)
                if dst_t is not None:
                    dve.wait_ge(sg["transposed"], 1)
                    dve.tensor_copy(two(dst_t[:]), halves(ps[:, 0:2, :])).then_inc(sg["dst_t_ready"], 1)

            @block.scalar
            def _(act):
                act.wait_ge(sg["var_ready"], 1)
                act.activation(std[:], var[:], ACT.Sqrt).then_inc(sg["std_ready"], 1)

            if dst_t is not None:
                @block.tensor
                def _(pe):
                    pe.wait_ge(sg["dst_ready"], 1)
                    for t in range(PAIRS):
                        last = pe.transpose(ps[:, t // 4, (t % 4) * TP:(t % 4 + 1) * TP], dst[:, t, :],
                                            c.ident[0:TP, 0:TP])
                    last.then_inc(sg["transposed"], 1)


def stage_fold(c, name, hd, zt, n_out, biased):
    nc, d, sg = c.nc, c.dram, c.stage("fold")
    ps = c.ps
    with ExitStack() as st:
        sb = alloc(c, st)
        w = {k: sb(f"{k}_{name}", [hd, H, D]) for k in ("wqT", "wkT", "wvT", "wo")}
        m = sb(f"m_{name}", [D, H, D])
        qk = sb(f"qk_{name}", [D, B, H, S])
        if biased:
            bq = sb(f"bq_{name}", [hd, H])
            bv = sb(f"bv_{name}", [hd, H, TP])
            bo = sb(f"bo_{name}", [1, D])
            wb = sb(f"wb_{name}", [D, H])
        with nc.Block() as block:
            @block.sync
            def _(sp):
                c.clear_old(sp)
                for k in ("wqT", "wkT", "wvT", "wo"):
                    sp.dma_start(w[k][:], d[f"{name}_{k}"]).then_inc(sg["weights"], DMA)
                if biased:
                    sp.dma_start(bq[:], d[f"{name}_bq"]).then_inc(sg["weights"], DMA)
                    sp.dma_start(bv[:], d[f"{name}_bv"]).then_inc(sg["weights"], DMA)
                    sp.dma_start(bo[:], d[f"{name}_bo"]).then_inc(sg["weights"], DMA)
                for h in range(0, H, 4):
                    sp.wait_ge(sg["q_folded"], h + 4)
                    sp.dma_start(d["qk"].rearrange("b p n -> p b n")[:, :, h * S:(h + 4) * S],
                                 qk[:, :, h:h + 4, :].rearrange("p b h q -> p b (h q)")).then_inc(sg["stored"], DMA)
                sp.wait_ge(sg["stored"], H // 4 * DMA)

            @block.tensor
            def _(pe):
                pe.wait_ge(sg["weights"], (7 if biased else 4) * DMA)
                for h in range(H):
                    last = pe.matmul(ps[:, h // 4, (h % 4) * D:(h % 4 + 1) * D], w["wqT"][:, h, :], w["wkT"][:, h, :],
                                     start=True, stop=True)
                last.then_inc(sg["m_product"], 1)
                for h in range(H):
                    last = pe.matmul(ps[:, 4 + h // 4, (h % 4) * D:(h % 4 + 1) * D], w["wvT"][:, h, :],
                                     w["wo"][:, h, :], start=True, stop=True)
                last.then_inc(sg["n_product"], 1)
                if biased:
                    pe.wait_ge(sg["n_ready"], 1)
                    for h in range(H):
                        last = pe.matmul(ps[:, 4, h:h + 1], w["wkT"][:, h, :], bq[:, h:h + 1], start=True, stop=True)
                    last.then_inc(sg["wb_product"], 1)
                    for h in range(H):
                        pe.matmul(ps[0:TP, 5, 0:D], bv[:, h, :], w["wo"][:, h, :], start=(h == 0), stop=False)
                    pe.matmul(ps[0:TP, 5, 0:D], c.ones[0:1, 0:TP], bo[:], start=False, stop=True).then_inc(
                        sg["ybias_product"], 1)
                pe.wait_ge(sg["m_ready"], 1)
                for h in range(H):
                    slot = 2 * (h % 2)
                    if h >= 2:
                        pe.wait_ge(sg["q_folded"], h - 1)
                    for a in range(2):
                        last = pe.matmul(ps[:, slot + a, 0:HALF], m[:, h, :], zt[:, a * HALF:(a + 1) * HALF],
                                         start=True, stop=True)
                    last.then_inc(sg["q_product"], 1)

            @block.scalar
            def _(act):
                act.wait_ge(sg["m_product"], 1)
                act.activation(m[:].rearrange("p (a h) d -> p a (h d)", a=4), ps[:, 0:4, :], ACT.Copy).then_inc(
                    sg["m_ready"], 1)
                if biased:
                    act.wait_ge(sg["wb_ready"], 1)
                for h in range(H):
                    slot = 2 * (h % 2)
                    act.wait_ge(sg["q_product"], h + 1)
                    src = halves(ps[:, slot:slot + 2, :]).rearrange("p a (b q) -> p a b q", b=B // 2)
                    dst = qk[:, :, h, :].rearrange("p (a b) q -> p a b q", a=2)
                    if biased:
                        act.activation(dst, src, ACT.Identity, bias=wb[:, h:h + 1]).then_inc(sg["q_folded"], 1)
                    else:
                        act.activation(dst, src, ACT.Copy).then_inc(sg["q_folded"], 1)

            @block.vector
            def _(dve):
                dve.wait_ge(sg["n_product"], 1)
                dve.tensor_copy(n_out[:].rearrange("p (a h) d -> p a (h d)", a=4), ps[:, 4:8, :]).then_inc(
                    sg["n_ready"], 1)
                if biased:
                    dve.wait_ge(sg["wb_product"], 1)
                    dve.tensor_copy(wb[:], ps[:, 4, 0:H]).then_inc(sg["wb_ready"], 1)
                    dve.wait_ge(sg["ybias_product"], 1)
                    dve.tensor_copy(c.ybias[:], ps[0:TP, 5, 0:D]).then_inc(sg["ybias_ready"], 1)


def stage_context_norm(c):
    nc, d, sg = c.nc, c.dram, c.stage("ctxnorm")
    ps = c.ps
    NT = SK // KT
    with ExitStack() as st:
        sb = alloc(c, st)
        raw = sb("cn_raw", [KT, 2, NT, D])
        z = sb("cn_z", [KT, 2, NT, D])
        zt = sb("cn_zt", [D, 2, SK])
        stats = sb("cn_stats", [KT, NT, 6])
        mv = sb("cn_mv", [KT, NT, 2])
        var = sb("cn_var", [KT, NT])
        std = sb("cn_std", [KT, NT])
        rstd = sb("cn_rstd", [KT, NT])
        shift = sb("cn_shift", [KT, 2, NT])
        scale = sb("cn_scale", [KT, 2, NT])
        gb = sb("cn_gb", [D, 2])
        gbrow = sb("cn_gbrow", [KT, 2, D])
        src = d["ctx"].rearrange("b (t p) d -> b p t d", p=KT)
        dst = d["ctx1"][:, 0:SK, :].rearrange("b (t p) d -> b p t d", p=KT)
        with nc.Block() as block:
            @block.sync
            def _(sp):
                c.clear_old(sp)
                sp.dma_start(gb[:], d["ln_m_col"]).then_inc(sg["affine"], DMA)
                sp.dma_start(gbrow[:], d["ln_m_row"]).then_inc(sg["affine"], DMA)
                for j in range(2):
                    sp.dma_start(raw[:, j, :, :], src[j]).then_inc(sg[f"raw_loaded_{j}"], DMA)
                    sp.sem_inc(sg[f"rows_stored_{j}"], DMA)
                    sp.sem_inc(sg[f"zt_stored_{j}"], DMA)

                def pair(i, final):
                    for j in range(2):
                        if not final:
                            sp.wait_ge(sg["normalised"], i * 2 + (j + 3))
                            sp.dma_start(raw[:, j, :, :], src[i * 2 + (j + 2)]).then_inc(sg[f"raw_loaded_{j}"], DMA)
                        sp.wait_ge(sg["zt_ready"], i * 8 + 4 * (j + 1))
                        sp.dma_start(d["ctx1T"][i * 2 + j, :, 0:SK], zt[:, j, :]).then_inc(sg[f"zt_stored_{j}"], DMA)
                        sp.wait_ge(sg["rows_ready"], i * 2 + (j + 1))
                        sp.dma_start(dst[i * 2 + j], z[:, j, :, :]).then_inc(sg[f"rows_stored_{j}"], DMA)

                with sp.Fori(0, PAIRS - 1) as i:
                    pair(i, False)
                pair(PAIRS - 1, True)
                for j in range(2):
                    sp.wait_ge(sg[f"rows_stored_{j}"], (PAIRS + 1) * DMA)
                    sp.wait_ge(sg[f"zt_stored_{j}"], (PAIRS + 1) * DMA)

            @block.vector
            def _(dve):
                with dve.Fori(0, PAIRS) as i:
                    for j in range(2):
                        dve.wait_ge(sg[f"raw_loaded_{j}"], i * DMA + DMA)
                        for t in range(NT):
                            last = dve.bn_stats(stats[:, t, :], raw[:, j, t, :])
                        last.then_inc(sg["stats"], 1)
                        dve.wait_ge(sg["stats"], i * 2 + (j + 1))
                        dve.sem_inc(sg["dve_seen"], 1)
                        for t in range(NT):
                            last = dve.bn_aggr(mv[:, t, :], stats[:, t, :])
                        last.then_inc(sg["aggr"], 1)
                        dve.wait_ge(sg["aggr"], i * 2 + (j + 1))
                        dve.tensor_scalar(var[:], mv[:, :, 1], LN_EPS, None, ALU.add).then_inc(sg["var"], 1)
                        dve.wait_ge(sg["std"], i * 2 + (j + 1))
                        dve.wait_ge(sg["normalised"], i * 2 + (j + 1))
                        dve.reciprocal(scale[:, j, :], std[:]).then_inc(sg["rstd"], 1)
                        dve.wait_ge(sg["rstd"], i * 2 + (j + 1))
                        dve.scalar_tensor_tensor(shift[:, j, :], mv[:, :, 0], -1.0, scale[:, j, :], ALU.mult,
                                                 ALU.mult).then_inc(sg["shift"], 1)

            @block.gpsimd
            def _(pool):
                pool.wait_ge(sg["affine"], 2 * DMA)
                with pool.Fori(0, PAIRS) as i:
                    for j in range(2):
                        pool.wait_ge(sg["transposed"], i * 8 + 4 * (j + 1))
                        pool.tensor_tensor(z[:, j, :, :], z[:, j, :, :],
                                           gbrow[:, 0:1, :].to_broadcast([KT, NT, D]), ALU.mult).then_inc(sg["times_g"], 1)
                        pool.wait_ge(sg["times_g"], i * 2 + (j + 1))
                        pool.tensor_tensor(z[:, j, :, :], z[:, j, :, :],
                                           gbrow[:, 1:2, :].to_broadcast([KT, NT, D]), ALU.add).then_inc(sg["rows_ready"], 1)

            @block.scalar
            def _(act):
                act.sem_inc(sg["normalised"], 2)
                act.wait_ge(sg["affine"], 2 * DMA)
                act.wait_ge(sg["var"], 1)
                act.activation(std[:], var[:], ACT.Sqrt).then_inc(sg["std"], 1)

                def pair(i, final):
                    for j in range(2):
                        act.wait_ge(sg["shift"], i * 2 + (j + 1))
                        act.wait_ge(sg[f"rows_stored_{j}"], i * DMA + DMA)
                        for t in range(NT):
                            last = act.activation(z[:, j, t, :], raw[:, j, t, :], ACT.Identity,
                                                  scale=scale[:, j, t:t + 1], bias=shift[:, j, t:t + 1])
                        last.then_inc(sg["normalised"], 1)
                        if not (final and j == 1):
                            act.wait_ge(sg["var"], i * 2 + (j + 2))
                            act.activation(std[:], var[:], ACT.Sqrt).then_inc(sg["std"], 1)
                        act.wait_ge(sg[f"zt_stored_{j}"], i * DMA + DMA)
                        for q in range(4):
                            act.wait_ge(sg["transposed"], i * 8 + (4 * j + q + 1))
                            act.activation(zt[:, j, q * 375:(q + 1) * 375], ps[:, 4 * j + q, 0:375], ACT.Identity,
                                           scale=gb[:, 0:1], bias=gb[:, 1:2]).then_inc(sg["zt_ready"], 1)

                with act.Fori(0, PAIRS - 1) as i:
                    pair(i, False)
                pair(PAIRS - 1, True)

            @block.tensor
            def _(pe):
                with pe.Fori(0, PAIRS) as i:
                    for j in range(2):
                        pe.wait_ge(sg["normalised"], i * 2 + (j + 3))
                        for q in range(4):
                            for k in range(3):
                                last = pe.transpose(ps[:, 4 * j + q, k * KT:(k + 1) * KT], z[:, j, 3 * q + k, :],
                                                    c.ident[0:KT, 0:KT])
                            last.then_inc(sg["transposed"], 1)


def stage_attention(c, name, n_in, scale, own_keys, side):
    nc, d, sg = c.nc, c.dram, c.stage(name)
    ps = c.ps
    widths = [KT] * (SK // KT) + ([S] if own_keys else [])
    NT = len(widths)
    NK = sum(widths)
    NKP = KT * NT
    chunks = [(k, 500) for k in range(0, SK, 500)] + ([(SK, S)] if own_keys else [])
    NC = len(chunks)
    P_BUFS = 3
    T_LOADS = 2
    N_LOADS = 1 + (1 if own_keys else 0) + (2 if side else 0)
    S_BANK, U_BANK, A_BANK = 0, 4, 6
    ctx_rows = d["ctx1"] if own_keys else d["ctx"]
    ctx_cols = d["ctx1T"] if own_keys else d["ctxT"]

    CH = (H // 2) * NC
    PAIR_USES = 2 * (2 + CH + 1) + 2
    GRANTED = 4

    def use_of(i, j, u):
        return i * PAIR_USES + (CH + 1 + j * (5 + CH) + u)

    def bank_of(j, u):
        return A_BANK + (CH + 1 + j * (5 + CH) + u) % 2

    def first_chunk(j):
        return 4 if j == 0 else 2

    todo = [(hp, m) for hp in range(H // 2) for m in range(NC)]
    NORM_AT, Y_AT = 3, 5

    def spread(first):
        places = range(first, NT - 1)
        return {k: range(CH * n // len(places), CH * (n + 1) // len(places)) for n, k in enumerate(places)}

    plan = [spread(Y_AT), spread(NORM_AT + 2)]

    def batch(i, j):
        return i * 2 + j

    def rows_loads(i):
        return i * (N_LOADS * DMA) + N_LOADS * DMA

    def slot_of(j, k):
        return S_BANK + 2 * ((j * NT + k) % 2)

    def buf_of(j, k):
        return (j * NT + k) % P_BUFS

    def p_free(n, j, k):
        m = j * NT + k
        back = P_BUFS if m >= P_BUFS else m + 2 * NT - max(t for t in range(2 * NT) if t % P_BUFS == m)
        return n * NT + (k + 1 - back + P_BUFS)

    with ExitStack() as st:
        sb = alloc(c, st)
        ct = sb("ct", [D, NK])
        ct_hi = [sb(f"ct_hi{j}", [D, NKP], F32R) for j in range(2)]
        ct_lo = [sb(f"ct_lo{j}", [D, NKP], F32R) for j in range(2)]
        cn = [sb(f"cn{j}", [KT, NT, D]) for j in range(2)]
        qf = sb("qf", [D, HQ])
        q_hi = [sb(f"q_hi{j}", [D, HQ], F32R) for j in range(2)]
        q_lo = [sb(f"q_lo{j}", [D, HQ], F32R) for j in range(2)]
        part_max = sb("part_max", [TP, H // 2, NC])
        row_max = sb("row_max", [TP, H // 2])
        max_hi = sb("max_hi", [TP, H // 2], F32R)
        max_parts = sb("max_parts", [TP, 2 * (H // 2)])
        neg_max = [sb(f"neg_max{j}", [16, HQ], F32R) for j in range(2)]
        negsel = sb("negsel", [16, H // 2, TP])
        ones_r = sb("ones_r", [16, KT], F32R)
        p_buf = [sb(f"p{n}", [KT, HQ]) for n in range(P_BUFS)]
        p_sum = sb("p_sum", [KT, HQ])
        recip = sb("recip", [D, HQ])
        u_norm = sb("u_norm", [D, H, TP])
        y_sb = sb("y_sb", [TP, D])
        if side:
            side_rows = sb("side_rows", [TP, H // 2, SK])
            side_cols = sb("side_cols", [KT, NT, HQ])
            mask_rows = sb("mask_rows", [2, SK], F32R)
            mask_col = [sb(f"mask_col{j}", [KT, NT]) for j in range(2)]
            scratch = sb("scratch", [TP, 500])

        def emit(run, prologue, pair, epilogue):
            prologue()
            pair(0, True, False)
            with run.Fori(1, PAIRS - 1) as i:
                pair(i, False, False)
            pair(PAIRS - 1, False, True)
            epilogue()

        with nc.Block() as block:
            @block.sync
            def _(sp):
                c.clear_old(sp)
                sp.dma_start(negsel[:], d["negsel"]).then_inc(sg["constants"], DMA)

                def load_t(n):
                    sp.dma_start(ct[:], ctx_cols[n]).then_inc(sg["t_loaded"], DMA)
                    sp.dma_start(qf[:], d["qk"][n]).then_inc(sg["t_loaded"], DMA)

                def load_n(n, j):
                    loaded = sg[f"rows_loaded_{j}"]
                    sp.dma_start(cn[j][:, 0:SK // KT, :],
                                 ctx_rows[n, 0:SK, :].rearrange("(t p) d -> p t d", p=KT)).then_inc(loaded, DMA)
                    if own_keys:
                        sp.dma_start(cn[j][0:S, NT - 1, :], ctx_rows[n, SK:SK + S, :]).then_inc(loaded, DMA)
                    if side:
                        sp.dma_start(mask_rows[:].bitcast(F32), d["mask_parts"][n]).then_inc(loaded, DMA)
                        sp.dma_start(mask_col[j][:], d["mask_col"][n]).then_inc(loaded, DMA)

                def store_y(i):
                    sp.wait_ge(sg["a_read"], use_of(i, 0, 4))
                    sp.sem_inc(sg["sp_seen"], 1)
                    sp.dma_start(d["y"][i - 1], y_sb[:]).then_inc(sg["y_stored"], DMA)
                    sp.wait_ge(sg["y_stored"], i * DMA)
                    sp.sem_inc(sg["y_sb_free"], 1)

                def prologue():
                    load_t(0)
                    load_n(0, 0)
                    if side:
                        sp.dma_start(side_rows[:], d["side_rows"]).then_inc(sg["constants"], DMA)
                    sp.sem_inc(sg["y_sb_free"], 1)
                    sp.wait_ge(sg["parts_made"], 1)
                    load_t(1)
                    if side:
                        sp.dma_start(side_cols[:], d["side_cols"]).then_inc(sg["side_cols_loaded"], DMA)

                def pair(i, first, final):
                    for j in range(2):
                        n = batch(i, j)
                        if not (final and j == 1):
                            sp.wait_ge(sg["p_applied"], n * NT + P_BUFS)
                            sp.sem_inc(sg["sp_seen"], 1)
                            sp.wait_ge(sg["a_read"], use_of(i, j, GRANTED if first and j == 0 else 0))
                            sp.sem_inc(sg["sp_seen"], 1)
                            load_n(n + 1, 1 - j)
                        if j == 0 and not first:
                            store_y(i)
                        if not final:
                            sp.wait_ge(sg["parts_made"], n + 2)
                            sp.sem_inc(sg["sp_seen"], 1)
                            load_t(n + 2)

                emit(sp, prologue, pair, lambda: store_y(PAIRS))

            @block.tensor
            def _(pe):
                pe.sem_inc(sg["p_applied"], P_BUFS)
                pe.sem_inc(sg["a_full"], GRANTED)
                pe.sem_inc(sg["a_read"], GRANTED)
                for what in ("u_read", "sum_full", "p_ready", "u_made") + (("side_added",) if side else ()):
                    pe.sem_inc(sg[what], 1)

                def maxima(i, j, u, nj, hp, m):
                    k0, kn = chunks[m]
                    pe.wait_ge(sg["a_read"], use_of(i, j, u - 1))
                    out = ps[0:TP, bank_of(j, u), 0:kn]
                    last = pe.matmul(out, q_hi[nj][:, hp * TP:(hp + 1) * TP], ct_hi[nj][:, k0:k0 + kn],
                                     start=True, stop=not side)
                    if side:
                        last = pe.matmul(out, ones_r[0:2, 0:TP], mask_rows[:, k0:k0 + kn], start=False, stop=True)
                    last.then_inc(sg["a_full"], 1)

                def turn_maxima(i, j, u, n):
                    pe.wait_ge(sg["max_parts_ready"], n + 1)
                    pe.wait_ge(sg["a_read"], use_of(i, j, u - 1))
                    pe.transpose(ps[0:16, bank_of(j, u), 0:TP], max_parts[:], c.ident[0:TP, 0:TP]).then_inc(sg["a_full"], 1)

                def score(i, j, k, first, a):
                    n = batch(i, j)
                    if a == 0:
                        if k == 0:
                            pe.wait_ge(sg["parts_made"], n + 1)
                        if not (first and j == 0 and k < 2):
                            pe.wait_ge(sg["side_added"] if side else sg["p_ready"], n * NT + k)
                    out = ps[0:KT, slot_of(j, k) + a, 0:HALF]
                    cols = slice(a * HALF, (a + 1) * HALF)
                    keys = slice(k * KT, (k + 1) * KT)
                    pe.matmul(out, ct_hi[j][:, keys], q_hi[j][:, cols], start=True, stop=False)
                    pe.matmul(out, ct_hi[j][:, keys], q_lo[j][:, cols], start=False, stop=False)
                    pe.matmul(out, ct_lo[j][:, keys], q_hi[j][:, cols], start=False, stop=False)
                    if k == 0 and a == 0:
                        pe.wait_ge(sg["a_read"], use_of(i, j, GRANTED if first and j == 0 else 0))
                    last = pe.matmul(out, ones_r[:], neg_max[j][:, cols], start=False, stop=True)
                    if a == 1:
                        last.then_inc(sg["scores_full"], 1)

                def apply(i, j, k, a):
                    n = batch(i, j)
                    kn = widths[k]
                    if a == 0:
                        if k == 0:
                            pe.wait_ge(sg[f"rows_loaded_{j}"], rows_loads(i))
                            pe.wait_ge(sg["u_read"], n + 1)
                        pe.wait_ge(sg["p_ready"], n * NT + (k + 2))
                    last = pe.matmul(ps[:, U_BANK + a, 0:HALF], cn[j][0:kn, k, :],
                                     p_buf[buf_of(j, k)][0:kn, a * HALF:(a + 1) * HALF],
                                     start=(k == 0), stop=(k == NT - 1))
                    if a == 1:
                        last.then_inc(sg["p_applied"], 1)

                def total(i, j, n):
                    pe.wait_ge(sg["p_summed"], n * NT + P_BUFS)
                    pe.wait_ge(sg["a_read"], use_of(i, j, 0))
                    for a in range(2):
                        pe.matmul(ps[:, bank_of(j, a), 0:HALF], c.ones[0:KT, :], p_sum[:, a * HALF:(a + 1) * HALF],
                                  start=True, stop=True).then_inc(sg["a_full"], 1)

                def project(i):
                    pe.wait_ge(sg["u_made"], i * 2 + 1)
                    pe.wait_ge(sg["a_read"], use_of(i, 0, 2))
                    for a in range(2):
                        for h in range(H):
                            last = pe.matmul(ps[0:TP, bank_of(0, 2 + a), 0:64], u_norm[:, h, :],
                                             n_in[:, h, a * 64:(a + 1) * 64], start=(h == 0), stop=(h == H - 1))
                        last.then_inc(sg["a_full"], 1)

                def prologue():
                    pe.wait_ge(sg["high_made"], 1)
                    pe.wait_ge(sg["ones_made"], 1)
                    pe.wait_ge(sg["constants"], (2 if side else 1) * DMA)
                    pe.wait_ge(sg["rows_loaded_0"], N_LOADS * DMA)
                    for u, (hp, m) in enumerate(todo):
                        maxima(0, 0, u + GRANTED - (CH + 1), 0, hp, m)
                    turn_maxima(0, 0, CH + GRANTED - (CH + 1), 0)

                def pair(i, first, final):
                    for j in range(2):
                        n = batch(i, j)
                        start, ahead = first and j == 0, not (final and j == 1)
                        for k in range(NT):
                            coming = list(plan[j].get(k, ())) if ahead else []

                            def next_chunk():
                                if coming:
                                    x = coming.pop(0)
                                    maxima(i, j, first_chunk(j) + x, 1 - j, *todo[x])

                            score(i, j, k, first, 0)
                            if k == Y_AT and j == 0 and not first:
                                project(i)
                            if ahead and k == min(plan[j]):
                                pe.wait_ge(sg["high_made"], n + 2)
                                pe.wait_ge(sg["a_read"], use_of(i, j, first_chunk(j)))
                                if side:
                                    pe.wait_ge(sg[f"rows_loaded_{1 - j}"], rows_loads(i + j))
                            next_chunk()
                            score(i, j, k, first, 1)
                            if k == 1 and not start:
                                total(i, j, n)
                            next_chunk()
                            for a in range(2):
                                if k >= 1:
                                    apply(i, j, k - 1, a)
                                elif j == 1:
                                    apply(i, 0, NT - 1, a)
                                elif not first:
                                    apply(i - 1, 1, NT - 1, a)
                                if k == NT - 1 and ahead and a == 0:
                                    turn_maxima(i, j, first_chunk(j) + CH, n + 1)
                                next_chunk()
                            while coming:
                                next_chunk()

                def epilogue():
                    for a in range(2):
                        apply(PAIRS - 1, 1, NT - 1, a)
                    pe.wait_ge(sg["a_read"], use_of(PAIRS - 1, 1, 2))
                    pe.sem_inc(sg["a_full"], CH + 1)
                    pe.sem_inc(sg["a_read"], CH + 1)
                    total(PAIRS, 0, B)
                    project(PAIRS)

                emit(pe, prologue, pair, epilogue)

            @block.scalar
            def _(act):
                def split_high(n, j):
                    act.wait_ge(sg["t_loaded"], n * (T_LOADS * DMA) + T_LOADS * DMA)
                    act.activation(ct_hi[j][:, 0:NK], ct[:], ACT.Copy)
                    act.activation(q_hi[j][:], qf[:], ACT.Copy).then_inc(sg["high_made"], 1)

                def copy_u(i, j, n):
                    act.wait_ge(sg["p_applied"], n * NT + P_BUFS)
                    if j == 1:
                        act.wait_ge(sg["a_full"], use_of(i, 0, 4))
                    act.activation(
                        u_norm[:, :, (1 - j) * S:(2 - j) * S].rearrange("p (a h) q -> p a h q", a=2),
                        halves(ps[:, U_BANK:U_BANK + 2, :]).rearrange("p a (h q) -> p a h q", q=S),
                        ACT.Copy).then_inc(sg["u_read"], 1)

                def copy_sum(i, j, n):
                    if not (isinstance(n, int) and n == 1):
                        act.wait_ge(sg["u_made"], n)
                    for a in range(2):
                        act.wait_ge(sg["a_full"], use_of(i, j, a + 1))
                        act.activation(recip[:, a * HALF:(a + 1) * HALF], ps[:, bank_of(j, a), 0:HALF],
                                       ACT.Copy).then_inc(sg["a_read"], 1)

                def pair(i, first, final):
                    for j in range(2):
                        n = batch(i, j)
                        start, ahead = first and j == 0, not (final and j == 1)
                        for k in range(NT):
                            kn = widths[k]
                            p = p_buf[buf_of(j, k)][0:kn, :]
                            if side:
                                if k == 0:
                                    act.wait_ge(sg[f"rows_loaded_{j}"], rows_loads(i))
                                act.wait_ge(sg["side_added"], n * NT + (k + 2))
                                act.activation(p, p, ACT.Exp, bias=mask_col[j][:, k:k + 1]).then_inc(sg["p_ready"], 1)
                            else:
                                act.wait_ge(sg["scores_full"], n * NT + (k + 1))
                                act.wait_ge(sg["p_applied"], p_free(n, j, k))
                                act.wait_ge(sg["p_summed"], p_free(n, j, k))
                                src = ps[0:kn, slot_of(j, k):slot_of(j, k) + 2, :]
                                act.activation(two(p), halves(src), ACT.Exp, scale=scale).then_inc(sg["p_ready"], 1)
                            if k == 0 and not start:
                                copy_u(i, j, n)
                            if k == 1 and not start:
                                copy_sum(i, j, n)
                            if k == 2 and ahead:
                                split_high(n + 1, 1 - j)

                def epilogue():
                    copy_u(PAIRS, 0, B)
                    copy_sum(PAIRS, 0, B)

                emit(act, lambda: split_high(0, 0), pair, epilogue)

            @block.gpsimd
            def _(pool):
                pool.sem_inc(sg["p_summed"], P_BUFS)

                def pair(i, first, final):
                    for j in range(2):
                        n = batch(i, j)
                        for k in range(1, NT):
                            kn = widths[k]
                            p = p_buf[buf_of(j, k)]
                            pool.wait_ge(sg["p_ready"], n * NT + (k + 2))
                            if k == 1:
                                if not (first and j == 0):
                                    pool.wait_ge(sg["a_full"], use_of(i, j, 2))
                                pool.tensor_tensor(p_sum[:], p_buf[buf_of(j, 0)][:], p[:], ALU.add).then_inc(
                                    sg["p_summed"], 2)
                            else:
                                pool.wait_ge(sg["p_summed"], n * NT + (k + P_BUFS))
                                pool.tensor_tensor(p_sum[0:kn, :], p_sum[0:kn, :], p[0:kn, :], ALU.add).then_inc(
                                    sg["p_summed"], 1)

                emit(pool, lambda: None, pair, lambda: None)

            @block.vector
            def _(dve):
                def split_low(n, j):
                    dve.wait_ge(sg["high_made"], n + 1)
                    dve.tensor_tensor(ct_lo[j][:, 0:NK], ct[:], ct_hi[j][:, 0:NK].bitcast(F32), ALU.subtract)

                def split_q_low(n, j):
                    dve.tensor_tensor(q_lo[j][:], qf[:], q_hi[j][:].bitcast(F32), ALU.subtract).then_inc(
                        sg["parts_made"], 1)

                def read_maxima(i, j, u, hp, m):
                    k0, kn = chunks[m]
                    bank = bank_of(j, u)
                    dve.wait_ge(sg["a_full"], use_of(i, j, u + 1))
                    if side:
                        dve.wait_ge(sg["a_read"], use_of(i, j, u))
                        dve.sem_inc(sg["chunk_seen"], 1)
                        dve.tensor_tensor_reduce(scratch[:, 0:kn], ps[0:TP, bank, 0:kn], side_rows[:, hp, k0:k0 + kn],
                                                 1.0, -3.0e38, ALU.add, ALU.max,
                                                 part_max[:, hp, m:m + 1]).then_inc(sg["a_read"], 1)
                    else:
                        dve.tensor_reduce(part_max[:, hp, m:m + 1], ps[0:TP, bank, 0:kn], X, ALU.max).then_inc(
                            sg["a_read"], 1)

                def finish_maxima(i, j, u, n, nj):
                    dve.wait_ge(sg["a_read"], use_of(i, j, u))
                    dve.tensor_reduce(row_max[:], part_max[:], X, ALU.max).then_inc(sg["row_max"], 1)
                    dve.wait_ge(sg["row_max"], n + 1)
                    dve.tensor_copy(max_hi[:], row_max[:]).then_inc(sg["max_hi"], 1)
                    dve.wait_ge(sg["max_hi"], n + 1)
                    dve.tensor_copy(max_parts[:, 0:H // 2], max_hi[:].bitcast(F32))
                    dve.tensor_tensor(max_parts[:, H // 2:H], row_max[:], max_hi[:].bitcast(F32),
                                      ALU.subtract).then_inc(sg["max_parts_ready"], 1)
                    bank = bank_of(j, u)
                    dve.wait_ge(sg["a_full"], use_of(i, j, u + 1))
                    dve.tensor_tensor(neg_max[nj][:].rearrange("p (a c) -> p a c", a=H // 2),
                                      ps[0:16, bank:bank + 1, 0:TP].to_broadcast([16, H // 2, TP]), negsel[:],
                                      ALU.mult).then_inc(sg["a_read"], 1)

                def invert(i, j, n, quarter):
                    if quarter == 0:
                        dve.wait_ge(sg["a_read"], use_of(i, j, 2))
                    cols = slice(quarter * HQ // 4, (quarter + 1) * HQ // 4)
                    dve.reciprocal(recip[:, cols], recip[:, cols]).then_inc(sg["inverted"], 1)

                def normalise(j, n):
                    dve.wait_ge(sg["inverted"], n * 4)
                    dve.wait_ge(sg["u_read"], n + 1)
                    u = u_norm[:, :, (1 - j) * S:(2 - j) * S]
                    dve.tensor_tensor(u, u, recip[:].rearrange("p (h q) -> p h q", q=S), ALU.mult).then_inc(
                        sg["u_made"], 1)

                def read_y(i):
                    dve.wait_ge(sg["y_sb_free"], i)
                    for a in range(2):
                        dve.wait_ge(sg["a_full"], use_of(i, 0, 3 + a))
                        dve.tensor_copy(y_sb[:, a * 64:(a + 1) * 64], ps[0:TP, bank_of(0, 2 + a), 0:64]).then_inc(
                            sg["a_read"], 1)

                def prologue():
                    for j in range(2):
                        if NKP > NK:
                            dve.memset(ct_hi[j][:, NK:NKP].bitcast(F32), 0.0)
                            dve.memset(ct_lo[j][:, NK:NKP].bitcast(F32), 0.0)
                    dve.memset(ones_r[:].bitcast(F32), 1.0).then_inc(sg["ones_made"], 1)
                    dve.wait_ge(sg["ones_made"], 1)
                    split_low(0, 0)
                    split_q_low(0, 0)
                    dve.wait_ge(sg["constants"], (2 if side else 1) * DMA)
                    for u, (hp, m) in enumerate(todo):
                        read_maxima(0, 0, u + GRANTED - (CH + 1), hp, m)
                    finish_maxima(0, 0, CH + GRANTED - (CH + 1), 0, 0)
                    if side:
                        dve.wait_ge(sg["side_cols_loaded"], DMA)

                def pair(i, first, final):
                    for j in range(2):
                        n = batch(i, j)
                        start, ahead = first and j == 0, not (final and j == 1)
                        for k in range(NT):
                            coming = [(first_chunk(j) + x, todo[x]) for x in plan[j].get(k, ())] if ahead else []
                            if k == Y_AT and j == 0 and not first:
                                read_y(i)
                            if coming:
                                u, chunk = coming.pop(0)
                                read_maxima(i, j, u, *chunk)
                            if side:
                                dve.wait_ge(sg["scores_full"], n * NT + (k + 1))
                                dve.wait_ge(sg["p_applied"], p_free(n, j, k))
                                dve.wait_ge(sg["p_summed"], p_free(n, j, k))
                                src = ps[0:KT, slot_of(j, k):slot_of(j, k) + 2, :]
                                dve.tensor_tensor(two(p_buf[buf_of(j, k)][:]), halves(src), two(side_cols[:, k, :]),
                                                  ALU.add).then_inc(sg["side_added"], 1)
                            if k in (1, 2) and not start:
                                invert(i, j, n, 2 * k - 2)
                                invert(i, j, n, 2 * k - 1)
                            if k == NORM_AT:
                                if not start:
                                    normalise(j, n)
                                if ahead:
                                    split_low(n + 1, 1 - j)
                            if k == NORM_AT + 1 and ahead:
                                split_q_low(n + 1, 1 - j)
                            for u, chunk in coming:
                                read_maxima(i, j, u, *chunk)
                            if k == NT - 1 and ahead:
                                finish_maxima(i, j, first_chunk(j) + CH, n + 1, 1 - j)

                def epilogue():
                    for quarter in range(4):
                        invert(PAIRS, 0, B, quarter)
                    normalise(0, B)
                    read_y(PAIRS)

                emit(dve, prologue, pair, epilogue)


def stage_add_y(c, biased):
    nc, d, sg = c.nc, c.dram, c.stage("addy")
    with nc.sbuf_tensor(f"y_all{c.count}", [TP, PAIRS, D], F32) as y, nc.Block() as block:
        @block.sync
        def _(sp):
            c.clear_old(sp)
            sp.dma_start(y[:], d["y"].rearrange("t p d -> p t d")).then_inc(sg["y_loaded"], DMA)
            sp.wait_ge(sg["y_loaded"], DMA)

        @block.vector
        def _(dve):
            dve.wait_ge(sg["y_loaded"], DMA)
            dve.tensor_tensor(c.x[:], c.x[:], y[:], ALU.add).then_inc(sg["x_added"], 1)
            if biased:
                dve.wait_ge(sg["x_added"], 1)
                dve.tensor_tensor(c.x[:], c.x[:], c.ybias[:].unsqueeze(1).to_broadcast([TP, PAIRS, D]),
                                  ALU.add).then_inc(sg["x_added"], 1)


def stage_store(c):
    nc, d, sg = c.nc, c.dram, c.stage("store")
    with nc.Block() as block:
        @block.sync
        def _(sp):
            c.clear_old(sp)
            sp.dma_start(d["out"].rearrange("(t p) d -> p t d", p=TP), c.x[:]).then_inc(sg["stored"], DMA)
            sp.wait_ge(sg["stored"], DMA)


def stage_own_keys(c, z, zt):
    nc, d, sg = c.nc, c.dram, c.stage("own")
    with nc.Block() as block:
        @block.sync
        def _(sp):
            c.clear_old(sp)
            for j in range(2):
                rows = d["ctx1"][:, SK:SK + S, :].rearrange("(t j) q d -> j q t d", j=2)
                sp.dma_start(rows[j], z[j * S:(j + 1) * S, :, :]).then_inc(sg["stored"], DMA)
            sp.dma_start(d["ctx1T"][:, :, SK:SK + S].rearrange("b p q -> p b q"),
                         zt[:].rearrange("p (b q) -> p b q", q=S)).then_inc(sg["stored"], DMA)
            sp.wait_ge(sg["stored"], 3 * DMA)


def stage_qkv(c, layer, zt, q_t, k_t, v_ext, wo, wo_bias):
    nc, d, sg = c.nc, c.dram, c.stage("qkv")
    ps = c.ps
    with ExitStack() as st:
        sb = alloc(c, st)
        w = {k: sb(k, [D, D]) for k in ("wq", "wk", "wv")}
        bqk = sb("bqk", [D, 2])
        bvo = sb("bvo", [1, 2, D])
        with nc.Block() as block:
            @block.sync
            def _(sp):
                c.clear_old(sp)
                for k in ("wq", "wk", "wv"):
                    sp.dma_start(w[k][:], d[f"f0_{k}"][layer]).then_inc(sg["weights"], DMA)
                sp.dma_start(wo[:], d["f0_wo"][layer]).then_inc(sg["weights"], DMA)
                sp.dma_start(bqk[:], d["f0_bqk"][layer]).then_inc(sg["weights"], DMA)
                sp.dma_start(bvo[:], d["f0_bvo"][layer:layer + 1]).then_inc(sg["weights"], DMA)

            @block.tensor
            def _(pe):
                pe.wait_ge(sg["weights"], 6 * DMA)
                for n, k in enumerate(("wq", "wk")):
                    for a in range(2):
                        last = pe.matmul(ps[:, 2 * n + a, 0:HALF], w[k][:], zt[:, a * HALF:(a + 1) * HALF],
                                         start=True, stop=True)
                    last.then_inc(sg["qk_product"], 1)
                for t in range(PAIRS):
                    out = ps[0:TP, 4 + t // 4, (t % 4) * D:(t % 4 + 1) * D]
                    pe.matmul(out, zt[:, t * TP:(t + 1) * TP], w["wv"][:], start=True, stop=False)
                    last = pe.matmul(out, c.ones[0:1, 0:TP], bvo[:, 0, :], start=False, stop=True)
                last.then_inc(sg["v_product"], 1)
                last = pe.matmul(ps[0:TP, 6, 0:D], c.ones[0:1, 0:TP], bvo[:, 1, :], start=True, stop=True)
                last.then_inc(sg["bo_product"], 1)

            @block.scalar
            def _(act):
                act.wait_ge(sg["weights"], 6 * DMA)
                act.wait_ge(sg["qk_product"], 1)
                act.activation(two(q_t[:]), halves(ps[:, 0:2, :]), ACT.Identity, bias=bqk[:, 0:1]).then_inc(sg["q_ready"], 1)
                act.wait_ge(sg["qk_product"], 2)
                act.activation(two(k_t[:]), halves(ps[:, 2:4, :]), ACT.Identity, bias=bqk[:, 1:2]).then_inc(sg["k_ready"], 1)

            @block.vector
            def _(dve):
                dve.memset(v_ext[:, :, :, 8:9], 1.0)
                dve.wait_ge(sg["v_product"], 1)
                for a in range(2):
                    dve.tensor_copy(v_ext[:, 4 * a:4 * a + 4, :, 0:8],
                                    ps[0:TP, 4 + a, :].rearrange("p (t h e) -> p t h e", t=4, h=H)).then_inc(sg["v_ready"], 1)
                dve.wait_ge(sg["bo_product"], 1)
                dve.tensor_copy(wo_bias[:], ps[0:TP, 6, 0:D]).then_inc(sg["bo_ready"], 1)


def stage_self_attention(c, r, q_t, k_t, v_ext, wo, wo_bias):
    nc, d, sg = c.nc, c.dram, c.stage("self")
    ps = c.ps
    S_BANK, T_BANK, O_BANK, Y_BANK = 0, 4, 6, 7
    G = 4
    with ExitStack() as st:
        sb = alloc(c, st)
        head_of = sb("head_of", [D, H])
        causal = sb("causal", [TP, TP])
        k_wide = sb("k_wide", [D, H, TP])
        q_now = sb("q_now", [D, TP])
        sc = sb("sc", [TP, H, TP])
        mx = sb("mx", [TP, H])
        probs = sb("probs", [TP, H, TP])
        p_t = [sb(f"p_t{g}", [TP, H // G, TP]) for g in range(G)]
        rs = sb("rs", [TP, H])
        o = sb("o", [TP, H, 8])
        o_t = sb("o_t", [D, TP])

        def emit(run, before, step, after):
            before()
            step(0, True, False)
            with run.Fori(1, PAIRS - 1) as i:
                step(i, False, False)
            step(PAIRS - 1, False, True)
            after()

        with nc.Block() as block:
            @block.sync
            def _(sp):
                c.clear_old(sp)
                sp.dma_start(head_of[:], d["head_of"]).then_inc(sg["masks"], DMA)
                sp.dma_start(causal[:], d["causal"]).then_inc(sg["masks"], DMA)

            @block.gpsimd
            def _(pool):
                pool.wait_ge(sg["masks"], 2 * DMA)
                pool.sem_inc(sg["scores_or_start"], 1)
                with pool.Fori(0, PAIRS) as i:
                    pool.wait_ge(sg["scores_or_start"], i + 1)
                    pool.tensor_tensor(k_wide[:], k_t[:, bass.ts(i, TP)].unsqueeze(1).to_broadcast([D, H, TP]),
                                       head_of[:].unsqueeze(2).to_broadcast([D, H, TP]), ALU.mult).then_inc(
                        sg["k_wide_made"], 1)

            @block.tensor
            def _(pe):
                def scores(n):
                    pe.wait_ge(sg["k_wide_made"], n)
                    pe.wait_ge(sg["q_now"], n)
                    if not (isinstance(n, int) and n == 1):
                        pe.wait_ge(sg["masked"], n - 1)
                    for a in range(4):
                        last = pe.matmul(ps[0:TP, S_BANK + a, 0:HALF], q_now[:], k_wide[:, 4 * a:4 * a + 4, :],
                                         start=True, stop=True)
                    last.then_inc(sg["scores_or_start"], 1)

                def weigh(i, g):
                    pe.wait_ge(sg["p_t_ready"], i * G + (g + 1))
                    for h in range(H // G * g, H // G * (g + 1)):
                        last = pe.matmul(ps[0:TP, O_BANK, h * 16:h * 16 + 9], p_t[g][:, h % (H // G), :],
                                         v_ext[:, bass.ts(i, 1), h, :], start=True, stop=True)
                    if g == G - 1:
                        last.then_inc(sg["o_product"], 1)

                def turn_o(n):
                    pe.wait_ge(sg["o_ready"], n)
                    pe.wait_ge(sg["y_added_or_start"], n)
                    pe.transpose(ps[:, Y_BANK, 0:TP], o[:].rearrange("p h e -> p (h e)"),
                                 c.ident[0:TP, 0:TP]).then_inc(sg["o_turned"], 1)

                def project(n):
                    pe.wait_ge(sg["o_t_ready"], n)
                    pe.matmul(ps[0:TP, Y_BANK, D:2 * D], o_t[:], wo[:], start=True, stop=True).then_inc(
                        sg["y_product"], 1)

                def step(i, first, final):
                    if not final:
                        scores(i + 2)
                    pe.wait_ge(sg["exp_done"], i + 1)
                    for g in range(G):
                        if not (first and g < 2):
                            pe.wait_ge(sg["p_t_ready"], i * G + (g - 1))
                        for h in range(H // G):
                            last = pe.transpose(ps[0:TP, T_BANK + g % 2, h * TP:(h + 1) * TP],
                                                probs[:, H // G * g + h, :], c.ident[0:TP, 0:TP])
                        last.then_inc(sg["turned"], 1)
                        if g == 0 and not first:
                            turn_o(i)
                        if g == 2 and not first:
                            project(i)
                        if g >= 1:
                            weigh(i, g - 1)
                    weigh(i, G - 1)

                def after():
                    turn_o(PAIRS)
                    project(PAIRS)

                emit(pe, lambda: scores(1), step, after)

            @block.scalar
            def _(act):
                def copy_o(n):
                    act.wait_ge(sg["o_turned"], n)
                    act.activation(o_t[:], ps[:, Y_BANK, 0:TP], ACT.Copy).then_inc(sg["o_t_ready"], 1)

                def before():
                    act.activation(q_now[:], q_t[:, 0:TP], ACT.Copy).then_inc(sg["q_now"], 1)

                def step(i, first, final):
                    if not final:
                        act.wait_ge(sg["scores_or_start"], i + 2)
                        act.activation(q_now[:], q_t[:, bass.ts(i + 1, TP)], ACT.Copy).then_inc(sg["q_now"], 1)
                    act.wait_ge(sg["less_max"], i + 1)
                    if not first:
                        act.wait_ge(sg["turned"], i * G)
                    act.activation(probs[:], sc[:], ACT.Exp).then_inc(sg["exp_done"], 1)
                    for g in range(G):
                        act.wait_ge(sg["turned"], i * G + (g + 1))
                        if g == 0 and not first:
                            act.wait_ge(sg["o_product"], i)
                        act.activation(p_t[g][:].rearrange("p h q -> p (h q)"), ps[0:TP, T_BANK + g % 2, 0:HALF],
                                       ACT.Copy).then_inc(sg["p_t_ready"], 1)
                        if g == 1 and not first:
                            copy_o(i)

                emit(act, before, step, lambda: copy_o(PAIRS))

            @block.vector
            def _(dve):
                def mask(n):
                    dve.wait_ge(sg["scores_or_start"], n + 1)
                    if not (isinstance(n, int) and n == 1):
                        dve.wait_ge(sg["exp_done"], n - 1)
                    for a in range(4):
                        last = dve.scalar_tensor_tensor(
                            sc[:, 4 * a:4 * a + 4, :],
                            ps[0:TP, S_BANK + a, 0:HALF].rearrange("p (h q) -> p h q", q=TP), 8 ** -0.5,
                            causal[:].unsqueeze(1).to_broadcast([TP, 4, TP]), ALU.mult, ALU.add)
                    last.then_inc(sg["masked"], 1)
                    dve.wait_ge(sg["masked"], n)
                    dve.tensor_reduce(mx[:], sc[:], X, ALU.max).then_inc(sg["mx"], 1)
                    dve.wait_ge(sg["mx"], n)
                    dve.tensor_tensor(sc[:], sc[:], mx[:].unsqueeze(2).to_broadcast([TP, H, TP]),
                                      ALU.subtract).then_inc(sg["less_max"], 1)

                def divide(n):
                    dve.wait_ge(sg["o_product"], n)
                    o_ps = ps[0:TP, O_BANK, 0:256].rearrange("p (h e) -> p h e", h=H)
                    dve.reciprocal(rs[:].unsqueeze(2), o_ps[:, :, 8:9]).then_inc(sg["rs"], 1)
                    dve.wait_ge(sg["rs"], n)
                    dve.tensor_tensor(o[:], o_ps[:, :, 0:8], rs[:].unsqueeze(2).to_broadcast([TP, H, 8]),
                                      ALU.mult).then_inc(sg["o_ready"], 1)

                def add_y(n, i):
                    dve.wait_ge(sg["y_product"], n)
                    rt = r[:, bass.ts(i, 1), :]
                    dve.tensor_tensor(rt, rt, ps[0:TP, Y_BANK:Y_BANK + 1, D:2 * D], ALU.add).then_inc(
                        sg["y_added_or_start"], 1)

                def before():
                    dve.wait_ge(sg["masks"], 2 * DMA)
                    dve.tensor_tensor(r[:], r[:], wo_bias[:].unsqueeze(1).to_broadcast([TP, PAIRS, D]),
                                      ALU.add).then_inc(sg["y_added_or_start"], 1)
                    mask(1)

                def step(i, first, final):
                    if not first:
                        divide(i)
                    if not final:
                        mask(i + 2)
                    if not first:
                        add_y(i, i - 1)

                def after():
                    divide(PAIRS)
                    add_y(PAIRS, PAIRS - 1)

                emit(dve, before, step, after)


def stage_top2(c, ht, gate_w, gate_b, cw, of_batch_mean):
    nc, d, sg = c.nc, c.dram, c.stage("top2")
    ps = c.ps
    with ExitStack() as st:
        sb = alloc(c, st)
        gw = sb("gw", [D, E])
        gb = sb("gb", [1, E])
        earlier = sb("earlier", [TP, E, E])
        sums = sb("sums", [D, B])
        mean = sb("mean", [D, TOK])
        lg = sb("lg", [TP, PAIRS, E])
        gt = sb("gt", [TP, PAIRS, E, E])
        eq = sb("eq", [TP, PAIRS, E, E])
        rank = sb("rank", [TP, PAIRS, E])
        mx = sb("mx", [TP, PAIRS])
        ex = sb("ex", [TP, PAIRS, E])
        tot = sb("tot", [TP, PAIRS])
        src = mean if of_batch_mean else ht
        with nc.Block() as block:
            @block.sync
            def _(sp):
                c.clear_old(sp)
                sp.dma_start(gw[:], gate_w).then_inc(sg["weights"], DMA)
                sp.dma_start(gb[:], gate_b).then_inc(sg["weights"], DMA)
                sp.dma_start(earlier[:], d["earlier"]).then_inc(sg["weights"], DMA)

            @block.tensor
            def _(pe):
                pe.wait_ge(sg["weights"], 3 * DMA)
                if of_batch_mean:
                    pe.wait_ge(sg["mean_ready"], 1)
                for t in range(PAIRS):
                    out = ps[0:TP, 0, t * E:(t + 1) * E]
                    pe.matmul(out, src[:, t * TP:(t + 1) * TP], gw[:], start=True, stop=False)
                    last = pe.matmul(out, c.ones[0:1, 0:TP], gb[:], start=False, stop=True)
                last.then_inc(sg["logits"], 1)

            @block.scalar
            def _(act):
                act.wait_ge(sg["less_max"], 1)
                act.activation(ex[:], ex[:], ACT.Exp).then_inc(sg["exp_done"], 1)

            @block.vector
            def _(dve):
                link = Link(dve, sg["dve_chain"])
                if of_batch_mean:
                    link(dve.tensor_reduce(sums[:], ht[:].rearrange("p (b q) -> p b q", q=S), X, ALU.add))
                    dve.tensor_scalar(mean[:].rearrange("p (b q) -> p b q", q=S),
                                      sums[:].unsqueeze(2).to_broadcast([D, B, S]), 1.0 / S, None,
                                      ALU.mult).then_inc(sg["mean_ready"], 1)
                dve.wait_ge(sg["weights"], 3 * DMA)
                dve.wait_ge(sg["logits"], 1)
                link(dve.tensor_copy(lg[:], ps[0:TP, 0, 0:PAIRS * E].rearrange("p (t e) -> p t e", e=E)))
                other = lg[:].unsqueeze(2).to_broadcast([TP, PAIRS, E, E])
                mine = lg[:].unsqueeze(3).to_broadcast([TP, PAIRS, E, E])
                link(dve.tensor_reduce(mx[:], lg[:], X, ALU.max))
                dve.tensor_tensor(ex[:], lg[:], mx[:].unsqueeze(2).to_broadcast([TP, PAIRS, E]), ALU.subtract).then_inc(
                    sg["less_max"], 1)
                link(dve.tensor_tensor(gt[:], other, mine, ALU.is_gt))
                link(dve.tensor_tensor(eq[:], other, mine, ALU.is_equal))
                link(dve.tensor_tensor(eq[:], eq[:], earlier[:].unsqueeze(1).to_broadcast([TP, PAIRS, E, E]), ALU.mult))
                link(dve.tensor_tensor(gt[:], gt[:], eq[:], ALU.add))
                link(dve.tensor_reduce(rank[:], gt[:], X, ALU.add))
                dve.wait_ge(sg["exp_done"], 1)
                link(dve.scalar_tensor_tensor(ex[:], rank[:], 2.0, ex[:], ALU.is_lt, ALU.mult))
                link(dve.tensor_reduce(tot[:], ex[:], X, ALU.add))
                link(dve.reciprocal(tot[:], tot[:]))
                dve.tensor_tensor(cw[:].rearrange("p e t -> p t e"), ex[:],
                                  tot[:].unsqueeze(2).to_broadcast([TP, PAIRS, E]), ALU.mult).then_inc(sg["cw_ready"], 1)


def stage_capacity(c, zt, cw):
    nc, d, sg = c.nc, c.dram, c.stage("cap")
    ps = c.ps
    with ExitStack() as st:
        sb = alloc(c, st)
        gw = sb("gw", [D, E])
        same = sb("same", [TP, TP])
        before = sb("before", [TP, TP])
        pr = sb("pr", [TP, PAIRS, E])
        mx = sb("mx", [TP, PAIRS])
        tot = sb("tot", [TP, PAIRS])
        diag = sb("diag", [TP, 2, E, TP])
        gt = sb("gt", [TP, E, TP])
        eq = sb("eq", [TP, E, TP])
        rank = sb("rank", [TP, PAIRS, E])

        def over_t(ap):
            return ap.unsqueeze(1).to_broadcast([TP, E, TP])

        with nc.Block() as block:
            @block.sync
            def _(sp):
                c.clear_old(sp)
                sp.dma_start(gw[:], d["f2_gate_w"]).then_inc(sg["weights"], DMA)
                sp.dma_start(same[:], d["same"]).then_inc(sg["weights"], DMA)
                sp.dma_start(before[:], d["before"]).then_inc(sg["weights"], DMA)

            @block.tensor
            def _(pe):
                pe.wait_ge(sg["weights"], 3 * DMA)
                for t in range(PAIRS):
                    last = pe.matmul(ps[0:TP, 0, t * E:(t + 1) * E], zt[:, t * TP:(t + 1) * TP], gw[:],
                                     start=True, stop=True)
                last.then_inc(sg["scores"], 1)
                with pe.Fori(0, PAIRS // 2) as i:
                    for j in range(2):
                        pe.wait_ge(sg["diag_made"], i * 2 + (j + 1))
                        for a in range(2):
                            last = pe.matmul(ps[0:TP, 2 + 2 * j + a, 0:HALF], c.ones[0:TP, 0:TP],
                                             diag[:, j, 4 * a:4 * a + 4, :], start=True, stop=True)
                        last.then_inc(sg["spread"], 1)

            @block.scalar
            def _(act):
                act.wait_ge(sg["less_max"], 1)
                act.activation(pr[:], pr[:], ACT.Exp).then_inc(sg["exp_done"], 1)

            @block.vector
            def _(dve):
                link = Link(dve, sg["dve_chain"])
                dve.wait_ge(sg["weights"], 3 * DMA)
                dve.wait_ge(sg["scores"], 1)
                scores = ps[0:TP, 0, 0:PAIRS * E].rearrange("p (t e) -> p t e", e=E)
                link(dve.tensor_reduce(mx[:], scores, X, ALU.max))
                dve.tensor_tensor(pr[:], scores, mx[:].unsqueeze(2).to_broadcast([TP, PAIRS, E]), ALU.subtract).then_inc(
                    sg["less_max"], 1)
                dve.wait_ge(sg["exp_done"], 1)
                link(dve.tensor_reduce(tot[:], pr[:], X, ALU.add))
                link(dve.reciprocal(tot[:], tot[:]))
                link(dve.tensor_tensor(pr[:], pr[:], tot[:].unsqueeze(2).to_broadcast([TP, PAIRS, E]), ALU.mult))
                with dve.Fori(0, PAIRS // 2) as i:
                    for j in range(2):
                        mine = pr[:, i * 2 + j, :].unsqueeze(2).to_broadcast([TP, E, TP])
                        dve.tensor_tensor(diag[:, j, :, :], over_t(c.ident[0:TP, 0:TP]), mine, ALU.mult).then_inc(
                            sg["diag_made"], 1)
                        dve.wait_ge(sg["spread"], i * 2 + (j + 1))
                        theirs = ps[0:TP, 2 + 2 * j:4 + 2 * j, 0:HALF].rearrange("p a (e t) -> p a e t", t=TP)
                        mine4 = pr[:, i * 2 + j, :].rearrange("p (a e) -> p a e", a=2).unsqueeze(3).to_broadcast([TP, 2, E // 2, TP])
                        gt4 = gt[:].rearrange("p (a e) t -> p a e t", a=2)
                        eq4 = eq[:].rearrange("p (a e) t -> p a e t", a=2)
                        dve.tensor_tensor(gt4, theirs, mine4, ALU.is_gt)
                        dve.tensor_tensor(eq4, theirs, mine4, ALU.is_equal).then_inc(sg["compared"], 1)
                        dve.wait_ge(sg["compared"], i * 2 + (j + 1))
                        dve.tensor_tensor(gt[:], gt[:], over_t(same[:]), ALU.mult)
                        dve.tensor_tensor(eq[:], eq[:], over_t(before[:]), ALU.mult).then_inc(sg["kept"], 1)
                        dve.wait_ge(sg["kept"], i * 2 + (j + 1))
                        dve.tensor_tensor(gt[:], gt[:], eq[:], ALU.add).then_inc(sg["before_me"], 1)
                        dve.wait_ge(sg["before_me"], i * 2 + (j + 1))
                        dve.tensor_reduce(rank[:, i * 2 + j, :], gt[:], X, ALU.add).then_inc(sg["rank"], 1)
                dve.wait_ge(sg["rank"], PAIRS)
                dve.scalar_tensor_tensor(cw[:].rearrange("p e t -> p t e"), rank[:], float(CAP), pr[:], ALU.is_lt,
                                         ALU.mult).then_inc(sg["cw_ready"], 1)


def stage_experts(c, ht, acc, cw, w1, w2, b1=None, b2=None):
    nc, d, sg = c.nc, c.dram, c.stage("experts")
    ps = c.ps
    F = DFF // 128
    with ExitStack() as st:
        sb = alloc(c, st)
        w1s = [sb(f"w1_{j}", [D, DFF]) for j in range(2)]
        w2s = [sb(f"w2_{j}", [128, F, D]) for j in range(2)]
        g = sb("g", [128, 2, F, TOK])
        if b1 is not None:
            b1s = sb("b1", [128, E, F])
            b2s = sb("b2", [E, D])
            cw_t = sb("cw_t", [E, PAIRS, TP])
        UP, DOWN = 0, 4

        def emit(run, before, step):
            before()
            with run.Fori(0, E // 2 - 1) as i:
                for j in range(2):
                    step(i, j, True, True)
            for j in range(2):
                step(E // 2 - 1, j, False, j == 0)

        with nc.Block() as block:
            @block.sync
            def _(sp):
                c.clear_old(sp)

                def before():
                    if b1 is not None:
                        sp.dma_start(b1s[:], b1).then_inc(sg["biases"], DMA)
                        sp.dma_start(b2s[:], b2).then_inc(sg["biases"], DMA)
                    for j in range(2):
                        sp.dma_start(w1s[j][:], w1[:, j, :]).then_inc(sg[f"w1_{j}"], DMA)
                        sp.dma_start(w2s[j][:], w2[:, j, :, :]).then_inc(sg[f"w2_{j}"], DMA)

                def step(i, j, two_more, one_more):
                    if two_more:
                        sp.wait_ge(sg["up_full"], i * 8 + 4 * (j + 1))
                        sp.dma_start(w1s[j][:], w1[:, i * 2 + (j + 2), :]).then_inc(sg[f"w1_{j}"], DMA)
                        sp.wait_ge(sg["down_full"], i * 2 + (j + 3))
                        sp.dma_start(w2s[j][:], w2[:, i * 2 + (j + 2), :, :]).then_inc(sg[f"w2_{j}"], DMA)

                emit(sp, before, step)

            @block.tensor
            def _(pe):
                def up(i, j):
                    pe.wait_ge(sg[f"w1_{j}"], i * DMA + DMA)
                    for f in range(F):
                        bank = UP + 2 * (f % 2)
                        pe.wait_ge(sg["gelu_done"], i * 8 + (4 * j + f + 1))
                        for a in range(2):
                            last = pe.matmul(ps[:, bank + a, 0:HALF], w1s[j][:, f * 128:(f + 1) * 128],
                                             ht[:, a * HALF:(a + 1) * HALF], start=True, stop=True)
                        last.then_inc(sg["up_full"], 1)

                def down(i, j):
                    pe.wait_ge(sg[f"w2_{j}"], i * DMA + DMA)
                    pe.wait_ge(sg["combined"], i * 2 + (j + 1))
                    pe.wait_ge(sg["gelu_done"], i * 8 + (4 * (j + 1) + 2))
                    for t in range(PAIRS):
                        for f in range(F):
                            last = pe.matmul(ps[0:TP, DOWN + 2 * j + t // 4, (t % 4) * D:(t % 4 + 1) * D],
                                             g[:, j, f, t * TP:(t + 1) * TP], w2s[j][:, f, :],
                                             start=(f == 0), stop=(f == F - 1))
                    last.then_inc(sg["down_full"], 1)

                def before():
                    pe.sem_inc(sg["gelu_done"], 2)
                    pe.sem_inc(sg["combined"], 2)
                    pe.sem_inc(sg["down_full"], 2)
                    if b1 is not None:
                        for t in range(PAIRS):
                            last = pe.transpose(ps[0:E, t // 4, (t % 4) * TP:(t % 4 + 1) * TP], cw[:, :, t],
                                                c.ident[0:TP, 0:TP])
                        last.then_inc(sg["cw_turned"], 1)
                        pe.wait_ge(sg["cw_t_ready"], 1)
                        pe.wait_ge(sg["biases"], 2 * DMA)
                        for t in range(PAIRS):
                            last = pe.matmul(ps[0:TP, 2 + t // 4, (t % 4) * D:(t % 4 + 1) * D], cw_t[:, t, :], b2s[:],
                                             start=True, stop=True)
                        last.then_inc(sg["b2_product"], 1)
                        pe.wait_ge(sg["b2_added"], 1)
                    up(0, 0)

                def step(i, j, two_more, one_more):
                    if one_more:
                        up(i + j, 1 - j)
                    down(i, j)

                emit(pe, before, step)

            @block.scalar
            def _(act):
                def before():
                    if b1 is not None:
                        act.wait_ge(sg["biases"], 2 * DMA)

                def step(i, j, two_more, one_more):
                    act.wait_ge(sg["down_full"], i * 2 + (j + 1))
                    for f in range(F):
                        act.wait_ge(sg["up_full"], i * 8 + (4 * j + f + 1))
                        src = halves(ps[:, UP + 2 * (f % 2):UP + 2 * (f % 2) + 2, :])
                        bias = b1s[:, i * 2 + j, f:f + 1] if b1 is not None else 0.0
                        act.activation(two(g[:, j, f, :]), src, ACT.Gelu, bias=bias).then_inc(sg["gelu_done"], 1)

                emit(act, before, step)

            @block.vector
            def _(dve):
                def before():
                    if b1 is not None:
                        dve.wait_ge(sg["cw_turned"], 1)
                        dve.tensor_copy(cw_t[:].rearrange("e (a t) q -> e a (t q)", a=2), ps[0:E, 0:2, 0:HALF]).then_inc(
                            sg["cw_t_ready"], 1)
                        dve.wait_ge(sg["b2_product"], 1)
                        dve.tensor_tensor(acc[:].rearrange("p (a t) d -> p a (t d)", a=2),
                                          acc[:].rearrange("p (a t) d -> p a (t d)", a=2), ps[0:TP, 2:4, :],
                                          ALU.add).then_inc(sg["b2_added"], 1)
                        dve.wait_ge(sg["b2_added"], 1)

                def step(i, j, two_more, one_more):
                    dve.wait_ge(sg["down_full"], i * 2 + (j + 3))
                    dve.wait_ge(sg["combined"], i * 2 + (j + 2))
                    for t in range(PAIRS):
                        last = dve.scalar_tensor_tensor(
                            acc[:, t, :], ps[0:TP, DOWN + 2 * j + t // 4, (t % 4) * D:(t % 4 + 1) * D],
                            cw[:, i * 2 + j, t:t + 1], acc[:, t, :], ALU.mult, ALU.add)
                    last.then_inc(sg["combined"], 1)

                emit(dve, before, step)


def stage_add(c, dst, src):
    nc, sg = c.nc, c.stage("add")
    with nc.Block() as block:
        @block.sync
        def _(sp):
            c.clear_old(sp)

        @block.vector
        def _(dve):
            dve.tensor_tensor(dst[:], dst[:], src[:], ALU.add).then_inc(sg["added"], 1)


def layer0_ffn(c):
    d = c.dram
    with ExitStack() as st:
        sb = alloc(c, st)
        r = sb("r", [TP, PAIRS, D])
        z = sb("z", [TP, PAIRS, D])
        zt = sb("zt", [D, TOK])
        cw = sb("cw", [TP, E, PAIRS])
        stage_norm(c, c.x, r)
        for layer in range(2):
            stage_norm(c, r, z, zt, affine=(d["ln1_w"][layer], d["ln1_b"][layer]))
            with ExitStack() as inner:
                sb = alloc(c, inner)
                q_t, k_t = sb("q_t", [D, TOK]), sb("k_t", [D, TOK])
                v_ext = sb("v_ext", [TP, PAIRS, H, 9])
                wo, wo_bias = sb("wo", [D, D]), sb("wo_bias", [TP, D])
                stage_qkv(c, layer, zt, q_t, k_t, v_ext, wo, wo_bias)
                stage_self_attention(c, r, q_t, k_t, v_ext, wo, wo_bias)
            stage_norm(c, r, z, zt, affine=(d["ln2_w"][layer], d["ln2_b"][layer]))
            stage_top2(c, zt, d["f0_gate_w"][layer], d["f0_gate_b"][layer], cw, of_batch_mean=(layer == 1))
            stage_experts(c, zt, r, cw, d["f0_w1"][layer], d["f0_w2"][layer], d["f0_b1"][layer], d["f0_b2"][layer])
        stage_add(c, c.x, r)


def layer1_ffn(c):
    with ExitStack() as st:
        sb = alloc(c, st)
        z = sb("z", [TP, PAIRS, D])
        zt = sb("zt", [D, TOK])
        stage_norm(c, c.x, z, zt)
        nc, d, sg = c.nc, c.dram, c.stage("ternary")
        ps = c.ps
        F = 4
        w = [sb(f"w{n}", [128, 512]) for n in range(2)]
        t0 = [sb(f"t{n}", [128, 512]) for n in range(2)]
        b1 = sb("b1", [128, F])
        b2 = sb("b2", [1, D])
        mag = sb("mag", [128, 2])
        thr = sb("thr", [128, 2, 2])
        g = sb("g", [128, F, TOK])
        with nc.Block() as block:
            @block.sync
            def _(sp):
                c.clear_old(sp)
                sp.dma_start(w[0][:], d["f1_w1T"]).then_inc(sg["weights"], DMA)
                sp.dma_start(w[1][:], d["f1_w2T"].rearrange("p f d -> p (f d)")).then_inc(sg["weights"], DMA)
                sp.dma_start(b1[:], d["f1_b1"]).then_inc(sg["weights"], DMA)
                sp.dma_start(b2[:], d["f1_b2"]).then_inc(sg["weights"], DMA)

            @block.vector
            def _(dve):
                link = Link(dve, sg["dve_chain"])
                dve.wait_ge(sg["weights"], 4 * DMA)
                for n in range(2):
                    last = dve.tensor_reduce(mag[:, n:n + 1], w[n][:], X, ALU.add, apply_absolute_value=True)
                last.then_inc(sg["magnitudes"], 1)
                dve.wait_ge(sg["magnitudes_summed"], 1)
                link(dve.tensor_scalar(thr[:, 0, :], ps[:, 0, 0:2], 1.0 / (128 * 512), 1e-8, ALU.mult, ALU.max))
                link(dve.tensor_scalar(thr[:, 0, :], thr[:, 0, :], 0.5, None, ALU.mult))
                link(dve.tensor_scalar(thr[:, 1, :], thr[:, 0, :], -1.0, None, ALU.mult))
                for n in range(2):
                    link(dve.tensor_scalar(t0[n][:], w[n][:], thr[:, 1, n:n + 1], None, ALU.is_lt))
                    link(dve.scalar_tensor_tensor(t0[n][:], w[n][:], thr[:, 0, n:n + 1], t0[n][:], ALU.is_gt, ALU.subtract))
                    link(dve.tensor_tensor(t0[n][:], t0[n][:], w[n][:], ALU.subtract))
                    link(dve.tensor_tensor(w[n][:], w[n][:], t0[n][:], ALU.add))
                dve.engine_nop().then_inc(sg["ternary_made"], 1)
                dve.wait_ge(sg["y_product"], 1)
                x2 = c.x[:].rearrange("p (a t) d -> p a (t d)", a=2)
                dve.tensor_tensor(x2, x2, ps[0:TP, 6:8, :], ALU.add).then_inc(sg["x_added"], 1)

            @block.tensor
            def _(pe):
                pe.wait_ge(sg["magnitudes"], 1)
                pe.matmul(ps[:, 0, 0:2], c.ones[:], mag[:], start=True, stop=True).then_inc(sg["magnitudes_summed"], 1)
                pe.wait_ge(sg["ternary_made"], 1)
                for f in range(F):
                    bank = 2 * (f % 3)
                    if f >= 3:
                        pe.wait_ge(sg["gelu_done"], f - 2)
                    for a in range(2):
                        last = pe.matmul(ps[:, bank + a, 0:HALF], w[0][:, f * 128:(f + 1) * 128],
                                         zt[:, a * HALF:(a + 1) * HALF], start=True, stop=True)
                    last.then_inc(sg["up_full"], 1)
                pe.wait_ge(sg["gelu_done"], F)
                for t in range(PAIRS):
                    out = ps[0:TP, 6 + t // 4, (t % 4) * D:(t % 4 + 1) * D]
                    for f in range(F):
                        pe.matmul(out, g[:, f, t * TP:(t + 1) * TP], w[1][:, f * D:(f + 1) * D],
                                  start=(f == 0), stop=False)
                    last = pe.matmul(out, c.ones[0:1, 0:TP], b2[:], start=False, stop=True)
                last.then_inc(sg["y_product"], 1)

            @block.scalar
            def _(act):
                act.wait_ge(sg["weights"], 4 * DMA)
                for f in range(F):
                    act.wait_ge(sg["up_full"], f + 1)
                    bank = 2 * (f % 3)
                    act.activation(two(g[:, f, :]), halves(ps[:, bank:bank + 2, :]), ACT.Gelu,
                                   bias=b1[:, f:f + 1]).then_inc(sg["gelu_done"], 1)


def layer2_attention(c):
    with ExitStack() as st:
        sb = alloc(c, st)
        z = sb("z", [TP, PAIRS, D])
        zt = sb("zt", [D, TOK])
        stage_norm(c, c.x, z, zt)
        nc, d, sg = c.nc, c.dram, c.stage("a2")
        ps = c.ps
        k_rows = sb("k_rows", [TP, PAIRS, D])
        k_cols = sb("k_cols", [D, TOK])
        causal = sb("causal", [TP, TP])
        sc = sb("sc", [TP, PAIRS, TP])
        mx = sb("mx", [TP, PAIRS])
        tot = sb("tot", [TP, PAIRS])
        p_t = sb("p_t", [TP, PAIRS, TP])

        def slot(bank, t, n=TP):
            return ps[0:TP, bank + t // 4, (t % 4) * n:(t % 4 + 1) * n]

        with nc.Block() as block:
            @block.sync
            def _(sp):
                c.clear_old(sp)
                sp.dma_start(k_rows[:], d["own_rows"]).then_inc(sg["loaded"], DMA)
                sp.dma_start(k_cols[:], d["own_cols"]).then_inc(sg["loaded"], DMA)
                sp.dma_start(causal[:], d["causal"]).then_inc(sg["loaded"], DMA)

            @block.tensor
            def _(pe):
                pe.wait_ge(sg["loaded"], 3 * DMA)
                for t in range(PAIRS):
                    last = pe.matmul(slot(0, t), zt[:, t * TP:(t + 1) * TP], k_cols[:, t * TP:(t + 1) * TP],
                                     start=True, stop=True)
                last.then_inc(sg["scores"], 1)
                pe.wait_ge(sg["p_ready"], 1)
                for t in range(PAIRS):
                    last = pe.transpose(slot(2, t), sc[:, t, :], c.ident[0:TP, 0:TP])
                last.then_inc(sg["p_turned"], 1)
                pe.wait_ge(sg["p_t_ready"], 1)
                for t in range(PAIRS):
                    last = pe.matmul(slot(4, t, D), p_t[:, t, :], k_rows[:, t, :], start=True, stop=True)
                last.then_inc(sg["y_product"], 1)

            @block.scalar
            def _(act):
                act.wait_ge(sg["less_max"], 1)
                act.activation(sc[:], sc[:], ACT.Exp).then_inc(sg["exp_done"], 1)
                act.wait_ge(sg["p_turned"], 1)
                act.activation(p_t[:].rearrange("p (a t) k -> p a (t k)", a=2), ps[0:TP, 2:4, 0:HALF], ACT.Copy).then_inc(
                    sg["p_t_ready"], 1)

            @block.vector
            def _(dve):
                link = Link(dve, sg["dve_chain"])
                dve.wait_ge(sg["loaded"], 3 * DMA)
                dve.wait_ge(sg["scores"], 1)
                for a in range(2):
                    last = dve.scalar_tensor_tensor(
                        sc[:, 4 * a:4 * a + 4, :], ps[0:TP, a, 0:HALF].rearrange("p (t k) -> p t k", k=TP), D ** -0.5,
                        causal[:].unsqueeze(1).to_broadcast([TP, 4, TP]), ALU.mult, ALU.add)
                link(last)
                link(dve.tensor_reduce(mx[:], sc[:], X, ALU.max))
                dve.tensor_tensor(sc[:], sc[:], mx[:].unsqueeze(2).to_broadcast([TP, PAIRS, TP]), ALU.subtract).then_inc(
                    sg["less_max"], 1)
                dve.wait_ge(sg["exp_done"], 1)
                link(dve.tensor_reduce(tot[:], sc[:], X, ALU.add))
                link(dve.reciprocal(tot[:], tot[:]))
                dve.tensor_tensor(sc[:], sc[:], tot[:].unsqueeze(2).to_broadcast([TP, PAIRS, TP]), ALU.mult).then_inc(
                    sg["p_ready"], 1)
                dve.wait_ge(sg["y_product"], 1)
                x2 = c.x[:].rearrange("p (a t) d -> p a (t d)", a=2)
                dve.tensor_tensor(x2, x2, ps[0:TP, 4:6, :], ALU.add).then_inc(sg["x_added"], 1)


def layer2_ffn(c):
    d = c.dram
    with ExitStack() as st:
        sb = alloc(c, st)
        z = sb("z", [TP, PAIRS, D])
        zt = sb("zt", [D, TOK])
        cw = sb("cw", [TP, E, PAIRS])
        stage_norm(c, c.x, z, zt)
        stage_capacity(c, zt, cw)
        stage_experts(c, zt, c.x, cw, d["f2_w1"], d["f2_w2"])


def stage_mask(c):
    nc, d, sg = c.nc, c.dram, c.stage("mask")
    with ExitStack() as st:
        sb = alloc(c, st)
        m = sb("m", [B, SK])
        hi = sb("hi", [B, SK], F32R)
        lo = sb("lo", [B, SK], F32R)
        with nc.Block() as block:
            @block.sync
            def _(sp):
                c.clear_old(sp)
                sp.dma_start(m[:], d["mask"]).then_inc(sg["loaded"], DMA)
                sp.wait_ge(sg["low"], 1)
                sp.dma_start(d["mask_parts"][:, 0, :], hi[:].bitcast(F32)).then_inc(sg["stored"], DMA)
                sp.dma_start(d["mask_parts"][:, 1, :], lo[:].bitcast(F32)).then_inc(sg["stored"], DMA)
                sp.wait_ge(sg["stored"], 2 * DMA)

            @block.vector
            def _(dve):
                dve.wait_ge(sg["loaded"], DMA)
                dve.tensor_copy(hi[:], m[:]).then_inc(sg["high"], 1)
                dve.wait_ge(sg["high"], 1)
                dve.tensor_tensor(lo[:], m[:], hi[:].bitcast(F32), ALU.subtract).then_inc(sg["low"], 1)


TINY = 1.17549435e-38
ERFC = [-1.26551223, 1.00002368, 0.37409196, 0.09678418, -0.18628806, 0.27886807, -1.13520398, 1.48851587,
        -0.82215223, 0.17087277]


def layer3_ffn(c):
    with ExitStack() as st:
        sb = alloc(c, st)
        z = sb("z", [TP, PAIRS, D])
        stage_norm(c, c.x, z)
        nc, d, sg = c.nc, c.dram, c.stage("tree")
        W = PAIRS * TREE_P
        LEVELS = DEPTH + 1
        IN, BIAS, OUT = 0, FAN * D, FAN * D + FAN
        ROW = OUT + FAN * D
        WEIGHED = 4
        SEEN = 4
        node = sb("node", [TP, PAIRS, TREE_P])
        index = sb("index", [TP, PAIRS, TREE_P], U32)
        platform = sb("platform", [TP, PAIRS, TREE_P])
        fan_less = sb("fan_less", [TP, W, FAN])
        row = sb("row", [TP, W, ROW])
        prod = sb("prod", [TP, 2, FAN, D])
        weighed = [sb(f"weighed{n}", [TP, FAN, D]) for n in range(WEIGHED)]
        logit = sb("logit", [TP, W, FAN])
        gel = sb("gel", [TP, W, FAN])
        mag, frac, poly, half_sq = (sb(k, [TP, W, FAN]) for k in ("mag", "frac", "poly", "half_sq"))
        best = sb("best", [TP, W])
        eq = sb("eq", [TP, W, FAN])
        move = sb("move", [TP, PAIRS, TREE_P])
        with nc.Block() as block:
            @block.sync
            def _(sp):
                c.clear_old(sp)
                sp.dma_start(platform[:], d["platform"]).then_inc(sg["constants"], DMA)
                sp.dma_start(fan_less[:], d["fan_less"]).then_inc(sg["constants"], DMA)

            @block.gpsimd
            def _(pool):
                with pool.Fori(0, LEVELS) as level:
                    pool.wait_ge(sg["index_ready"], level + 1)
                    pool.sem_inc(sg["pool_seen"], 1)
                    for w in range(W):
                        if w % SEEN == 0:
                            pool.wait_ge(sg["slots_free"], level * W + (w + SEEN))
                            pool.sem_inc(sg["pool_seen"], 1)
                        t, p = w // TREE_P, w % TREE_P
                        pool.indirect_dma_start(
                            row[:, w, :], None, d["tree_rows"],
                            bass.IndirectOffsetOnAxis(ap=index[:, t, p:p + 1], axis=0)).then_inc(sg[f"row_{w}"], DMA)

            @block.scalar
            def _(act):
                act.sem_inc(sg["slots_free"], W)

                with act.Fori(0, LEVELS) as level:
                    act.wait_ge(sg["exponent"], level + 1)
                    act.activation(poly[:], poly[:], ACT.Exp).then_inc(sg["exp_done"], 1)
                    act.wait_ge(sg["gelu_ready"], level + 1)
                    for w in range(W):
                        act.wait_ge(sg["weighed_added"], level * W + (w + 1))
                        for f in range(FAN):
                            act.activation(weighed[w % WEIGHED][:, f, :], row[:, w, OUT + f * D:OUT + (f + 1) * D],
                                           ACT.Copy, scale=gel[:, w, f:f + 1]).then_inc(sg["slots_free"] if f == FAN - 1 else sg["part_weighed"], 1)

            @block.tensor
            def _(pe):
                pe.sem_inc(sg["weighed_added"], WEIGHED)
                for t in range(PAIRS):
                    pe.matmul(c.ps[0:TP, t, 0:D], c.ident[0:TP, 0:TP], c.x[:, t, :], start=True, stop=False,
                              skip_group_check=True)
                with pe.Fori(0, LEVELS) as level:
                    for w in range(W):
                        pe.wait_ge(sg["slots_free"], level * W + (w + 1 + W))
                        for f in range(FAN):
                            last = pe.matmul(c.ps[0:TP, w // TREE_P, 0:D], c.ident[0:TP, 0:TP],
                                             weighed[w % WEIGHED][:, f, :], start=False, stop=False,
                                             skip_group_check=True)
                        last.then_inc(sg["weighed_added"], 1)

            @block.vector
            def _(dve):
                CHAIN = 23

                def gelu(level, link):
                    link(dve.scalar_tensor_tensor(mag[:], logit[:], -1.0, logit[:], ALU.mult, ALU.max))
                    link(dve.tensor_scalar(frac[:], mag[:], 0.5 * 0.5 ** 0.5, 1.0, ALU.mult, ALU.add))
                    link(dve.reciprocal(frac[:], frac[:]))
                    link(dve.tensor_scalar(poly[:], frac[:], ERFC[-1], None, ALU.mult))
                    for coefficient in reversed(ERFC[1:-1]):
                        link(dve.scalar_tensor_tensor(poly[:], poly[:], coefficient, frac[:], ALU.add, ALU.mult))
                    link(dve.scalar_tensor_tensor(half_sq[:], mag[:], 0.5, mag[:], ALU.mult, ALU.mult))
                    dve.scalar_tensor_tensor(poly[:], poly[:], ERFC[0], half_sq[:], ALU.add, ALU.subtract).then_inc(
                        sg["exponent"], 1)
                    dve.wait_ge(sg["exp_done"], level + 1)
                    link(dve.tensor_tensor(poly[:], poly[:], frac[:], ALU.mult))
                    link(dve.scalar_tensor_tensor(poly[:], poly[:], TINY, poly[:], ALU.is_ge, ALU.mult))
                    link(dve.scalar_tensor_tensor(poly[:], mag[:], 0.5, poly[:], ALU.mult, ALU.mult))
                    dve.wait_ge(sg["slots_free"], level * W + W)
                    dve.scalar_tensor_tensor(gel[:], logit[:], 0.0, poly[:], ALU.max, ALU.subtract).then_inc(
                        sg["gelu_ready"], 1)
                    dve.wait_ge(sg["gelu_ready"], level + 1)

                dve.wait_ge(sg["constants"], 2 * DMA)
                dve.memset(node[:], 0.0).then_inc(sg["root"], 1)
                dve.wait_ge(sg["root"], 1)
                dve.sem_inc(sg["product"], 2)
                with dve.Fori(0, LEVELS) as level:
                    link = Link(dve, sg["dve_chain"])
                    link.start = level * CHAIN
                    dve.tensor_tensor(index[:], node[:], platform[:], ALU.add).then_inc(sg["index_ready"], 1)
                    for w in range(W):
                        t = w // TREE_P
                        dve.wait_ge(sg[f"row_{w}"], level * DMA + DMA)
                        dve.sem_inc(sg["dve_seen"], 1)
                        dve.wait_ge(sg["product"], level * W + (w + 1))
                        dve.sem_inc(sg["dve_seen"], 1)
                        for f in range(FAN):
                            last = dve.tensor_tensor_reduce(
                                prod[:, w % 2, f, :], row[:, w, IN + f * D:IN + (f + 1) * D], z[:, t, :],
                                1.0, 0.0, ALU.mult, ALU.add, logit[:, w, f:f + 1])
                        last.then_inc(sg["product"], 1)
                    dve.wait_ge(sg["product"], level * W + (W + 2))
                    link(dve.tensor_tensor(logit[:], logit[:], row[:, :, BIAS:BIAS + FAN], ALU.add))
                    gelu(level, link)
                    link(dve.tensor_reduce(best[:], gel[:], X, ALU.max))
                    link(dve.tensor_tensor(eq[:], gel[:], best[:].unsqueeze(2).to_broadcast([TP, W, FAN]), ALU.is_equal))
                    link(dve.tensor_tensor(eq[:], eq[:], fan_less[:], ALU.mult))
                    link(dve.tensor_reduce(move[:].rearrange("p t f -> p (t f)"), eq[:], X, ALU.min))
                    link(dve.tensor_scalar(node[:], node[:], float(FAN), 10.0, ALU.mult, ALU.add))
                    link(dve.tensor_tensor(node[:], node[:], move[:], ALU.add))
                    assert link.n == CHAIN
                dve.wait_ge(sg["weighed_added"], LEVELS * W + WEIGHED)
                dve.tensor_copy(c.x[:], c.ps[0:TP, 0:PAIRS, 0:D]).then_inc(sg["x_ready"], 1)


LAST = 8


def program(nc, d):
    with ExitStack() as st:
        c = Core(nc, d)
        sb = alloc(c, st)
        c.x = sb("x", [TP, PAIRS, D])
        c.ident = sb("ident", [128, 128])
        c.ones = sb("ones", [128, 128])
        c.ybias = sb("ybias", [TP, D])
        c.ps = st.enter_context(nc.psum_tensor("ps", [128, 8, 512], F32))
        stage_load(c)

        def attend(name, hd, scale, latents=False, side=False):
            with ExitStack() as inner:
                n_prod = alloc(c, inner)(f"n_{name}", [D, H, D])
                with ExitStack() as prep:
                    z = alloc(c, prep)(f"z_{name}", [TP, PAIRS, D])
                    zt = alloc(c, prep)(f"zt_{name}", [D, TOK])
                    if latents:
                        stage_norm(c, c.x, z, None)
                        stage_norm(c, z, z, zt, affine=(d["ln_l_g"], d["ln_l_b"]))
                        stage_own_keys(c, z, zt)
                    else:
                        stage_norm(c, c.x, z, zt)
                    stage_fold(c, name, hd, zt, n_prod, biased=(name == "a0"))
                stage_attention(c, name, n_prod, scale, latents, side)
            stage_add_y(c, biased=(name == "a0"))

        attend("a0", D // H, (D // H) ** -0.5)
        if LAST >= 2:
            layer0_ffn(c)
        if LAST >= 3:
            stage_context_norm(c)
            attend("a1", 64, 64 ** -0.5, latents=True)
        if LAST >= 4:
            layer1_ffn(c)
        if LAST >= 5:
            layer2_attention(c)
        if LAST >= 6:
            layer2_ffn(c)
        if LAST >= 7:
            stage_mask(c)
            attend("a3", 64, 1.0, side=True)
        if LAST >= 8:
            layer3_ffn(c)
        stage_store(c)


def kernel(**a):
    import numpy as np
    import concourse.bacc as bacc
    from concourse import mybir as _mybir
    from concourse.bass_utils import run_bass_kernel_spmd

    a = {k: np.asarray(v) for k, v in a.items()}
    f32 = np.float32
    ins = {}

    def put(name, array):
        ins[name] = np.ascontiguousarray(array)

    def heads_t(w, hd):
        return w.reshape(D, H, hd).transpose(2, 1, 0)

    def heads(w, hd):
        return w.reshape(H, hd, D).transpose(1, 0, 2)

    ctx = a["ctx_1024"]
    put("x", a["x"].reshape(TOK, D))
    put("ctx", ctx)
    put("ctxT", ctx.transpose(0, 2, 1))
    wkv = a["L0_xattn_Wkv"]
    put("a0_wqT", heads_t(a["L0_xattn_Wq"], 8))
    put("a0_wkT", heads_t(wkv[:, :D], 8))
    put("a0_wvT", heads_t(wkv[:, D:], 8))
    put("a0_wo", heads(a["L0_xattn_Wo"], 8))
    put("a0_bq", a["L0_xattn_bq"].reshape(H, 8).T)
    put("a0_bv", np.broadcast_to(a["L0_xattn_bkv"][D:].reshape(H, 8).T[:, :, None], (8, H, TP)))
    put("a0_bo", a["L0_xattn_bo"][None])
    inner = H * 64
    wkv = a["L1_xattn_Wkv"]
    put("a1_wqT", heads_t(a["L1_xattn_Wq"], 64))
    put("a1_wkT", heads_t(wkv[:, :inner], 64))
    put("a1_wvT", heads_t(wkv[:, inner:], 64))
    put("a1_wo", heads(a["L1_xattn_Wout"], 64))
    put("ln_m_col", np.stack([a["L1_xattn_ln_m_g"], a["L1_xattn_ln_m_b"]], 1))
    put("ln_m_row", np.broadcast_to(np.stack([a["L1_xattn_ln_m_g"], a["L1_xattn_ln_m_b"]])[None], (KT, 2, D)))
    for k in ("ln_l_g", "ln_l_b"):
        put(k, np.broadcast_to(a[f"L1_xattn_{k}"][None], (TP, D)))
    for k, name in (("wqT", "Wq"), ("wkT", "Wk"), ("wvT", "Wv")):
        put(f"a3_{k}", heads_t(a[f"L3_xattn_{name}"], 64))
    put("a3_wo", heads(a["L3_xattn_Wo"], 64))
    side = a["fside_1x16xSxS2_0"]
    put("side_rows", side.reshape(H // 2, TP, SK).transpose(1, 0, 2))
    put("side_cols", side.reshape(HQ, SK // KT, KT).transpose(2, 1, 0))
    mask = a["mask_Bx1x1xS2_ff0"].reshape(B, SK)
    put("mask", mask)
    put("mask_col", mask.reshape(B, SK // KT, KT).transpose(0, 2, 1))
    for k in ("ln1_w", "ln1_b", "ln2_w", "ln2_b"):
        put(k, np.broadcast_to(a[f"L0_ffn_{k}"][:, None, :], (2, TP, D)))
    put("f0_wq", a["L0_ffn_wq"])
    put("f0_wk", a["L0_ffn_wk"])
    put("f0_wv", a["L0_ffn_wv"])
    put("f0_wo", a["L0_ffn_wo"])
    put("f0_bqk", np.stack([a["L0_ffn_bq"], a["L0_ffn_bk"]], -1))
    put("f0_bvo", np.stack([a["L0_ffn_bv"], a["L0_ffn_bo"]], 1))
    put("f0_gate_w", a["L0_ffn_gate_w"])
    put("f0_gate_b", a["L0_ffn_gate_b"][:, None, :])
    put("f0_w1", a["L0_ffn_e_w1"].transpose(0, 2, 1, 3))
    put("f0_b1", a["L0_ffn_e_b1"].reshape(2, E, 4, 128).transpose(0, 3, 1, 2))
    put("f0_w2", a["L0_ffn_e_w2"].reshape(2, E, 4, 128, D).transpose(0, 3, 1, 2, 4))
    put("f0_b2", a["L0_ffn_e_b2"])
    put("f1_w1T", a["L1_ffn_W1"].T)
    put("f1_b1", a["L1_ffn_b1"].reshape(4, 128).T)
    put("f1_w2T", a["L1_ffn_W2"].T.reshape(4, 128, D).transpose(1, 0, 2))
    put("f1_b2", a["L1_ffn_b2"][None])
    own = ctx[:, :S, :]
    put("own_rows", own.reshape(PAIRS, TP, D).transpose(1, 0, 2))
    put("own_cols", own.reshape(TOK, D).T)
    put("f2_gate_w", a["L2_ffn_gate_w"])
    put("f2_w1", a["L2_ffn_w1"].transpose(1, 0, 2))
    put("f2_w2", a["L2_ffn_w2"].reshape(E, 4, 128, D).transpose(2, 0, 1, 3))
    nodes = TREE_P * G
    put("tree_rows", np.concatenate([a["L3_ffn_W_in"].reshape(nodes, FAN * D), a["L3_ffn_b_in"].reshape(nodes, FAN),
                                     a["L3_ffn_W_out"].T.reshape(nodes, FAN * D)], 1))
    put("ident", np.eye(128, dtype=f32))
    put("ones", np.ones((128, 128), f32))
    p16 = np.arange(16)[:, None, None]
    put("negsel", np.broadcast_to(np.where(p16 % 8 == np.arange(8)[None, :, None], f32(-1), f32(0)), (16, 8, TP)))
    r = np.arange(TP)
    same = (r[:, None] // S) == (r[None, :] // S)
    before = same & (r[None, :] < r[:, None])
    put("causal", np.where(same & (r[None, :] <= r[:, None]), f32(0), f32(-1e30)))
    put("same", same.astype(f32))
    put("before", before.astype(f32))
    put("head_of", (np.arange(128)[:, None] // 8 == np.arange(16)[None, :]).astype(f32))
    e8 = np.arange(8)
    put("earlier", np.broadcast_to((e8[None, :] < e8[:, None]).astype(f32)[None], (TP, 8, 8)))
    put("platform", np.broadcast_to(np.arange(4, dtype=f32)[None, None, :] * f32(G), (TP, PAIRS, 4)))
    put("fan_less", np.broadcast_to(np.arange(4, dtype=f32)[None, None, :] - f32(9), (TP, 32, 4)))

    nc = bacc.Bacc("TRN2", target_bir_lowering=False, num_devices=1)
    dram = {k: nc.dram_tensor(k, v.shape, _mybir.dt.from_np(v.dtype), kind="ExternalInput").ap() for k, v in ins.items()}
    dram["qk"] = nc.dram_tensor("qk", (B, D, HQ), F32, kind="Internal").ap()
    dram["y"] = nc.dram_tensor("y", (PAIRS, TP, D), F32, kind="Internal").ap()
    dram["ctx1"] = nc.dram_tensor("ctx1", (B, SK + S, D), F32, kind="Internal").ap()
    dram["ctx1T"] = nc.dram_tensor("ctx1T", (B, D, SK + S), F32, kind="Internal").ap()
    dram["mask_parts"] = nc.dram_tensor("mask_parts", (B, 2, SK), F32, kind="Internal").ap()
    dram["out"] = nc.dram_tensor("out", (TOK, D), F32, kind="ExternalOutput").ap()
    program(nc, dram)
    got = run_bass_kernel_spmd(nc, [ins], core_ids=[0])
    return got.results[0]["out"].reshape(B, S, D)
```
